# Optimizing a Trainium2 kernel written in Bass

```python
import numpy as np
import jax
import jax.numpy as jnp

def _softmax(x, axis=-1):
    return jax.nn.softmax(x, axis=axis)

def _gelu(x):
    return jax.nn.gelu(x, approximate=True)

def _silu(x):
    return jax.nn.silu(x)

def _sigmoid(x):
    return jax.nn.sigmoid(x)

def _layernorm(x, axis=-1, eps=1e-05):
    m = jnp.mean(x, axis=axis, keepdims=True)
    v = jnp.var(x, axis=axis, keepdims=True)
    return (x - m) / jnp.sqrt(v + eps)

def _scatter_add(tgt, idx, src, axis=0):
    return tgt.at[idx].add(src)

def _segment_sum(src, seg, n):
    return jax.ops.segment_sum(src, seg, n)
kernel_name = 'mk_hybrid_d1_jaxref_r8_65bfdd'

def setup_inputs(seed: int=0):
    np.random.seed(seed)
    _w = jnp.asarray

    def _L0_attn_a_setup():
        import jax, jax.numpy as jnp
        from jax import lax
        import numpy as np
        D_MODEL = 256
        D_STATE = 128
        D_CONV = 4
        EXPAND = 2
        HEADDIM = 64
        NGROUPS = 1
        D_INNER = EXPAND * D_MODEL
        D_SSM = D_INNER
        NHEADS = D_SSM // HEADDIM
        CONV_DIM = D_SSM + 2 * NGROUPS * D_STATE
        D_IN_PROJ = 2 * D_INNER + 2 * NGROUPS * D_STATE + NHEADS
        BATCH = 2
        SEQLEN = 256
        EPS = 1e-05

        def _silu(x):
            return x * jax.nn.sigmoid(x)
        key = jax.random.key(seed)
        ks = jax.random.split(key, 8)
        u = jax.random.normal(ks[0], (BATCH, SEQLEN, D_MODEL), jnp.float32)
        W_in = jax.random.normal(ks[1], (D_IN_PROJ, D_MODEL), jnp.float32) * 0.02
        conv_w = jax.random.normal(ks[2], (CONV_DIM, 1, D_CONV), jnp.float32) * 0.2
        conv_b = jax.random.normal(ks[3], (CONV_DIM,), jnp.float32) * 0.02
        dt = jnp.exp(jax.random.uniform(ks[4], (NHEADS,)) * (jnp.log(0.1) - jnp.log(0.001)) + jnp.log(0.001))
        dt_bias = dt + jnp.log(-jnp.expm1(-dt))
        A_log = jnp.log(jax.random.uniform(ks[5], (NHEADS,), minval=1.0, maxval=16.0))
        D = jnp.ones((NHEADS,), jnp.float32)
        norm_w = jnp.ones((D_SSM,), jnp.float32)
        W_out = jax.random.normal(ks[6], (D_MODEL, D_INNER), jnp.float32) * 0.02
        return dict(u=u, W_in=W_in, conv_w=conv_w, conv_b=conv_b, dt_bias=dt_bias, A_log=A_log, D=D, norm_w=norm_w, W_out=W_out)
    _L0_attn_a_in = _L0_attn_a_setup()

    def _L0_attn_b_setup():
        import jax, jax.numpy as jnp
        import numpy as np
        EMBED = 256
        LATENT = 256
        HEADS = 16
        HEAD_DIM = LATENT // HEADS
        K = 64
        P = 4
        BATCH = 2
        SEQ = 256
        NEG_INF = float('-inf')

        def _causal_mask(S, Sk):
            col = jnp.arange(Sk)[None, :]
            row = jnp.arange(S)[:, None]
            return (col >= P) & (col - P > row)
        key = jax.random.key(seed)
        ks = jax.random.split(key, 12)
        s = 0.02
        x = jax.random.normal(ks[0], (BATCH, SEQ, EMBED), jnp.float32)
        Wq = jax.random.normal(ks[1], (EMBED, LATENT), jnp.float32) * s
        bq = jnp.zeros((LATENT,), jnp.float32)
        Wk = jax.random.normal(ks[2], (EMBED, LATENT), jnp.float32) * s
        bk = jnp.zeros((LATENT,), jnp.float32)
        Wv = jax.random.normal(ks[3], (EMBED, LATENT), jnp.float32) * s
        bv = jnp.zeros((LATENT,), jnp.float32)
        Wo = jax.random.normal(ks[4], (LATENT, EMBED), jnp.float32) * s
        bo = jnp.zeros((EMBED,), jnp.float32)
        pk = jax.random.normal(ks[5], (1, P, LATENT), jnp.float32)
        pv = jax.random.normal(ks[6], (1, P, LATENT), jnp.float32)
        return {'x': x, 'Wq': Wq, 'bq': bq, 'Wk': Wk, 'bk': bk, 'Wv': Wv, 'bv': bv, 'Wo': Wo, 'bo': bo, 'pk': pk, 'pv': pv}
    _L0_attn_b_in = _L0_attn_b_setup()

    def _L0_ffn_setup():
        import jax, jax.numpy as jnp
        import numpy as np
        E = 8
        K = 2
        D = 256
        F = 1024
        R = 16
        SCALING = 32.0 / 16.0

        def gelu_new(x):
            return jax.nn.gelu(x, approximate=True)
        key = jax.random.key(seed)
        ks = jax.random.split(key, 9)
        std = 0.02
        hidden_states = jax.random.normal(ks[0], (1, 128, D), dtype=jnp.float32)
        Wr = jax.random.normal(ks[1], (D, E), dtype=jnp.float32) * std
        br = jnp.zeros((E,), dtype=jnp.float32)
        W1 = jax.random.normal(ks[2], (D, F), dtype=jnp.float32) * std
        b1 = jnp.zeros((F,), dtype=jnp.float32)
        W2 = jax.random.normal(ks[3], (F, D), dtype=jnp.float32) * std
        b2 = jnp.zeros((D,), dtype=jnp.float32)
        A1 = jax.random.normal(ks[4], (E, R, D), dtype=jnp.float32) * std
        B1 = jax.random.normal(ks[5], (E, F, R), dtype=jnp.float32) * std
        A2 = jax.random.normal(ks[6], (E, R, F), dtype=jnp.float32) * std
        B2 = jax.random.normal(ks[7], (E, D, R), dtype=jnp.float32) * std
        return {'hidden_states': hidden_states, 'Wr': Wr, 'br': br, 'W1': W1, 'b1': b1, 'W2': W2, 'b2': b2, 'A1': A1, 'B1': B1, 'A2': A2, 'B2': B2}
    _L0_ffn_in = _L0_ffn_setup()
    _d = {'L0_attn_a_u': _L0_attn_a_in['u'], 'L0_attn_a_W_in': _L0_attn_a_in['W_in'], 'L0_attn_a_conv_w': _L0_attn_a_in['conv_w'], 'L0_attn_a_conv_b': _L0_attn_a_in['conv_b'], 'L0_attn_a_dt_bias': _L0_attn_a_in['dt_bias'], 'L0_attn_a_A_log': _L0_attn_a_in['A_log'], 'L0_attn_a_D': _L0_attn_a_in['D'], 'L0_attn_a_norm_w': _L0_attn_a_in['norm_w'], 'L0_attn_a_W_out': _L0_attn_a_in['W_out'], 'L0_attn_b_Wq': _L0_attn_b_in['Wq'], 'L0_attn_b_bq': _L0_attn_b_in['bq'], 'L0_attn_b_Wk': _L0_attn_b_in['Wk'], 'L0_attn_b_bk': _L0_attn_b_in['bk'], 'L0_attn_b_Wv': _L0_attn_b_in['Wv'], 'L0_attn_b_bv': _L0_attn_b_in['bv'], 'L0_attn_b_Wo': _L0_attn_b_in['Wo'], 'L0_attn_b_bo': _L0_attn_b_in['bo'], 'L0_attn_b_pk': _L0_attn_b_in['pk'], 'L0_attn_b_pv': _L0_attn_b_in['pv'], 'L0_ffn_Wr': _L0_ffn_in['Wr'], 'L0_ffn_br': _L0_ffn_in['br'], 'L0_ffn_W1': _L0_ffn_in['W1'], 'L0_ffn_b1': _L0_ffn_in['b1'], 'L0_ffn_W2': _L0_ffn_in['W2'], 'L0_ffn_b2': _L0_ffn_in['b2'], 'L0_ffn_A1': _L0_ffn_in['A1'], 'L0_ffn_B1': _L0_ffn_in['B1'], 'L0_ffn_A2': _L0_ffn_in['A2'], 'L0_ffn_B2': _L0_ffn_in['B2']}
    _x0 = _d['L0_attn_a_u']
    _d['L0_attn_a_u'] = jax.random.normal(jax.random.fold_in(jax.random.key(seed), 1), (2, 512, 256), dtype=_x0.dtype)
    del _x0
    return _d

def reference(L0_attn_a_u, L0_attn_a_W_in, L0_attn_a_conv_w, L0_attn_a_conv_b, L0_attn_a_dt_bias, L0_attn_a_A_log, L0_attn_a_D, L0_attn_a_norm_w, L0_attn_a_W_out, L0_attn_b_Wq, L0_attn_b_bq, L0_attn_b_Wk, L0_attn_b_bk, L0_attn_b_Wv, L0_attn_b_bv, L0_attn_b_Wo, L0_attn_b_bo, L0_attn_b_pk, L0_attn_b_pv, L0_ffn_Wr, L0_ffn_br, L0_ffn_W1, L0_ffn_b1, L0_ffn_W2, L0_ffn_b2, L0_ffn_A1, L0_ffn_B1, L0_ffn_A2, L0_ffn_B2):

    def _L0_attn_a_ref(u, W_in, conv_w, conv_b, dt_bias, A_log, D, norm_w, W_out):
        import jax, jax.numpy as jnp
        from jax import lax
        import numpy as np
        D_MODEL = 256
        D_STATE = 128
        D_CONV = 4
        EXPAND = 2
        HEADDIM = 64
        NGROUPS = 1
        D_INNER = EXPAND * D_MODEL
        D_SSM = D_INNER
        NHEADS = D_SSM // HEADDIM
        CONV_DIM = D_SSM + 2 * NGROUPS * D_STATE
        D_IN_PROJ = 2 * D_INNER + 2 * NGROUPS * D_STATE + NHEADS
        BATCH = 2
        SEQLEN = 256
        EPS = 1e-05

        def _silu(x):
            return x * jax.nn.sigmoid(x)
        batch, seqlen, _ = u.shape
        zxbcdt = jnp.einsum('bld,ed->ble', u, W_in)
        z = zxbcdt[..., :D_SSM]
        xBC = zxbcdt[..., D_SSM:D_SSM + CONV_DIM]
        dt = zxbcdt[..., D_SSM + CONV_DIM:]
        xc = lax.conv_general_dilated(xBC.transpose(0, 2, 1), conv_w, window_strides=(1,), padding=[(D_CONV - 1, 0)], feature_group_count=CONV_DIM, dimension_numbers=('NCH', 'OIH', 'NCH'))
        xBC = _silu((xc + conv_b[None, :, None]).transpose(0, 2, 1))
        x = xBC[..., :D_SSM]
        Bm = xBC[..., D_SSM:D_SSM + NGROUPS * D_STATE]
        Cm = xBC[..., D_SSM + NGROUPS * D_STATE:]
        A = -jnp.exp(A_log)
        dt_s = jax.nn.softplus(dt + dt_bias)
        dA = jnp.exp(dt_s * A)
        xh = x.reshape(batch, seqlen, NHEADS, HEADDIM)

        def step(state, inp):
            dA_t, dt_t, B_t, C_t, x_t = inp
            dB = dt_t[:, :, None] * B_t[:, None, :]
            state = dA_t[:, :, None, None] * state + x_t[..., None] * dB[:, :, None, :]
            y = jnp.einsum('bn,bhpn->bhp', C_t, state)
            return (state, y)
        state0 = jnp.zeros((batch, NHEADS, HEADDIM, D_STATE), u.dtype)
        xs = (dA.transpose(1, 0, 2), dt_s.transpose(1, 0, 2), Bm.transpose(1, 0, 2), Cm.transpose(1, 0, 2), xh.transpose(1, 0, 2, 3))
        _, ys = lax.scan(step, state0, xs)
        y = ys.transpose(1, 0, 2, 3) + xh * D[None, None, :, None]
        y = y.reshape(batch, seqlen, D_SSM)
        yg = y * _silu(z)
        yn = yg * lax.rsqrt(jnp.mean(yg * yg, axis=-1, keepdims=True) + EPS) * norm_w
        return jnp.einsum('bld,ed->ble', yn, W_out)

    def _L0_attn_b_ref(x, Wq, bq, Wk, bk, Wv, bv, Wo, bo, pk, pv):
        import jax, jax.numpy as jnp
        import numpy as np
        EMBED = 256
        LATENT = 256
        HEADS = 16
        HEAD_DIM = LATENT // HEADS
        K = 64
        P = 4
        BATCH = 2
        SEQ = 256
        NEG_INF = float('-inf')

        def _causal_mask(S, Sk):
            col = jnp.arange(Sk)[None, :]
            row = jnp.arange(S)[:, None]
            return (col >= P) & (col - P > row)
        B, S, _ = x.shape
        Sk = S + P
        q = (x @ Wq + bq).reshape(B, S, HEADS, HEAD_DIM).transpose(0, 2, 1, 3)
        k = jnp.concatenate([x @ Wk + bk, jnp.broadcast_to(pk, (B, P, LATENT))], axis=1)
        v = jnp.concatenate([x @ Wv + bv, jnp.broadcast_to(pv, (B, P, LATENT))], axis=1)
        k = k.reshape(B, Sk, HEADS, HEAD_DIM).transpose(0, 2, 1, 3)
        v = v.reshape(B, Sk, HEADS, HEAD_DIM).transpose(0, 2, 1, 3)
        scores = jnp.einsum('bhqd,bhkd->bhqk', q, k) / HEAD_DIM ** 0.5
        scores = jnp.where(_causal_mask(S, Sk)[None, None], NEG_INF, scores)
        topk_vals, topk_idx = jax.lax.top_k(scores, K)
        bi = jnp.arange(B)[:, None, None, None]
        hi = jnp.arange(HEADS)[None, :, None, None]
        si = jnp.arange(S)[None, None, :, None]
        masked = jnp.full_like(scores, NEG_INF).at[bi, hi, si, topk_idx].set(topk_vals)
        attn = jax.nn.softmax(masked, axis=-1)
        out = jnp.einsum('bhqk,bhkd->bhqd', attn, v)
        out = out.transpose(0, 2, 1, 3).reshape(B, S, LATENT)
        return out @ Wo + bo

    def _L0_ffn_ref(hidden_states, Wr, br, W1, b1, W2, b2, A1, B1, A2, B2):
        import jax, jax.numpy as jnp
        import numpy as np
        E = 8
        K = 2
        D = 256
        F = 1024
        R = 16
        SCALING = 32.0 / 16.0

        def gelu_new(x):
            return jax.nn.gelu(x, approximate=True)
        B, S, Dm = hidden_states.shape
        x = hidden_states.reshape(-1, Dm)
        probs = jax.nn.softmax(x @ Wr + br, axis=-1)
        w, idx = jax.lax.top_k(probs, K)
        combine = jnp.einsum('tk,tke->te', w, jax.nn.one_hot(idx, E, dtype=x.dtype))
        base_h1 = x @ W1 + b1
        t1 = jnp.einsum('td,erd->ter', x, A1)
        l1 = jnp.einsum('ter,efr->tef', t1, B1) * SCALING
        a = gelu_new(base_h1[:, None, :] + l1)
        ca = a * combine[:, :, None]
        mix = ca.sum(axis=1)
        t2 = jnp.einsum('tef,erf->ter', ca, A2)
        l2 = jnp.einsum('ter,edr->td', t2, B2) * SCALING
        out = mix @ W2 + combine.sum(-1, keepdims=True) * b2 + l2
        return out.reshape(B, S, Dm)
    x = L0_attn_a_u
    x = x + _L0_attn_a_ref(_layernorm(x, axis=-1), L0_attn_a_W_in, L0_attn_a_conv_w, L0_attn_a_conv_b, L0_attn_a_dt_bias, L0_attn_a_A_log, L0_attn_a_D, L0_attn_a_norm_w, L0_attn_a_W_out)
    x = x + _L0_ffn_ref(_layernorm(x, axis=-1), L0_ffn_Wr, L0_ffn_br, L0_ffn_W1, L0_ffn_b1, L0_ffn_W2, L0_ffn_b2, L0_ffn_A1, L0_ffn_B1, L0_ffn_A2, L0_ffn_B2)
    x = x + _L0_attn_b_ref(_layernorm(x, axis=-1), L0_attn_b_Wq, L0_attn_b_bq, L0_attn_b_Wk, L0_attn_b_bk, L0_attn_b_Wv, L0_attn_b_bv, L0_attn_b_Wo, L0_attn_b_bo, L0_attn_b_pk, L0_attn_b_pv)
    x = x + _L0_ffn_ref(_layernorm(x, axis=-1), L0_ffn_Wr, L0_ffn_br, L0_ffn_W1, L0_ffn_b1, L0_ffn_W2, L0_ffn_b2, L0_ffn_A1, L0_ffn_B1, L0_ffn_A2, L0_ffn_B2)
    return x

_drawn_inputs = setup_inputs


def setup_inputs(seed=0):
    import zlib

    import numpy as np

    out = dict(_drawn_inputs(seed))
    spreads = {'L0_attn_a_D': (1.0, 0.2),
     'L0_attn_a_norm_w': (1.0, 0.2),
     'L0_attn_b_bq': (0.0, 0.8),
     'L0_attn_b_bk': (0.0, 0.8),
     'L0_attn_b_bv': (0.0, 0.27),
     'L0_attn_b_bo': (0.0, 0.1),
     'L0_ffn_br': (0.0, 0.707),
     'L0_ffn_b1': (0.0, 0.341),
     'L0_ffn_b2': (0.0, 0.1)}
    factors = {'L0_attn_a_dt_bias': 8.0,
     'L0_attn_a_A_log': 8.0,
     'L0_attn_b_Wq': 5.057,
     'L0_attn_b_Wk': 4.848,
     'L0_attn_b_Wv': 3.785,
     'L0_attn_b_pk': 8.0,
     'L0_attn_b_pv': 8.0,
     'L0_ffn_Wr': 3.983,
     'L0_ffn_A1': 6.436,
     'L0_ffn_B1': 6.542,
     'L0_ffn_A2': 6.331,
     'L0_ffn_B2': 6.386}
    for name, (base, spread) in spreads.items():
        noise = np.random.default_rng([zlib.crc32(name.encode()), seed]).standard_normal(out[name].shape)
        drawn = base * np.exp(spread * noise) if base else spread * noise
        out[name] = jnp.asarray(drawn.astype(out[name].dtype))
    for name, factor in factors.items():
        out[name] = (out[name] * factor).astype(out[name].dtype)
    return out
```

```python
from contextlib import ExitStack

import concourse.bass as bass
from concourse import mybir

P = 128
BATCH, SEQ, DM = 2, 512, 256
TPB = SEQ // P
NT = BATCH * TPB
KD = DM // P
EPS = 1e-5

DI, DS, NH, HD, DCONV = 512, 128, 8, 64, 4
CD = DI + 2 * DS
CT = CD // P
IN_PROJ = DI + CD + NH
ET = DI // P

AH, AD, PRE, TOPK = 16, 16, 4, 64
SLOT = 32
QT = AH * SLOT // P
HPT = P // SLOT
SENT = -3.0e38
NEG = -1.0e30
DIAG = P + PRE

NE, RK, FF = 8, 16, 1024
FT = FF // P
LORA = 2.0

F32 = mybir.dt.float32
BF16 = mybir.dt.bfloat16
I32 = mybir.dt.int32
U32 = mybir.dt.uint32
ALU = mybir.AluOpType
ACT = mybir.ActivationFunctionType

C_CW, C_CB, C_NW, C_B1, C_BQ, C_BK = 0, 24, 30, 34, 42, 46
NCOL = 50
R_DTB, R_AL, R_D, R_BR, R_B2, R_BV, R_BO = 0, 8, 16, 24, 32, 288, 544
NROW = 800


class Tiles:
    pass


def place(nc, ctx):
    def sb(name, shape, dt=F32):
        return ctx.enter_context(nc.sbuf_tensor(name, shape, dt))

    T = Tiles()
    T.x = sb("x", [P, NT, DM])
    T.xn = sb("xn", [P, NT, DM])
    T.xnT = sb("xnT", [P, BATCH, KD, SEQ])
    T.ln_st = sb("ln_st", [P, NT, 6])
    T.ln_mv = sb("ln_mv", [P, NT, 2])
    T.ln_ve = sb("ln_ve", [P, NT])
    T.ln_r = sb("ln_r", [P, NT])
    T.cols = sb("cols", [P, NCOL])
    T.rows = sb("rows", [P, NROW])
    T.w_in = sb("w_in", [P, KD, IN_PROJ])
    T.w_out = sb("w_out", [P, ET, DM])
    T.wq = sb("wq", [P, KD, AH * SLOT])
    T.wk = sb("wk", [P, KD, AH * SLOT])
    T.wv = sb("wv", [P, KD, DM])
    T.wo = sb("wo", [P, KD, DM])
    T.pre_v = sb("pre_v", [PRE, DM])
    T.pre_k = sb("pre_k", [P, QT, PRE])
    T.w_ra = sb("w_ra", [P, KD, NE + P])
    T.w1 = sb("w1", [P, KD, FF])
    T.b1l = sb("b1l", [P, FF])
    T.w2a = sb("w2a", [P, FT, DM + P])
    T.b2l = sb("b2l", [P, DM])
    T.ident = sb("ident", [P, P])
    T.ones = sb("ones", [P, P])
    T.upto = sb("upto", [P, P])
    T.after = sb("after", [P, P])
    T.half = sb("half", [P, NT])
    T.iota8 = sb("iota8", [P, NE])
    T.ident_b = sb("ident_b", [P, P], BF16)
    T.mask_b = sb("mask_b", [P, DIAG], BF16)
    T.ps = ctx.enter_context(nc.psum_tensor("ps", [P, 8, 512], F32))
    return T


def start_up(nc, T, d):
    with ExitStack() as ctx:
        s_load = ctx.enter_context(nc.semaphore("s_load"))
        s_zero = ctx.enter_context(nc.semaphore("s_zero"))
        s_const = ctx.enter_context(nc.semaphore("s_const"))
        s_nw = ctx.enter_context(nc.semaphore("s_nw"))
        block = ctx.enter_context(nc.Block())
        loads = [
            (T.x[:, :, :], d["x"].rearrange("b (t p) m -> p (b t) m", p=P)),
            (T.cols[:, :], d["cols"]),
            (T.rows[:, :], d["rows"].partition_broadcast(P)),
            (T.w_in[:, :, :], d["w_in"].rearrange("(k p) e -> p k e", p=P)),
            (T.w_out[:, :, :], d["w_out"].rearrange("(k p) e -> p k e", p=P)),
            (T.w_ra[:, :, :], d["w_ra"].rearrange("(k p) e -> p k e", p=P)),
            (T.w1[:, :, :], d["w1"].rearrange("(k p) e -> p k e", p=P)),
            (T.b1l[:, :], d["b1l"]),
            (T.w2a[:, :, :], d["w2a"].rearrange("(k p) e -> p k e", p=P)),
            (T.b2l[:, :], d["b2l"]),
            (T.wq[:, :, :], d["wq"].rearrange("(k p) e -> p k e", p=P)),
            (T.wk[:, :, :], d["wk"].rearrange("(k p) e -> p k e", p=P)),
            (T.wv[:, :, :], d["wv"].rearrange("(k p) e -> p k e", p=P)),
            (T.wo[:, :, :], d["wo"].rearrange("(k p) e -> p k e", p=P)),
            (T.pre_k[:, :, :], d["pre_k"]),
            (T.pre_v[:, :], d["pre_v"]),
        ]

        @block.sync
        def _(sp):
            for dst, src in loads:
                sp.dma_start(dst, src).then_inc(s_load, 16)
            sp.wait_ge(s_load, 16 * len(loads))

        @block.gpsimd
        def _(pool):
            pool.memset(T.ident[:, :], 0.0).then_inc(s_zero, 1)
            pool.memset(T.ones[:, :], 1.0).then_inc(s_zero, 1)
            pool.memset(T.mask_b[:, :], 0.0).then_inc(s_zero, 1)
            pool.memset(T.ident_b[:, :], 0.0).then_inc(s_zero, 1)
            pool.memset(T.half[:, :], -0.5).then_inc(s_zero, 1)
            for e in range(NE):
                pool.memset(T.iota8[:, e:e + 1], float(e)).then_inc(s_zero, 1)
            pool.wait_ge(s_zero, 5 + NE)
            pool.affine_select(out=T.ident[:, :], in_=T.ident[:, :], compare_op=ALU.not_equal, fill=1.0, base=0,
                               pattern=[[-1, P]], channel_multiplier=1).then_inc(s_const, 1)
            pool.affine_select(out=T.ident_b[:, :], in_=T.ident_b[:, :], compare_op=ALU.not_equal, fill=1.0, base=0,
                               pattern=[[-1, P]], channel_multiplier=1).then_inc(s_const, 1)
            pool.affine_select(out=T.upto[:, :], in_=T.ones[:, :], compare_op=ALU.is_ge, fill=0.0, base=0,
                               pattern=[[1, P]], channel_multiplier=-1).then_inc(s_const, 1)
            pool.affine_select(out=T.after[:, :], in_=T.ones[:, :], compare_op=ALU.is_gt, fill=0.0, base=0,
                               pattern=[[-1, P]], channel_multiplier=1).then_inc(s_const, 1)
            pool.affine_select(out=T.mask_b[:, :], in_=T.mask_b[:, :], compare_op=ALU.is_ge, fill=NEG, base=PRE,
                               pattern=[[-1, DIAG]], channel_multiplier=1).then_inc(s_const, 1)
            pool.wait_ge(s_const, 5)

        @block.vector
        def _(dve):
            dve.wait_ge(s_load, 16 * len(loads))
            for e in range(ET):
                dve.tensor_scalar(T.w_out[:, e, :], T.w_out[:, e, :], T.cols[:, C_NW + e:C_NW + e + 1], None,
                                  ALU.mult).then_inc(s_nw, 1)
            dve.wait_ge(s_nw, ET)


class Norm:

    def __init__(self, nc, ctx, T, tag):
        def sem(name):
            return ctx.enter_context(nc.semaphore(f"{tag}_{name}"))
        self.T = T
        self.stat = sem("stat")
        self.mean = sem("mean")
        self.var_eps = sem("var_eps")
        self.rstd = sem("rstd")
        self.normed = sem("normed")
        self.turned = sem("turned")
        self.ready = sem("ready")

    def vector(self, dve, b):
        T, lo, hi = self.T, b * TPB, (b + 1) * TPB
        for g in range(lo, hi):
            dve.bn_stats(T.ln_st[:, g, :], T.x[:, g, :]).then_inc(self.stat, 1)
        dve.wait_ge(self.stat, hi)
        for g in range(lo, hi):
            dve.bn_aggr(T.ln_mv[:, g, :], T.ln_st[:, g, :]).then_inc(self.mean, 1)
        dve.wait_ge(self.mean, hi)
        dve.tensor_scalar(T.ln_ve[:, lo:hi], T.ln_mv[:, lo:hi, 1], EPS, None, ALU.add).then_inc(self.var_eps, 1)
        dve.wait_ge(self.rstd, b + 1)
        for g in range(lo, hi):
            dve.tensor_scalar(T.xn[:, g, :], T.x[:, g, :], T.ln_mv[:, g, 0:1], T.ln_r[:, g:g + 1], ALU.subtract,
                              ALU.mult).then_inc(self.normed, 1)

    def gpsimd(self, pool, b):
        T, lo, hi = self.T, b * TPB, (b + 1) * TPB
        pool.wait_ge(self.var_eps, b + 1)
        pool.tensor_tensor(T.ln_r[:, lo:hi], T.ln_ve[:, lo:hi], T.half[:, lo:hi], ALU.pow).then_inc(self.rstd, 1)

    def tensor(self, pe, b):
        T = self.T
        for t in range(TPB):
            pe.wait_ge(self.normed, b * TPB + t + 1)
            for k in range(KD):
                last = pe.transpose(T.ps[:, k, t * P:(t + 1) * P], T.xn[:, b * TPB + t, k * P:(k + 1) * P],
                                    T.ident[:, :])
        last.then_inc(self.turned, 1)

    def scalar(self, act, b):
        T = self.T
        act.wait_ge(self.turned, b + 1)
        act.activation(T.xnT[:, b, :, :], T.ps[:, 0:KD, :], ACT.Copy).then_inc(self.ready, 1)


def mamba(nc, T):
    with ExitStack() as ctx:
        def sb(name, shape, dt=F32):
            return ctx.enter_context(nc.sbuf_tensor("m_" + name, shape, dt))

        def sem(name):
            return ctx.enter_context(nc.semaphore("m_" + name))

        ps = T.ps
        acc = sb("acc", [P, 2, SEQ])
        xcT = sb("xcT", [P, CT, SEQ])
        zs = sb("zs", [P, TPB, DI])
        NS = TPB * NH
        sm = sb("sm", [P, 12, NS])
        v, rl, na, u, s1, s2, s3, s4, dts, a, dw, _ = [sm[:, i, :] for i in range(12)]
        neg_a = sb("neg_a", [P, NH])
        ex = sb("ex", [P, 3, NS])
        rhs_a = sb("rhs_a", [P, 2, NH, P])
        decay = sb("decay", [P, 2, NH, P])
        gm = sb("gm", [P, 2, P])
        mix = sb("mix", [P, 2, NH, P])
        b_tok = sb("b_tok", [P, 2, P])
        xh = sb("xh", [P, 2, DI])
        xw = sb("xw", [P, 2, DI])
        xd = sb("xd", [P, 2, DI])
        state = sb("state", [P, 2, DI])
        st_dec = sb("st_dec", [P, DI])
        y = sb("y", [P, 3, DI])
        yg = sb("yg", [P, 2, DI])
        sq = sb("sq", [P, DI])
        ygT = sb("ygT", [P, 2, ET, P])
        ssq = sb("ssq", [P, NT])
        msq = sb("msq", [P, NT])
        rr = sb("rr", [P, NT])

        norm = Norm(nc, ctx, T, "m_ln")
        s_xbc = sem("xbc")
        s_pre = sem("pre")
        s_cv = sem("cv")
        s_conv = sem("conv")
        s_silu = sem("silu")
        s_z = sem("z")
        s_zs = sem("zs")
        s_dt = sem("dt")
        s_na = sem("na")
        s_u = sem("u")
        s_nega = sem("nega")
        s_a = sem("a")
        s_cum = sem("cum")
        s_ex = sem("ex")
        s_dw = sem("dw")
        s_ra = sem("ra")
        s_g = sem("g")
        s_gm = sem("gm")
        s_seg = sem("seg")
        s_decay = sem("decay")
        s_mix = sem("mix")
        s_xhp = sem("xhp")
        s_xh = sem("xh")
        s_xw = sem("xw")
        s_xd = sem("xd")
        s_y = sem("y")
        s_stp = sem("stp")
        s_state = sem("state")
        s_yg = sem("yg")
        s_ssq = sem("ssq")
        s_msq = sem("msq")
        s_rr = sem("rr")
        s_ygTp = sem("ygTp")
        s_ygT = sem("ygT")
        s_o = sem("o")
        s_x = sem("x")
        s_dve = sem("dve")
        block = ctx.enter_context(nc.Block())
        XB, ZB, SEG, Y1, Y2, SMALL, STP = (4, 5), (7, 2), 2, 4, 5, 6, 7

        def heads(ap):
            return ap.rearrange("p (h q) -> p h q", h=NH)

        def per_head(ap, n=HD):
            return ap.unsqueeze(2).to_broadcast([P, NH, n])

        @block.tensor
        def _(pe):
            for b in range(BATCH):
                xT = T.xnT[:, b, :, :]
                if b:
                    pe.wait_ge(s_x, b * TPB)
                norm.tensor(pe, b)
                pe.wait_ge(norm.ready, b + 1)
                for ct in range(CT):
                    i = b * CT + ct
                    if i >= 2:
                        pe.wait_ge(s_conv, i - 1)
                    for k in range(KD):
                        last = pe.matmul(ps[:, XB[i % 2], :], T.w_in[:, k, DI + ct * P:DI + (ct + 1) * P], xT[:, k, :],
                                         start=(k == 0), stop=(k == KD - 1))
                    last.then_inc(s_xbc, 1)
                for t in range(TPB):
                    for k in range(KD):
                        last = pe.matmul(ps[:, SMALL, t * NH:(t + 1) * NH], xT[:, k, t * P:(t + 1) * P],
                                         T.w_in[:, k, DI + CD:IN_PROJ], start=(k == 0), stop=(k == KD - 1))
                last.then_inc(s_dt, 1)
                for t in range(TPB):
                    j = b * TPB + t
                    if j >= 2:
                        pe.wait_ge(s_zs, j - 1)
                    for k in range(KD):
                        last = pe.matmul(ps[:, ZB[j % 2], :], xT[:, k, t * P:(t + 1) * P], T.w_in[:, k, 0:DI],
                                         start=(k == 0), stop=(k == KD - 1))
                    last.then_inc(s_z, 1)
                pe.wait_ge(s_a, b + 1)
                for n, w in enumerate((T.upto, T.after, T.ones)):
                    last = pe.matmul(ps[:, SMALL, (n + 1) * NS:(n + 2) * NS], w[:, :], a, start=True, stop=True)
                last.then_inc(s_cum, 1)
                pe.wait_ge(s_zs, (b + 1) * TPB)
                for c in range(TPB):
                    n, q = b * TPB + c, (b * TPB + c) % 2
                    cols = slice(c * P, (c + 1) * P)
                    pe.wait_ge(s_silu, (b + 1) * CT)
                    if n:
                        pe.wait_ge(s_ygT, n)
                    for e in range(ET):
                        last = pe.transpose(ps[:, 0, e * P:(e + 1) * P], xcT[:, e, cols], T.ident[:, :])
                    last.then_inc(s_xhp, 1)
                    if n:
                        pe.wait_ge(s_gm, 2 * n)
                    pe.transpose(ps[:, 1, P:2 * P], xcT[:, ET, cols], T.ident[:, :])
                    pe.matmul(ps[:, 1, 0:P], xcT[:, ET, cols], xcT[:, ET + 1, cols], start=True,
                              stop=True).then_inc(s_g, 1)
                    pe.wait_ge(s_ra, n + 1)
                    if n:
                        pe.wait_ge(s_decay, n)
                    for i in range(2):
                        last = pe.matmul(ps[:, SEG + i, :], T.after[:, :], rhs_a[:, q, 4 * i:4 * i + 4, :], start=True,
                                         stop=True)
                    last.then_inc(s_seg, 1)
                    pe.wait_ge(s_mix, n + 1)
                    pe.wait_ge(s_xh, n + 1)
                    if c:
                        pe.wait_ge(s_state, b * (TPB - 1) + c)
                        pe.matmul(ps[:, Y2, :], xcT[:, ET + 1, cols], state[:, (c - 1) % 2, :], start=True, stop=True)
                    for h in range(NH):
                        last = pe.matmul(ps[:, Y1, h * HD:(h + 1) * HD], mix[:, q, h, :],
                                         xh[:, q, h * HD:(h + 1) * HD], start=True, stop=True)
                    last.then_inc(s_y, 1)
                    if c < TPB - 1:
                        pe.wait_ge(s_xw, n + 1)
                        pe.matmul(ps[:, STP, :], b_tok[:, q, :], xw[:, q, :], start=True, stop=True).then_inc(s_stp, 1)
                    pe.wait_ge(s_yg, n + 1)
                    for e in range(ET):
                        last = pe.transpose(ps[:, 0, e * P:(e + 1) * P], yg[:, q, e * P:(e + 1) * P], T.ident[:, :])
                    last.then_inc(s_ygTp, 1)
                    pe.wait_ge(s_ygT, n + 1)
                    for e in range(ET):
                        last = pe.matmul(ps[:, SMALL, DM:2 * DM], ygT[:, q, e, :], T.w_out[:, e, :], start=(e == 0),
                                         stop=(e == ET - 1))
                    last.then_inc(s_o, 1)

        @block.scalar
        def _(act):
            for b in range(BATCH):
                norm.scalar(act, b)

                def silu(i):
                    act.wait_ge(s_conv, i + 1)
                    act.activation(xcT[:, i % CT, :], acc[:, i % 2, :], ACT.Silu).then_inc(s_silu, 1)

                for ct in range(CT):
                    i = b * CT + ct
                    act.wait_ge(s_xbc, i + 1)
                    if i >= 2:
                        act.wait_ge(s_silu, i - 1)
                    act.activation(acc[:, i % 2, :], ps[:, XB[i % 2], :], ACT.Identity,
                                   bias=T.cols[:, C_CB + ct:C_CB + ct + 1],
                                   scale=T.cols[:, C_CW + 4 * ct + 3:C_CW + 4 * ct + 4]).then_inc(s_pre, 1)
                    if ct:
                        silu(i - 1)
                silu(b * CT + CT - 1)
                for t in range(TPB):
                    j = b * TPB + t
                    act.wait_ge(s_z, j + 1)
                    act.activation(zs[:, t, :], ps[:, ZB[j % 2], :], ACT.Silu).then_inc(s_zs, 1)
                act.wait_ge(s_na, b + 1)
                act.activation(u, na, ACT.Exp).then_inc(s_u, 1)
                if b == 0:
                    act.activation(neg_a[:, :], T.rows[:, R_AL:R_AL + NH], ACT.Exp).then_inc(s_nega, 1)
                act.wait_ge(s_cum, b + 1)
                act.activation(ex[:, :, :], ps[:, SMALL, NS:4 * NS].rearrange("p (n s) -> p n s", n=3),
                               ACT.Exp).then_inc(s_ex, 1)
                for c in range(TPB):
                    n, q = b * TPB + c, (b * TPB + c) % 2
                    act.wait_ge(s_xhp, n + 1)
                    act.activation(xh[:, q, :], ps[:, 0, :], ACT.Copy).then_inc(s_xh, 1)
                    act.wait_ge(s_seg, n + 1)
                    act.activation(decay[:, q, :, :].rearrange("p h t -> p (h t)"),
                                   ps[:, SEG:SEG + 2, :].rearrange("p i t -> p (i t)"), ACT.Exp).then_inc(s_decay, 1)
                    act.wait_ge(s_yg, n + 1)
                    act.activation(sq[:, :], yg[:, q, :], ACT.Square, accum_out=ssq[:, n:n + 1]).then_inc(s_ssq, 1)
                    act.wait_ge(s_ygTp, n + 1)
                    act.activation(ygT[:, q, :, :].rearrange("p e t -> p (e t)"), ps[:, 0, :],
                                   ACT.Copy).then_inc(s_ygT, 1)
                    act.wait_ge(s_ssq, n + 1)

        @block.gpsimd
        def _(pool):
            for b in range(BATCH):
                norm.gpsimd(pool, b)
                pool.wait_ge(s_ex, b + 1)
                pool.wait_ge(s_a, b + 1)
                pool.tensor_tensor(dw, ex[:, 1, :], dts, ALU.mult).then_inc(s_dw, 1)
                for c in range(TPB):
                    n, q = b * TPB + c, (b * TPB + c) % 2
                    if n >= 2:
                        pool.wait_ge(s_seg, n - 1)
                    pool.tensor_tensor(rhs_a[:, q, :, :], T.upto[:, :].unsqueeze(1).to_broadcast([P, NH, P]),
                                       per_head(a[:, c * NH:(c + 1) * NH], P), ALU.mult).then_inc(s_ra, 1)
                    pool.wait_ge(s_xh, n + 1)
                    if n >= 2:
                        pool.wait_ge(s_yg, n - 1)
                    pool.tensor_tensor(heads(xd[:, q, :]), heads(xh[:, q, :]), per_head(T.rows[:, R_D:R_D + NH]),
                                       ALU.mult).then_inc(s_xd, 1)
                    pool.wait_ge(s_dw, b + 1)
                    if c >= 2:
                        pool.wait_ge(s_stp, b * (TPB - 1) + c - 1)
                    elif b:
                        pool.wait_ge(s_stp, b * (TPB - 1))
                    pool.tensor_tensor(heads(xw[:, q, :]), heads(xh[:, q, :]), per_head(dw[:, c * NH:(c + 1) * NH]),
                                       ALU.mult).then_inc(s_xw, 1)
                    pool.wait_ge(s_msq, n + 1)
                    pool.tensor_tensor(rr[:, n:n + 1], msq[:, n:n + 1], T.half[:, 0:1], ALU.pow).then_inc(s_rr, 1)

        @block.vector
        def _(dve):
            done = [0]

            def link(ins):
                done[0] += 1
                ins.then_inc(s_dve, 1)
                dve.wait_ge(s_dve, done[0])

            for b in range(BATCH):
                norm.vector(dve, b)
                for ct in range(CT):
                    i = b * CT + ct
                    dve.wait_ge(s_pre, i + 1)
                    for lag in range(1, DCONV):
                        w = T.cols[:, C_CW + 4 * ct + 3 - lag:C_CW + 4 * ct + 4 - lag]
                        ins = dve.scalar_tensor_tensor(acc[:, i % 2, lag:SEQ], ps[:, XB[i % 2], 0:SEQ - lag], w,
                                                       acc[:, i % 2, lag:SEQ], ALU.mult, ALU.add)
                        if lag < DCONV - 1:
                            link(ins)
                        else:
                            ins.then_inc(s_conv, 1)
                dve.wait_ge(s_dt, b + 1)
                if b:
                    dve.wait_ge(s_ra, b * TPB)
                    dve.wait_ge(s_dw, b)
                    dve.wait_ge(s_cum, b)
                for c in range(TPB):
                    ins = dve.tensor_tensor(v[:, c * NH:(c + 1) * NH], ps[:, SMALL, c * NH:(c + 1) * NH],
                                            T.rows[:, R_DTB:R_DTB + NH], ALU.add)
                link(ins)
                dve.scalar_tensor_tensor(na, v, -1.0, v, ALU.mult, ALU.min).then_inc(s_na, 1)
                link(dve.tensor_scalar(rl, v, 0.0, None, ALU.max))
                dve.wait_ge(s_u, b + 1)
                link(dve.tensor_scalar(s1, u, 2.0, None, ALU.add))
                link(dve.reciprocal(s2, s1))
                link(dve.tensor_tensor(s1, u, s2, ALU.mult))
                link(dve.tensor_tensor(s2, s1, s1, ALU.mult))
                link(dve.tensor_scalar(s3, s2, 2.0 / 17, 2.0 / 15, ALU.mult, ALU.add))
                for k in range(13, -1, -2):
                    link(dve.tensor_tensor(s4, s3, s2, ALU.mult))
                    if k > 0:
                        link(dve.tensor_scalar(s3, s4, 2.0 / k, None, ALU.add))
                link_last = dve.tensor_tensor(s4, s3, s1, ALU.mult)
                link(link_last)
                link(dve.tensor_tensor(dts, s4, rl, ALU.add))
                if b == 0:
                    dve.wait_ge(s_nega, 1)
                    link(dve.tensor_scalar(neg_a[:, :], neg_a[:, :], -1.0, None, ALU.mult))
                dve.tensor_tensor(a.rearrange("p (c h) -> p c h", h=NH), dts.rearrange("p (c h) -> p c h", h=NH),
                                  neg_a[:, :].unsqueeze(1).to_broadcast([P, TPB, NH]), ALU.mult).then_inc(s_a, 1)
                for c in range(TPB):
                    n, q = b * TPB + c, (b * TPB + c) % 2
                    dve.wait_ge(s_g, n + 1)
                    dve.tensor_tensor(gm[:, q, :], ps[:, 1, 0:P], T.upto[:, :], ALU.mult).then_inc(s_gm, 1)
                    dve.tensor_copy(b_tok[:, q, :], ps[:, 1, P:2 * P]).then_inc(s_gm, 1)
                    dve.wait_ge(s_gm, 2 * n + 2)
                    dve.wait_ge(s_decay, n + 1)
                    if n >= 2:
                        dve.wait_ge(s_y, n - 1)
                    for h in range(NH):
                        ins = dve.scalar_tensor_tensor(mix[:, q, h, :], decay[:, q, h, :],
                                                       dts[:, c * NH + h:c * NH + h + 1], gm[:, q, :], ALU.mult,
                                                       ALU.mult)
                    ins.then_inc(s_mix, 1)
                    dve.wait_ge(s_y, n + 1)
                    dve.wait_ge(s_ex, b + 1)
                    dve.wait_ge(s_xd, n + 1)
                    link(dve.tensor_tensor(y[:, 0, :], ps[:, Y1, :], xd[:, q, :], ALU.add))
                    if c:
                        link(dve.tensor_tensor(heads(y[:, 1, :]), heads(ps[:, Y2, :]),
                                               per_head(ex[:, 0, c * NH:(c + 1) * NH]), ALU.mult))
                        link(dve.tensor_tensor(y[:, 2, :], y[:, 0, :], y[:, 1, :], ALU.add))
                    dve.wait_ge(s_zs, (b + 1) * TPB)
                    if n >= 2:
                        dve.wait_ge(s_ygTp, n - 1)
                    dve.tensor_tensor(yg[:, q, :], y[:, 2 if c else 0, :], zs[:, c, :], ALU.mult).then_inc(s_yg, 1)
                    if c < TPB - 1:
                        if c:
                            link(dve.tensor_tensor(heads(st_dec[:, :]), heads(state[:, (c - 1) % 2, :]),
                                                   per_head(ex[:, 2, c * NH:(c + 1) * NH]), ALU.mult))
                        dve.wait_ge(s_stp, b * (TPB - 1) + c + 1)
                        if c:
                            dve.tensor_tensor(state[:, c % 2, :], st_dec[:, :], ps[:, STP, :],
                                              ALU.add).then_inc(s_state, 1)
                        else:
                            dve.tensor_copy(state[:, c % 2, :], ps[:, STP, :]).then_inc(s_state, 1)
                    dve.wait_ge(s_ssq, n + 1)
                    dve.tensor_scalar(msq[:, n:n + 1], ssq[:, n:n + 1], 1.0 / DI, EPS, ALU.mult,
                                      ALU.add).then_inc(s_msq, 1)
                    dve.wait_ge(s_rr, n + 1)
                    dve.wait_ge(s_o, n + 1)
                    dve.scalar_tensor_tensor(T.x[:, n, :], ps[:, SMALL, DM:2 * DM], rr[:, n:n + 1], T.x[:, n, :],
                                             ALU.mult, ALU.add).then_inc(s_x, 1)
            dve.wait_ge(s_x, NT)


def ffn(nc, T, tag, out=None):
    with ExitStack() as ctx:
        def sb(name, shape, dt=F32):
            return ctx.enter_context(nc.sbuf_tensor(f"{tag}_{name}", shape, dt))

        def sem(name):
            return ctx.enter_context(nc.semaphore(f"{tag}_{name}"))

        ps = T.ps
        lg = sb("lg", [P, NT, NE])
        top = sb("top", [P, NT, NE])
        idx = sb("idx", [P, NT, NE], U32)
        idf = sb("idf", [P, NT, NE])
        neg = sb("neg", [P, NT])
        pr = sb("pr", [P, NT, NE])
        pk = sb("pk", [P, NT, 2])
        psum_ = sb("psum", [P, NT])
        rs = sb("rs", [P, NT])
        w = sb("w", [P, NT, 2])
        wsum = sb("wsum", [P, NT])
        oh = sb("oh", [P, NT, 2, NE])
        ohw = sb("ohw", [P, NT, 2, NE])
        ohd = sb("ohd", [P, NT, 2, NE])
        tm = sb("tm", [P, 2, 2, P])
        tmT = sb("tmT", [P, 2, SEQ])
        aT = sb("aT", [P, 2, FT, SEQ])
        t2 = sb("t2", [P, 2, 3, P])
        t2T = sb("t2T", [P, 2, P])
        xa = sb("xa", [P, 2, 3, DM])
        norm = Norm(nc, ctx, T, tag + "_ln")
        s_rt = sem("rt")
        s_lg = sem("lg")
        s_neg = sem("neg")
        s_pr = sem("pr")
        s_tm = sem("tm")
        s_tmTp = sem("tmTp")
        s_tmT = sem("tmT")
        s_h0 = sem("h0")
        s_g0 = sem("g0")
        s_h1 = sem("h1")
        s_g1 = sem("g1")
        s_dn = sem("dn")
        s_t2 = sem("t2")
        s_xa = sem("xa")
        s_t2p = sem("t2p")
        s_t2T = sem("t2T")
        s_l2 = sem("l2")
        s_x = sem("x")
        s_out = sem("out")
        s_dve = sem("dve")
        block = ctx.enter_context(nc.Block())
        RT, HB, DN, TP, L2 = (2, 3), (6, 7, 2, 3), (0, 1), 4, 5

        def by_rank(ap):
            return ap.rearrange("p (e r) -> p e r", e=NE)

        def per_rank(ap):
            return ap.unsqueeze(2).to_broadcast([P, NE, RK])

        @block.tensor
        def _(pe):
            for b in range(BATCH):
                xT = T.xnT[:, b, :, :]
                if b:
                    pe.wait_ge(s_x, b * TPB)
                norm.tensor(pe, b)
                pe.wait_ge(norm.ready, b + 1)
                for t in range(TPB):
                    g = b * TPB + t
                    if t >= 2:
                        pe.wait_ge(s_tm, g - 1)
                    for k in range(KD):
                        last = pe.matmul(ps[:, RT[g % 2], 0:NE + P], xT[:, k, t * P:(t + 1) * P], T.w_ra[:, k, :],
                                         start=(k == 0), stop=(k == KD - 1))
                    last.then_inc(s_rt, 1)
                for t in range(TPB):
                    g = b * TPB + t
                    pe.wait_ge(s_tm, g + 1)
                    for s in range(2):
                        last = pe.transpose(ps[:, TP + s, t * P:(t + 1) * P], tm[:, g % 2, s, :], T.ident[:, :])
                    last.then_inc(s_tmTp, 1)
                pe.wait_ge(s_tmT, b + 1)

                def second(f):
                    i = b * FT + f
                    pe.wait_ge(s_g0, i + 1)
                    pe.matmul(ps[:, HB[f % 4], :], T.b1l[:, f * P:(f + 1) * P], tmT[:, 1, :], start=False, stop=True,
                              skip_group_check=True).then_inc(s_h1, 1)

                for f in range(FT):
                    i = b * FT + f
                    if f >= 4:
                        pe.wait_ge(s_g1, i - 3)
                    o = ps[:, HB[f % 4], :]
                    for k in range(KD):
                        pe.matmul(o, T.w1[:, k, f * P:(f + 1) * P], xT[:, k, :], start=(k == 0), stop=False,
                                  skip_group_check=True)
                    pe.matmul(o, T.b1l[:, f * P:(f + 1) * P], tmT[:, 0, :], start=False, stop=True,
                              skip_group_check=True).then_inc(s_h0, 1)
                    if f:
                        second(f - 1)
                second(FT - 1)
                pe.wait_ge(s_g1, (b + 1) * FT)
                for t in range(TPB):
                    g = b * TPB + t
                    if t:
                        pe.wait_ge(s_xa, g)
                    for s in range(2):
                        for f in range(FT):
                            last = pe.matmul(ps[:, DN[s], 0:DM + P], aT[:, s, f, t * P:(t + 1) * P], T.w2a[:, f, :],
                                             start=(f == 0), stop=(f == FT - 1))
                    last.then_inc(s_dn, 1)
                    pe.wait_ge(s_t2, g + 1)
                    pe.transpose(ps[:, TP, 0:P], t2[:, g % 2, 2, :], T.ident[:, :]).then_inc(s_t2p, 1)
                    pe.wait_ge(s_t2T, g + 1)
                    if t:
                        pe.wait_ge(s_x, g)
                    pe.matmul(ps[:, L2, 0:DM], t2T[:, g % 2, :], T.b2l[:, :], start=True, stop=True).then_inc(s_l2, 1)

        @block.scalar
        def _(act):
            for b in range(BATCH):
                norm.scalar(act, b)
                for g in range(b * TPB, (b + 1) * TPB):
                    act.wait_ge(s_neg, g + 1)
                    act.activation(pr[:, g, :], lg[:, g, :], ACT.Exp, bias=neg[:, g:g + 1],
                                   accum_out=psum_[:, g:g + 1]).then_inc(s_pr, 1)
                    act.activation(pk[:, g, :], top[:, g, 0:2], ACT.Exp, bias=neg[:, g:g + 1]).then_inc(s_pr, 1)
                act.wait_ge(s_tmTp, (b + 1) * TPB)
                act.activation(tmT[:, :, :], ps[:, TP:TP + 2, :], ACT.Copy).then_inc(s_tmT, 1)
                if b:
                    act.wait_ge(s_dn, b * TPB)

                def gelu(f, s, ready, done):
                    i = b * FT + f
                    act.wait_ge(ready, i + 1)
                    act.activation(aT[:, s, f, :], ps[:, HB[f % 4], :], ACT.Gelu_apprx_tanh,
                                   bias=T.cols[:, C_B1 + f:C_B1 + f + 1]).then_inc(done, 1)

                for f in range(FT):
                    gelu(f, 0, s_h0, s_g0)
                    if f:
                        gelu(f - 1, 1, s_h1, s_g1)
                gelu(FT - 1, 1, s_h1, s_g1)
                for t in range(TPB):
                    g = b * TPB + t
                    act.wait_ge(s_t2p, g + 1)
                    act.activation(t2T[:, g % 2, :], ps[:, TP, 0:P], ACT.Copy).then_inc(s_t2T, 1)

        @block.gpsimd
        def _(pool):
            for b in range(BATCH):
                norm.gpsimd(pool, b)

        @block.vector
        def _(dve):
            done = [0]

            def link(ins):
                done[0] += 1
                ins.then_inc(s_dve, 1)
                dve.wait_ge(s_dve, done[0])

            for b in range(BATCH):
                norm.vector(dve, b)
                for t in range(TPB):
                    g = b * TPB + t
                    dve.wait_ge(s_rt, g + 1)
                    link(dve.tensor_tensor(lg[:, g, :], ps[:, RT[g % 2], 0:NE], T.rows[:, R_BR:R_BR + NE], ALU.add))
                    link(dve.max(top[:, g, :], lg[:, g, :]))
                    dve.tensor_scalar(neg[:, g:g + 1], top[:, g, 0:1], -1.0, None, ALU.mult).then_inc(s_neg, 1)
                    link(dve.max_index(idx[:, g, :], top[:, g, :], lg[:, g, :]))
                    link(dve.tensor_copy(idf[:, g, :], idx[:, g, :]))
                    for s in range(2):
                        ins = dve.tensor_scalar(oh[:, g, s, :], T.iota8[:, :], idf[:, g, s:s + 1], None, ALU.is_equal)
                    link(ins)
                    dve.tensor_scalar(ohd[:, g, 0, :], oh[:, g, 0, :], LORA, None, ALU.mult)
                    link(dve.tensor_tensor(ohd[:, g, 1, :], oh[:, g, 1, :], oh[:, g, 0, :], ALU.subtract))
                    link(dve.tensor_scalar(ohd[:, g, 1, :], ohd[:, g, 1, :], LORA, None, ALU.mult))
                    if g >= 2:
                        dve.wait_ge(s_tmTp, g - 1)
                    for s in range(2):
                        ins = dve.tensor_tensor(by_rank(tm[:, g % 2, s, :]), by_rank(ps[:, RT[g % 2], NE:NE + P]),
                                                per_rank(ohd[:, g, s, :]), ALU.mult)
                    ins.then_inc(s_tm, 1)
                for t in range(TPB):
                    g = b * TPB + t
                    dve.wait_ge(s_pr, 2 * g + 2)
                    link(dve.reciprocal(rs[:, g:g + 1], psum_[:, g:g + 1]))
                    link(dve.tensor_scalar(w[:, g, :], pk[:, g, :], rs[:, g:g + 1], None, ALU.mult))
                    link(dve.tensor_tensor(wsum[:, g:g + 1], w[:, g, 0:1], w[:, g, 1:2], ALU.add))
                    for s in range(2):
                        ins = dve.tensor_scalar(ohw[:, g, s, :], oh[:, g, s, :], w[:, g, s:s + 1], LORA, ALU.mult,
                                                ALU.mult)
                    link(ins)
                for t in range(TPB):
                    g, q = b * TPB + t, (b * TPB + t) % 2
                    dve.wait_ge(s_dn, g + 1)
                    for s in range(2):
                        ins = dve.tensor_tensor(by_rank(t2[:, q, s, :]), by_rank(ps[:, DN[s], DM:DM + P]),
                                                per_rank(ohw[:, g, s, :]), ALU.mult)
                    link(ins)
                    dve.tensor_tensor(t2[:, q, 2, :], t2[:, q, 0, :], t2[:, q, 1, :], ALU.add).then_inc(s_t2, 1)
                    link(dve.scalar_tensor_tensor(xa[:, q, 0, :], ps[:, DN[0], 0:DM], w[:, g, 0:1], T.x[:, g, :],
                                                  ALU.mult, ALU.add))
                    dve.scalar_tensor_tensor(xa[:, q, 1, :], ps[:, DN[1], 0:DM], w[:, g, 1:2], xa[:, q, 0, :],
                                             ALU.mult, ALU.add).then_inc(s_xa, 1)
                    dve.wait_ge(s_xa, g + 1)
                    link(dve.scalar_tensor_tensor(xa[:, q, 2, :], T.rows[:, R_B2:R_B2 + DM], wsum[:, g:g + 1],
                                                  xa[:, q, 1, :], ALU.mult, ALU.add))
                    dve.wait_ge(s_l2, g + 1)
                    dve.tensor_tensor(T.x[:, g, :], ps[:, L2, 0:DM], xa[:, q, 2, :], ALU.add).then_inc(s_x, 1)
            dve.wait_ge(s_x, NT)

        @block.sync
        def _(sp):
            if out is not None:
                for g in range(NT):
                    b, t = divmod(g, TPB)
                    sp.wait_ge(s_x, g + 1)
                    sp.dma_start(out[b, t * P:(t + 1) * P, :], T.x[:, g, :]).then_inc(s_out, 16)
                sp.wait_ge(s_out, 16 * NT)


def attention(nc, T):
    with ExitStack() as ctx:
        def sb(name, shape, dt=F32):
            return ctx.enter_context(nc.sbuf_tensor("a_" + name, shape, dt))

        def sem(name):
            return ctx.enter_context(nc.semaphore("a_" + name))

        ps = T.ps
        WMAX = SEQ + PRE
        ROUNDS = TOPK // 8
        qT = sb("qT", [P, QT, SEQ])
        kT = sb("kT", [P, QT, WMAX])
        v = sb("v", [P, TPB, DM])
        bqs = sb("bqs", [P, QT])
        S = sb("S", [P, 3, WMAX])
        left = sb("left", [P, WMAX])
        m8 = sb("m8", [P, 2, ROUNDS, 8])
        nm = sb("nm", [P, 2])
        E = sb("E", [P, 2, WMAX])
        pr = sb("pr", [P, 2, WMAX])
        prT = sb("prT", [P, 2, SEQ])
        preT = sb("preT", [PRE, 2, P])
        rsum = sb("rsum", [P, 2, AH])
        rinv = sb("rinv", [P, 2, AH])
        o = sb("o", [P, 2, DM])
        oT = sb("oT", [P, 2, KD, P])
        xa = sb("xa", [P, DM])
        norm = Norm(nc, ctx, T, "a_ln")
        s_bqs = sem("bqs")
        s_qk = sem("qk")
        s_qkT = sem("qkT")
        s_v = sem("v")
        s_vs = sem("vs")
        s_pk = sem("pk")
        s_sc = sem("sc")
        s_S = sem("S")
        s_m8 = sem("m8")
        s_nm = sem("nm")
        s_E = sem("E")
        s_sel = sem("sel")
        s_tp = sem("tp")
        s_pT = sem("pT")
        s_pv = sem("pv")
        s_on = sem("on")
        s_oTp = sem("oTp")
        s_oT = sem("oT")
        s_f = sem("f")
        s_x = sem("x")
        s_dve = sem("dve")
        block = ctx.enter_context(nc.Block())
        QB, VB = (2, 3, 4, 5), (6, 7)
        SC, TB, XT, OB, FB = (2, 4), 6, 7, 0, 1
        UPB = TPB * AH
        units = [(b, t, h) for b in range(BATCH) for t in range(TPB) for h in range(AH)]

        def width(t):
            return (t + 1) * P + PRE

        def wide(i):
            return ps[:, SC[i % 2]:SC[i % 2] + 2, :].rearrange("p a c -> p (a c)")

        @block.tensor
        def _(pe):
            def project(b):
                xT = T.xnT[:, b, :, :]
                norm.tensor(pe, b)
                pe.wait_ge(norm.ready, b + 1)
                for i in range(2 * QT):
                    w, m = (T.wq, T.wk)[i // QT], i % QT
                    if i >= 4:
                        pe.wait_ge(s_qkT, b * 2 * QT + i - 3)
                    for k in range(KD):
                        last = pe.matmul(ps[:, QB[i % 4], :], w[:, k, m * P:(m + 1) * P], xT[:, k, :], start=(k == 0),
                                         stop=(k == KD - 1))
                    last.then_inc(s_qk, 1)
                for t in range(TPB):
                    if t >= 2:
                        pe.wait_ge(s_vs, b * TPB + t - 1)
                    for k in range(KD):
                        last = pe.matmul(ps[:, VB[t % 2], 0:DM], xT[:, k, t * P:(t + 1) * P], T.wv[:, k, :],
                                         start=(k == 0), stop=(k == KD - 1))
                    last.then_inc(s_v, 1)
                pe.wait_ge(s_qkT, (b + 1) * 2 * QT)
                pe.wait_ge(s_vs, (b + 1) * TPB)
                pe.wait_ge(s_pk, 1)

            def scores(i):
                b, t, h = units[i]
                if i >= 2:
                    pe.wait_ge(s_S, i - 1)
                m, r = h // HPT, SLOT * (h % HPT)
                q = qT[r:r + AD, m, t * P:(t + 1) * P]
                out = wide(i)
                lo, hi = t * P, min(width(t), SEQ)
                pe.matmul(out[:, 0:hi], q, kT[r:r + AD, m, 0:hi], start=True, stop=False, skip_group_check=True)
                last = pe.matmul(out[:, lo:hi], T.ident_b[:, :], T.mask_b[:, 0:hi - lo], start=False, stop=True,
                                 skip_group_check=True)
                if width(t) > SEQ:
                    pe.matmul(out[:, SEQ:WMAX], q, kT[r:r + AD, m, SEQ:WMAX], start=True, stop=False,
                              skip_group_check=True)
                    last = pe.matmul(out[:, SEQ:WMAX], T.ident_b[:, :], T.mask_b[:, P:DIAG], start=False, stop=True,
                                     skip_group_check=True)
                last.then_inc(s_sc, 1)

            def values(i):
                b, t, h = units[i]
                pe.wait_ge(s_sel, i + 1)
                if i:
                    pe.wait_ge(s_pT, i)
                for j in range(t + 1):
                    pe.transpose(ps[:, TB, j * P:(j + 1) * P], pr[:, i % 2, j * P:(j + 1) * P], T.ident[:, :])
                pe.transpose(ps[0:PRE, XT, 0:P], pr[:, i % 2, (t + 1) * P:(t + 1) * P + PRE],
                             T.ident[:, :]).then_inc(s_tp, 1)
                pe.wait_ge(s_pT, i + 1)
                if h == 0 and i:
                    pe.wait_ge(s_on, i // AH)
                out = ps[:, OB, h * AD:(h + 1) * AD]
                hc = slice(h * AD, (h + 1) * AD)
                for j in range(t + 1):
                    pe.matmul(out, prT[:, i % 2, j * P:(j + 1) * P], v[:, j, hc], start=(j == 0), stop=False)
                tail = v[0:PRE, t + 1, hc] if t + 1 < TPB else T.pre_v[:, hc]
                pe.matmul(out, preT[:, i % 2, :], tail, start=False, stop=True).then_inc(s_pv, 1)

            def finish(g):
                pe.wait_ge(s_on, g + 1)
                if g:
                    pe.wait_ge(s_x, g)
                for k in range(KD):
                    last = pe.transpose(ps[:, FB, k * P:(k + 1) * P], o[:, g % 2, k * P:(k + 1) * P], T.ident[:, :])
                last.then_inc(s_oTp, 1)
                pe.wait_ge(s_oT, g + 1)
                for k in range(KD):
                    last = pe.matmul(ps[:, FB, DM:2 * DM], oT[:, g % 2, k, :], T.wo[:, k, :], start=(k == 0),
                                     stop=(k == KD - 1))
                last.then_inc(s_f, 1)

            for b in range(BATCH):
                project(b)
                scores(b * UPB)
                for i in range(b * UPB, (b + 1) * UPB):
                    if i + 1 < (b + 1) * UPB:
                        scores(i + 1)
                    if i > b * UPB:
                        values(i - 1)
                        if i % AH == 1 and i // AH % TPB:
                            finish(i // AH - 1)
                values((b + 1) * UPB - 1)
                finish((b + 1) * TPB - 1)
                pe.wait_ge(s_x, (b + 1) * TPB)

        @block.scalar
        def _(act):
            act.activation(bqs[:, :], T.cols[:, C_BQ:C_BQ + QT], ACT.Copy, scale=AD ** -0.5).then_inc(s_bqs, 1)
            act.wait_ge(s_bqs, 1)

            def evacuate(i):
                t = units[i][1]
                act.wait_ge(s_sc, i + 1)
                if i >= 3:
                    act.wait_ge(s_m8, 2 * i - 4 - 0)
                    act.wait_ge(s_E, i - 2)
                act.activation(S[:, i % 3, 0:width(t)], wide(i)[:, 0:width(t)], ACT.Copy).then_inc(s_S, 1)

            def exponent(i):
                t = units[i][1]
                act.wait_ge(s_m8, 2 * i + 1)
                act.activation(nm[:, i % 2:i % 2 + 1], m8[:, i % 2, 0, 0:1], ACT.Copy, scale=-1.0).then_inc(s_nm, 1)
                act.wait_ge(s_nm, i + 1)
                if i >= 2:
                    act.wait_ge(s_sel, i - 1)
                act.activation(E[:, i % 2, 0:width(t)], S[:, i % 3, 0:width(t)], ACT.Exp,
                               bias=nm[:, i % 2:i % 2 + 1]).then_inc(s_E, 1)

            def turn(i):
                t = units[i][1]
                act.wait_ge(s_tp, i + 1)
                act.activation(prT[:, i % 2, 0:(t + 1) * P], ps[:, TB, 0:(t + 1) * P], ACT.Copy)
                if i >= 2:
                    pass
                act.activation(preT[:, i % 2, :], ps[0:PRE, XT, 0:P], ACT.Copy).then_inc(s_pT, 1)

            def turn_out(g):
                act.wait_ge(s_oTp, g + 1)
                act.activation(oT[:, g % 2, :, :], ps[:, FB, 0:DM].rearrange("p (k t) -> p k t", k=KD),
                               ACT.Copy).then_inc(s_oT, 1)

            for b in range(BATCH):
                norm.scalar(act, b)
                for i in range(2 * QT):
                    m = i % QT
                    act.wait_ge(s_qk, b * 2 * QT + i + 1)
                    if i < QT:
                        ins = act.activation(qT[:, m, :], ps[:, QB[i % 4], :], ACT.Identity, bias=bqs[:, m:m + 1],
                                             scale=AD ** -0.5)
                    else:
                        ins = act.activation(kT[:, m, 0:SEQ], ps[:, QB[i % 4], :], ACT.Identity,
                                             bias=T.cols[:, C_BK + m:C_BK + m + 1])
                    ins.then_inc(s_qkT, 1)
                first = b * UPB
                evacuate(first)
                for i in range(first, first + UPB):
                    if i + 1 < first + UPB:
                        evacuate(i + 1)
                    exponent(i)
                    if i > first:
                        turn(i - 1)
                    if i % AH == 1 and i // AH % TPB:
                        turn_out(i // AH - 1)
                turn(first + UPB - 1)
                turn_out((b + 1) * TPB - 1)

        @block.gpsimd
        def _(pool):
            pool.tensor_copy(kT[:, :, SEQ:WMAX], T.pre_k[:, :, :]).then_inc(s_pk, 1)
            for b in range(BATCH):
                norm.gpsimd(pool, b)

        @block.vector
        def _(dve):
            done = [0]

            def link(ins):
                done[0] += 1
                ins.then_inc(s_dve, 1)
                dve.wait_ge(s_dve, done[0])

            def select(i):
                t, h = units[i][1:]
                g = i // AH
                w = width(t)
                s, m = S[:, i % 3, 0:w], m8[:, i % 2, :, :]
                dve.wait_ge(s_S, i + 1)
                dve.max(m[:, 0, :], s).then_inc(s_m8, 1)
                dve.wait_ge(s_m8, 2 * i + 1)
                for r in range(ROUNDS):
                    ins = dve.match_replace(left[:, 0:w], m[:, r, :], s if r == 0 else left[:, 0:w], SENT)
                    if r == 0:
                        ins.then_inc(s_m8, 1)
                        dve.wait_ge(s_m8, 2 * i + 2)
                    else:
                        link(ins)
                    if r + 1 < ROUNDS:
                        link(dve.max(m[:, r + 1, :], left[:, 0:w]))
                dve.wait_ge(s_E, i + 1)
                if i >= 2:
                    dve.wait_ge(s_tp, i - 1)
                dve.scalar_tensor_tensor(pr[:, i % 2, 0:w], left[:, 0:w], SENT, E[:, i % 2, 0:w], ALU.is_equal,
                                         ALU.mult, accum_out=rsum[:, g % 2, h:h + 1]).then_inc(s_sel, 1)

            def normalise(g):
                dve.wait_ge(s_sel, (g + 1) * AH)
                link(dve.reciprocal(rinv[:, g % 2, :], rsum[:, g % 2, :]))
                dve.wait_ge(s_pv, (g + 1) * AH)
                dve.tensor_tensor(o[:, g % 2, :].rearrange("p (h d) -> p h d", h=AH),
                                  ps[:, OB, 0:DM].rearrange("p (h d) -> p h d", h=AH),
                                  rinv[:, g % 2, :].unsqueeze(2).to_broadcast([P, AH, AD]), ALU.mult).then_inc(s_on, 1)

            def residual(g):
                link(dve.tensor_tensor(xa[:, :], T.x[:, g, :], T.rows[:, R_BO:R_BO + DM], ALU.add))
                dve.wait_ge(s_f, g + 1)
                dve.tensor_tensor(T.x[:, g, :], ps[:, FB, DM:2 * DM], xa[:, :], ALU.add).then_inc(s_x, 1)

            for b in range(BATCH):
                norm.vector(dve, b)
                for t in range(TPB):
                    dve.wait_ge(s_v, b * TPB + t + 1)
                    dve.tensor_tensor(v[:, t, :], ps[:, VB[t % 2], 0:DM], T.rows[:, R_BV:R_BV + DM],
                                      ALU.add).then_inc(s_vs, 1)
                for i in range(b * UPB, (b + 1) * UPB):
                    select(i)
                    if i % AH == 0 and i // AH % TPB:
                        normalise(i // AH - 1)
                    if i % AH == 2 and i // AH % TPB:
                        residual(i // AH - 1)
                normalise((b + 1) * TPB - 1)
                residual((b + 1) * TPB - 1)
            dve.wait_ge(s_x, NT)


def hybrid_layer(nc, d, out):
    with ExitStack() as ctx:
        T = place(nc, ctx)
        start_up(nc, T, d)
        mamba(nc, T)
        ffn(nc, T, "f1")
        attention(nc, T)
        ffn(nc, T, "f2", out)


def kernel(**inputs):
    import numpy as np
    import concourse.bacc as bacc
    from concourse.bass_utils import run_bass_kernel_spmd

    a = {k[3:]: np.asarray(v) for k, v in inputs.items()}

    def columns(v):
        return v.reshape(-1, P).T

    def slots(w):
        p = np.zeros((w.shape[0], AH, SLOT), w.dtype)
        p[:, :, :AD] = w.reshape(w.shape[0], AH, AD)
        return p.reshape(w.shape[0], AH * SLOT)

    cw = a["attn_a_conv_w"].reshape(CT, P, DCONV).transpose(1, 0, 2).reshape(P, CT * DCONV)
    bq, bk = (columns(slots(a[f"attn_b_{n}"][None])[0]) for n in ("bq", "bk"))
    host = {
        "x": a["attn_a_u"],
        "cols": np.concatenate([cw, columns(a["attn_a_conv_b"]), columns(a["attn_a_norm_w"]), columns(a["ffn_b1"]),
                                bq, bk], axis=1),
        "rows": np.concatenate([a["attn_a_dt_bias"], a["attn_a_A_log"], a["attn_a_D"], a["ffn_br"], a["ffn_b2"],
                                a["attn_b_bv"], a["attn_b_bo"]]),
        "w_in": a["attn_a_W_in"].T,
        "w_out": a["attn_a_W_out"].T,
        "w_ra": np.concatenate([a["ffn_Wr"], a["ffn_A1"].reshape(NE * RK, DM).T], axis=1),
        "w1": a["ffn_W1"],
        "b1l": a["ffn_B1"].transpose(0, 2, 1).reshape(NE * RK, FF),
        "w2a": np.concatenate([a["ffn_W2"], a["ffn_A2"].reshape(NE * RK, FF).T], axis=1),
        "b2l": a["ffn_B2"].transpose(0, 2, 1).reshape(NE * RK, DM),
        "wq": slots(a["attn_b_Wq"]),
        "wk": slots(a["attn_b_Wk"]),
        "wv": a["attn_b_Wv"],
        "wo": a["attn_b_Wo"],
        "pre_k": slots(a["attn_b_pk"][0]).T.reshape(QT, P, PRE).transpose(1, 0, 2),
        "pre_v": a["attn_b_pv"][0],
    }
    nc = bacc.Bacc("TRN2", target_bir_lowering=False, num_devices=1)
    arrays, d = {}, {}
    for name, v in host.items():
        v = np.ascontiguousarray(v)
        arrays[f"in_{name}"] = v
        d[name] = nc.dram_tensor(f"in_{name}", v.shape, mybir.dt.from_np(v.dtype), kind="ExternalInput").ap()
    out = nc.dram_tensor("out", (BATCH, SEQ, DM), F32, kind="ExternalOutput").ap()
    hybrid_layer(nc, d, out)
    r = run_bass_kernel_spmd(nc, [arrays], core_ids=[0])
    return r.results[0]["out"]
```

```python
import math
from contextlib import ExitStack

import concourse.bass as bass
from concourse import mybir

P = 128
BATCH, SEQ, DM = 2, 512, 256
TPB = SEQ // P
NT = BATCH * TPB
KD = DM // P
EPS = 1e-5

DI, DS, NH, HD, DCONV = 512, 128, 8, 64, 4
CD = DI + 2 * DS
CT = CD // P
IN_PROJ = DI + CD + NH
ET = DI // P

AH, AD, PRE, TOPK = 16, 16, 4, 64
SLOT = 32
QT = AH * SLOT // P
HPT = P // SLOT
SENT = -3.0e38
NEG = -1.0e30
GH = 4
YR, ER, NR = 4, 3, 4
DEPTH = 16
AIM = TOPK - DEPTH // 2
FAR = (DEPTH - 1.5) ** 2
SHIFT = 5.0
DIAG = P + PRE

NE, RK, FF = 8, 16, 1024
FT = FF // P
LORA = 2.0

F32 = mybir.dt.float32
BF16 = mybir.dt.bfloat16
I32 = mybir.dt.int32
U32 = mybir.dt.uint32
ALU = mybir.AluOpType
ACT = mybir.ActivationFunctionType
AX_X = mybir.AxisListType.X
RADD = bass.bass_isa.ReduceOp.add

C_CW, C_CB, C_NW, C_B1, C_BQ, C_BK = 0, 24, 30, 34, 42, 46
NCOL = 50
R_DTB, R_AL, R_D, R_BR, R_B2, R_BV, R_BO = 0, 8, 16, 24, 32, 288, 544
NROW = 800


class Tiles:
    pass


def place(nc, ctx):
    def sb(name, shape, dt=F32):
        return ctx.enter_context(nc.sbuf_tensor(name, shape, dt))

    T = Tiles()
    T.x = sb("x", [P, NT, DM])
    T.xn = sb("xn", [P, NT, DM])
    T.xnT = sb("xnT", [P, BATCH, KD, SEQ])
    T.ln_st = sb("ln_st", [P, NT, 6])
    T.ln_mv = sb("ln_mv", [P, NT, 2])
    T.ln_ve = sb("ln_ve", [P, NT])
    T.ln_r = sb("ln_r", [P, NT])
    T.cols = sb("cols", [P, NCOL])
    T.rows = sb("rows", [P, NROW])
    T.wq = sb("wq", [P, KD, AH * SLOT])
    T.wk = sb("wk", [P, KD, AH * SLOT])
    T.wv = sb("wv", [P, KD, DM])
    T.wo = sb("wo", [P, KD, DM])
    T.pre_v = sb("pre_v", [PRE, DM])
    T.pre_k = sb("pre_k", [P, QT, PRE])
    T.w_ra = sb("w_ra", [P, KD, NE + P])
    T.w1 = sb("w1", [P, KD, FF])
    T.b1l = sb("b1l", [P, FF])
    T.w2a = sb("w2a", [P, FT, DM + P])
    T.b2l = sb("b2l", [P, DM])
    T.ident = sb("ident", [P, P])
    T.ones = sb("ones", [P, P])
    T.upto = sb("upto", [P, P])
    T.after = sb("after", [P, P])
    T.half = sb("half", [P, NT])
    T.iota16 = sb("iota16", [P, DEPTH])
    T.iota8 = T.iota16[:, 0:NE]
    T.minus1 = sb("minus1", [P, GH])
    T.blocks = sb("blocks", [P, P])
    T.tab = sb("tab", [P, TPB, 4])
    T.ident_b = sb("ident_b", [P, P], BF16)
    T.mask_b = sb("mask_b", [P, DIAG], BF16)
    T.ps = ctx.enter_context(nc.psum_tensor("ps", [P, 8, 512], F32))
    return T


def start_up(nc, T, d):
    with ExitStack() as ctx:
        s_load = ctx.enter_context(nc.semaphore("s_load"))
        s_zero = ctx.enter_context(nc.semaphore("s_zero"))
        s_const = ctx.enter_context(nc.semaphore("s_const"))
        s_nw = ctx.enter_context(nc.semaphore("s_nw"))
        block = ctx.enter_context(nc.Block())
        loads = [
            (T.x[:, :, :], d["x"].rearrange("b (t p) m -> p (b t) m", p=P)),
            (T.cols[:, :], d["cols"]),
            (T.rows[:, :], d["rows"].partition_broadcast(P)),
            (T.w_in[:, :, :], d["w_in"].rearrange("(k p) e -> p k e", p=P)),
            (T.w_out[:, :, :], d["w_out"].rearrange("(k p) e -> p k e", p=P)),
            (T.w_ra[:, :, :], d["w_ra"].rearrange("(k p) e -> p k e", p=P)),
            (T.w1[:, :, :], d["w1"].rearrange("(k p) e -> p k e", p=P)),
            (T.b1l[:, :], d["b1l"]),
            (T.w2a[:, :, :], d["w2a"].rearrange("(k p) e -> p k e", p=P)),
            (T.b2l[:, :], d["b2l"]),
            (T.wq[:, :, :], d["wq"].rearrange("(k p) e -> p k e", p=P)),
            (T.wk[:, :, :], d["wk"].rearrange("(k p) e -> p k e", p=P)),
            (T.wv[:, :, :], d["wv"].rearrange("(k p) e -> p k e", p=P)),
            (T.wo[:, :, :], d["wo"].rearrange("(k p) e -> p k e", p=P)),
            (T.pre_k[:, :, :], d["pre_k"]),
            (T.pre_v[:, :], d["pre_v"]),
            (T.tab[:, :, :], d["tab"]),
        ]

        @block.sync
        def _(sp):
            for dst, src in loads:
                sp.dma_start(dst, src).then_inc(s_load, 16)
            sp.wait_ge(s_load, 16 * len(loads))

        @block.gpsimd
        def _(pool):
            pool.memset(T.ident[:, :], 0.0).then_inc(s_zero, 1)
            pool.memset(T.ones[:, :], 1.0).then_inc(s_zero, 1)
            pool.memset(T.mask_b[:, :], 0.0).then_inc(s_zero, 1)
            pool.memset(T.ident_b[:, :], 0.0).then_inc(s_zero, 1)
            pool.memset(T.half[:, :], -0.5).then_inc(s_zero, 1)
            pool.memset(T.minus1[:, :], -1.0).then_inc(s_zero, 1)
            for e in range(DEPTH):
                pool.memset(T.iota16[:, e:e + 1], float(e)).then_inc(s_zero, 1)
            pool.wait_ge(s_zero, 6 + DEPTH)
            pool.affine_select(out=T.ident[:, :], in_=T.ident[:, :], compare_op=ALU.not_equal, fill=1.0, base=0,
                               pattern=[[-1, P]], channel_multiplier=1).then_inc(s_const, 1)
            pool.affine_select(out=T.ident_b[:, :], in_=T.ident_b[:, :], compare_op=ALU.not_equal, fill=1.0, base=0,
                               pattern=[[-1, P]], channel_multiplier=1).then_inc(s_const, 1)
            pool.affine_select(out=T.upto[:, :], in_=T.ones[:, :], compare_op=ALU.is_ge, fill=0.0, base=0,
                               pattern=[[1, P]], channel_multiplier=-1).then_inc(s_const, 1)
            pool.affine_select(out=T.after[:, :], in_=T.ones[:, :], compare_op=ALU.is_gt, fill=0.0, base=0,
                               pattern=[[-1, P]], channel_multiplier=1).then_inc(s_const, 1)
            pool.affine_select(out=T.mask_b[:, :], in_=T.mask_b[:, :], compare_op=ALU.is_ge, fill=NEG, base=PRE,
                               pattern=[[-1, DIAG]], channel_multiplier=1).then_inc(s_const, 1)
            blocks = T.blocks[:, :].rearrange("p (a c) -> p a c", a=HPT)
            pool.affine_select(out=blocks, in_=T.ones[:, :].rearrange("p (a c) -> p a c", a=HPT),
                               compare_op=ALU.is_ge, fill=0.0, base=0, pattern=[[-SLOT, HPT], [0, SLOT]],
                               channel_multiplier=1).then_inc(s_const, 1)
            pool.wait_ge(s_const, 6)
            pool.affine_select(out=blocks, in_=blocks, compare_op=ALU.is_ge, fill=0.0, base=SLOT - 1,
                               pattern=[[SLOT, HPT], [0, SLOT]], channel_multiplier=-1).then_inc(s_const, 1)
            pool.wait_ge(s_const, 7)

        @block.vector
        def _(dve):
            dve.wait_ge(s_load, 16 * len(loads))
            for e in range(ET):
                dve.tensor_scalar(T.w_out[:, e, :], T.w_out[:, e, :], T.cols[:, C_NW + e:C_NW + e + 1], None,
                                  ALU.mult).then_inc(s_nw, 1)
            dve.wait_ge(s_nw, ET)


class Norm:

    def __init__(self, nc, ctx, T, tag):
        def sem(name):
            return ctx.enter_context(nc.semaphore(f"{tag}_{name}"))
        self.T = T
        self.stat = sem("stat")
        self.mean = sem("mean")
        self.var_eps = sem("var_eps")
        self.rstd = sem("rstd")
        self.normed = sem("normed")
        self.turned = sem("turned")
        self.ready = sem("ready")

    def vector(self, dve, b):
        T, lo, hi = self.T, b * TPB, (b + 1) * TPB
        for g in range(lo, hi):
            dve.bn_stats(T.ln_st[:, g, :], T.x[:, g, :]).then_inc(self.stat, 1)
        dve.wait_ge(self.stat, hi)
        for g in range(lo, hi):
            dve.bn_aggr(T.ln_mv[:, g, :], T.ln_st[:, g, :]).then_inc(self.mean, 1)
        dve.wait_ge(self.mean, hi)
        dve.tensor_scalar(T.ln_ve[:, lo:hi], T.ln_mv[:, lo:hi, 1], EPS, None, ALU.add).then_inc(self.var_eps, 1)
        dve.wait_ge(self.rstd, b + 1)
        for g in range(lo, hi):
            dve.tensor_scalar(T.xn[:, g, :], T.x[:, g, :], T.ln_mv[:, g, 0:1], T.ln_r[:, g:g + 1], ALU.subtract,
                              ALU.mult).then_inc(self.normed, 1)

    def gpsimd(self, pool, b):
        T, lo, hi = self.T, b * TPB, (b + 1) * TPB
        pool.wait_ge(self.var_eps, b + 1)
        pool.tensor_tensor(T.ln_r[:, lo:hi], T.ln_ve[:, lo:hi], T.half[:, lo:hi], ALU.pow).then_inc(self.rstd, 1)

    def tensor(self, pe, b):
        T = self.T
        for t in range(TPB):
            pe.wait_ge(self.normed, b * TPB + t + 1)
            for k in range(KD):
                last = pe.transpose(T.ps[:, k, t * P:(t + 1) * P], T.xn[:, b * TPB + t, k * P:(k + 1) * P],
                                    T.ident[:, :])
        last.then_inc(self.turned, 1)

    def scalar(self, act, b):
        T = self.T
        act.wait_ge(self.turned, b + 1)
        act.activation(T.xnT[:, b, :, :], T.ps[:, 0:KD, :], ACT.Copy).then_inc(self.ready, 1)


def mamba(nc, T):
    with ExitStack() as ctx:
        def sb(name, shape, dt=F32):
            return ctx.enter_context(nc.sbuf_tensor("m_" + name, shape, dt))

        def sem(name):
            return ctx.enter_context(nc.semaphore("m_" + name))

        ps = T.ps
        acc = sb("acc", [P, 2, SEQ])
        xcT = sb("xcT", [P, CT, SEQ])
        zs = sb("zs", [P, TPB, DI])
        NS = TPB * NH
        sm = sb("sm", [P, 12, NS])
        v, rl, na, u, s1, s2, s3, s4, dts, a, dw, _ = [sm[:, i, :] for i in range(12)]
        neg_a = sb("neg_a", [P, NH])
        ex = sb("ex", [P, 3, NS])
        rhs_a = sb("rhs_a", [P, 2, NH, P])
        decay = sb("decay", [P, 2, NH, P])
        gm = sb("gm", [P, 2, P])
        mix = sb("mix", [P, 2, NH, P])
        b_tok = sb("b_tok", [P, 2, P])
        xh = sb("xh", [P, 2, DI])
        xw = sb("xw", [P, 2, DI])
        xd = sb("xd", [P, 2, DI])
        state = sb("state", [P, 2, DI])
        st_dec = sb("st_dec", [P, DI])
        y = sb("y", [P, 3, DI])
        yg = sb("yg", [P, 2, DI])
        sq = sb("sq", [P, DI])
        ygT = sb("ygT", [P, 2, ET, P])
        ssq = sb("ssq", [P, NT])
        msq = sb("msq", [P, NT])
        rr = sb("rr", [P, NT])

        norm = Norm(nc, ctx, T, "m_ln")
        s_xbc = sem("xbc")
        s_pre = sem("pre")
        s_cv = sem("cv")
        s_conv = sem("conv")
        s_silu = sem("silu")
        s_z = sem("z")
        s_zs = sem("zs")
        s_dt = sem("dt")
        s_na = sem("na")
        s_u = sem("u")
        s_nega = sem("nega")
        s_a = sem("a")
        s_cum = sem("cum")
        s_ex = sem("ex")
        s_dw = sem("dw")
        s_ra = sem("ra")
        s_g = sem("g")
        s_gm = sem("gm")
        s_seg = sem("seg")
        s_decay = sem("decay")
        s_mix = sem("mix")
        s_xhp = sem("xhp")
        s_xh = sem("xh")
        s_xw = sem("xw")
        s_xd = sem("xd")
        s_y = sem("y")
        s_stp = sem("stp")
        s_state = sem("state")
        s_yg = sem("yg")
        s_ssq = sem("ssq")
        s_msq = sem("msq")
        s_rr = sem("rr")
        s_ygTp = sem("ygTp")
        s_ygT = sem("ygT")
        s_o = sem("o")
        s_x = sem("x")
        s_dve = sem("dve")
        block = ctx.enter_context(nc.Block())
        XB, ZB, SEG, Y1, Y2, SMALL, STP = (4, 5), (7, 2), 2, 4, 5, 6, 7

        def heads(ap):
            return ap.rearrange("p (h q) -> p h q", h=NH)

        def per_head(ap, n=HD):
            return ap.unsqueeze(2).to_broadcast([P, NH, n])

        @block.tensor
        def _(pe):
            for b in range(BATCH):
                xT = T.xnT[:, b, :, :]
                if b:
                    pe.wait_ge(s_x, b * TPB)
                norm.tensor(pe, b)
                pe.wait_ge(norm.ready, b + 1)
                for ct in range(CT):
                    i = b * CT + ct
                    if i >= 2:
                        pe.wait_ge(s_conv, i - 1)
                    for k in range(KD):
                        last = pe.matmul(ps[:, XB[i % 2], :], T.w_in[:, k, DI + ct * P:DI + (ct + 1) * P], xT[:, k, :],
                                         start=(k == 0), stop=(k == KD - 1))
                    last.then_inc(s_xbc, 1)
                for t in range(TPB):
                    for k in range(KD):
                        last = pe.matmul(ps[:, SMALL, t * NH:(t + 1) * NH], xT[:, k, t * P:(t + 1) * P],
                                         T.w_in[:, k, DI + CD:IN_PROJ], start=(k == 0), stop=(k == KD - 1))
                last.then_inc(s_dt, 1)
                for t in range(TPB):
                    j = b * TPB + t
                    if j >= 2:
                        pe.wait_ge(s_zs, j - 1)
                    for k in range(KD):
                        last = pe.matmul(ps[:, ZB[j % 2], :], xT[:, k, t * P:(t + 1) * P], T.w_in[:, k, 0:DI],
                                         start=(k == 0), stop=(k == KD - 1))
                    last.then_inc(s_z, 1)
                pe.wait_ge(s_a, b + 1)
                for n, w in enumerate((T.upto, T.after, T.ones)):
                    last = pe.matmul(ps[:, SMALL, (n + 1) * NS:(n + 2) * NS], w[:, :], a, start=True, stop=True)
                last.then_inc(s_cum, 1)
                pe.wait_ge(s_zs, (b + 1) * TPB)
                for c in range(TPB):
                    n, q = b * TPB + c, (b * TPB + c) % 2
                    cols = slice(c * P, (c + 1) * P)
                    pe.wait_ge(s_silu, (b + 1) * CT)
                    if n:
                        pe.wait_ge(s_ygT, n)
                    for e in range(ET):
                        last = pe.transpose(ps[:, 0, e * P:(e + 1) * P], xcT[:, e, cols], T.ident[:, :])
                    last.then_inc(s_xhp, 1)
                    if n:
                        pe.wait_ge(s_gm, 2 * n)
                    pe.transpose(ps[:, 1, P:2 * P], xcT[:, ET, cols], T.ident[:, :])
                    pe.matmul(ps[:, 1, 0:P], xcT[:, ET, cols], xcT[:, ET + 1, cols], start=True,
                              stop=True).then_inc(s_g, 1)
                    pe.wait_ge(s_ra, n + 1)
                    if n:
                        pe.wait_ge(s_decay, n)
                    for i in range(2):
                        last = pe.matmul(ps[:, SEG + i, :], T.after[:, :], rhs_a[:, q, 4 * i:4 * i + 4, :], start=True,
                                         stop=True)
                    last.then_inc(s_seg, 1)
                    pe.wait_ge(s_mix, n + 1)
                    pe.wait_ge(s_xh, n + 1)
                    if c:
                        pe.wait_ge(s_state, b * (TPB - 1) + c)
                        pe.matmul(ps[:, Y2, :], xcT[:, ET + 1, cols], state[:, (c - 1) % 2, :], start=True, stop=True)
                    for h in range(NH):
                        last = pe.matmul(ps[:, Y1, h * HD:(h + 1) * HD], mix[:, q, h, :],
                                         xh[:, q, h * HD:(h + 1) * HD], start=True, stop=True)
                    last.then_inc(s_y, 1)
                    if c < TPB - 1:
                        pe.wait_ge(s_xw, n + 1)
                        pe.matmul(ps[:, STP, :], b_tok[:, q, :], xw[:, q, :], start=True, stop=True).then_inc(s_stp, 1)
                    pe.wait_ge(s_yg, n + 1)
                    for e in range(ET):
                        last = pe.transpose(ps[:, 0, e * P:(e + 1) * P], yg[:, q, e * P:(e + 1) * P], T.ident[:, :])
                    last.then_inc(s_ygTp, 1)
                    pe.wait_ge(s_ygT, n + 1)
                    for e in range(ET):
                        last = pe.matmul(ps[:, SMALL, DM:2 * DM], ygT[:, q, e, :], T.w_out[:, e, :], start=(e == 0),
                                         stop=(e == ET - 1))
                    last.then_inc(s_o, 1)

        @block.scalar
        def _(act):
            for b in range(BATCH):
                norm.scalar(act, b)

                def silu(i):
                    act.wait_ge(s_conv, i + 1)
                    act.activation(xcT[:, i % CT, :], acc[:, i % 2, :], ACT.Silu).then_inc(s_silu, 1)

                for ct in range(CT):
                    i = b * CT + ct
                    act.wait_ge(s_xbc, i + 1)
                    if i >= 2:
                        act.wait_ge(s_silu, i - 1)
                    act.activation(acc[:, i % 2, :], ps[:, XB[i % 2], :], ACT.Identity,
                                   bias=T.cols[:, C_CB + ct:C_CB + ct + 1],
                                   scale=T.cols[:, C_CW + 4 * ct + 3:C_CW + 4 * ct + 4]).then_inc(s_pre, 1)
                    if ct:
                        silu(i - 1)
                silu(b * CT + CT - 1)
                for t in range(TPB):
                    j = b * TPB + t
                    act.wait_ge(s_z, j + 1)
                    act.activation(zs[:, t, :], ps[:, ZB[j % 2], :], ACT.Silu).then_inc(s_zs, 1)
                act.wait_ge(s_na, b + 1)
                act.activation(u, na, ACT.Exp).then_inc(s_u, 1)
                if b == 0:
                    act.activation(neg_a[:, :], T.rows[:, R_AL:R_AL + NH], ACT.Exp).then_inc(s_nega, 1)
                act.wait_ge(s_cum, b + 1)
                act.activation(ex[:, :, :], ps[:, SMALL, NS:4 * NS].rearrange("p (n s) -> p n s", n=3),
                               ACT.Exp).then_inc(s_ex, 1)
                for c in range(TPB):
                    n, q = b * TPB + c, (b * TPB + c) % 2
                    act.wait_ge(s_xhp, n + 1)
                    act.activation(xh[:, q, :], ps[:, 0, :], ACT.Copy).then_inc(s_xh, 1)
                    act.wait_ge(s_seg, n + 1)
                    act.activation(decay[:, q, :, :].rearrange("p h t -> p (h t)"),
                                   ps[:, SEG:SEG + 2, :].rearrange("p i t -> p (i t)"), ACT.Exp).then_inc(s_decay, 1)
                    act.wait_ge(s_yg, n + 1)
                    act.activation(sq[:, :], yg[:, q, :], ACT.Square, accum_out=ssq[:, n:n + 1]).then_inc(s_ssq, 1)
                    act.wait_ge(s_ygTp, n + 1)
                    act.activation(ygT[:, q, :, :].rearrange("p e t -> p (e t)"), ps[:, 0, :],
                                   ACT.Copy).then_inc(s_ygT, 1)
                    act.wait_ge(s_ssq, n + 1)

        @block.gpsimd
        def _(pool):
            for b in range(BATCH):
                norm.gpsimd(pool, b)
                pool.wait_ge(s_ex, b + 1)
                pool.wait_ge(s_a, b + 1)
                pool.tensor_tensor(dw, ex[:, 1, :], dts, ALU.mult).then_inc(s_dw, 1)
                for c in range(TPB):
                    n, q = b * TPB + c, (b * TPB + c) % 2
                    if n >= 2:
                        pool.wait_ge(s_seg, n - 1)
                    pool.tensor_tensor(rhs_a[:, q, :, :], T.upto[:, :].unsqueeze(1).to_broadcast([P, NH, P]),
                                       per_head(a[:, c * NH:(c + 1) * NH], P), ALU.mult).then_inc(s_ra, 1)
                    pool.wait_ge(s_xh, n + 1)
                    if n >= 2:
                        pool.wait_ge(s_yg, n - 1)
                    pool.tensor_tensor(heads(xd[:, q, :]), heads(xh[:, q, :]), per_head(T.rows[:, R_D:R_D + NH]),
                                       ALU.mult).then_inc(s_xd, 1)
                    pool.wait_ge(s_dw, b + 1)
                    if c >= 2:
                        pool.wait_ge(s_stp, b * (TPB - 1) + c - 1)
                    elif b:
                        pool.wait_ge(s_stp, b * (TPB - 1))
                    pool.tensor_tensor(heads(xw[:, q, :]), heads(xh[:, q, :]), per_head(dw[:, c * NH:(c + 1) * NH]),
                                       ALU.mult).then_inc(s_xw, 1)
                    pool.wait_ge(s_msq, n + 1)
                    pool.tensor_tensor(rr[:, n:n + 1], msq[:, n:n + 1], T.half[:, 0:1], ALU.pow).then_inc(s_rr, 1)

        @block.vector
        def _(dve):
            done = [0]

            def link(ins):
                done[0] += 1
                ins.then_inc(s_dve, 1)
                dve.wait_ge(s_dve, done[0])

            for b in range(BATCH):
                norm.vector(dve, b)
                for ct in range(CT):
                    i = b * CT + ct
                    dve.wait_ge(s_pre, i + 1)
                    for lag in range(1, DCONV):
                        w = T.cols[:, C_CW + 4 * ct + 3 - lag:C_CW + 4 * ct + 4 - lag]
                        ins = dve.scalar_tensor_tensor(acc[:, i % 2, lag:SEQ], ps[:, XB[i % 2], 0:SEQ - lag], w,
                                                       acc[:, i % 2, lag:SEQ], ALU.mult, ALU.add)
                        if lag < DCONV - 1:
                            link(ins)
                        else:
                            ins.then_inc(s_conv, 1)
                dve.wait_ge(s_dt, b + 1)
                if b:
                    dve.wait_ge(s_ra, b * TPB)
                    dve.wait_ge(s_dw, b)
                    dve.wait_ge(s_cum, b)
                for c in range(TPB):
                    ins = dve.tensor_tensor(v[:, c * NH:(c + 1) * NH], ps[:, SMALL, c * NH:(c + 1) * NH],
                                            T.rows[:, R_DTB:R_DTB + NH], ALU.add)
                link(ins)
                dve.scalar_tensor_tensor(na, v, -1.0, v, ALU.mult, ALU.min).then_inc(s_na, 1)
                link(dve.tensor_scalar(rl, v, 0.0, None, ALU.max))
                dve.wait_ge(s_u, b + 1)
                link(dve.tensor_scalar(s1, u, 2.0, None, ALU.add))
                link(dve.reciprocal(s2, s1))
                link(dve.tensor_tensor(s1, u, s2, ALU.mult))
                link(dve.tensor_tensor(s2, s1, s1, ALU.mult))
                link(dve.tensor_scalar(s3, s2, 2.0 / 17, 2.0 / 15, ALU.mult, ALU.add))
                for k in range(13, -1, -2):
                    link(dve.tensor_tensor(s4, s3, s2, ALU.mult))
                    if k > 0:
                        link(dve.tensor_scalar(s3, s4, 2.0 / k, None, ALU.add))
                link_last = dve.tensor_tensor(s4, s3, s1, ALU.mult)
                link(link_last)
                link(dve.tensor_tensor(dts, s4, rl, ALU.add))
                if b == 0:
                    dve.wait_ge(s_nega, 1)
                    link(dve.tensor_scalar(neg_a[:, :], neg_a[:, :], -1.0, None, ALU.mult))
                dve.tensor_tensor(a.rearrange("p (c h) -> p c h", h=NH), dts.rearrange("p (c h) -> p c h", h=NH),
                                  neg_a[:, :].unsqueeze(1).to_broadcast([P, TPB, NH]), ALU.mult).then_inc(s_a, 1)
                for c in range(TPB):
                    n, q = b * TPB + c, (b * TPB + c) % 2
                    dve.wait_ge(s_g, n + 1)
                    dve.tensor_tensor(gm[:, q, :], ps[:, 1, 0:P], T.upto[:, :], ALU.mult).then_inc(s_gm, 1)
                    dve.tensor_copy(b_tok[:, q, :], ps[:, 1, P:2 * P]).then_inc(s_gm, 1)
                    dve.wait_ge(s_gm, 2 * n + 2)
                    dve.wait_ge(s_decay, n + 1)
                    if n >= 2:
                        dve.wait_ge(s_y, n - 1)
                    for h in range(NH):
                        ins = dve.scalar_tensor_tensor(mix[:, q, h, :], decay[:, q, h, :],
                                                       dts[:, c * NH + h:c * NH + h + 1], gm[:, q, :], ALU.mult,
                                                       ALU.mult)
                    ins.then_inc(s_mix, 1)
                    dve.wait_ge(s_y, n + 1)
                    dve.wait_ge(s_ex, b + 1)
                    dve.wait_ge(s_xd, n + 1)
                    link(dve.tensor_tensor(y[:, 0, :], ps[:, Y1, :], xd[:, q, :], ALU.add))
                    if c:
                        link(dve.tensor_tensor(heads(y[:, 1, :]), heads(ps[:, Y2, :]),
                                               per_head(ex[:, 0, c * NH:(c + 1) * NH]), ALU.mult))
                        link(dve.tensor_tensor(y[:, 2, :], y[:, 0, :], y[:, 1, :], ALU.add))
                    dve.wait_ge(s_zs, (b + 1) * TPB)
                    if n >= 2:
                        dve.wait_ge(s_ygTp, n - 1)
                    dve.tensor_tensor(yg[:, q, :], y[:, 2 if c else 0, :], zs[:, c, :], ALU.mult).then_inc(s_yg, 1)
                    if c < TPB - 1:
                        if c:
                            link(dve.tensor_tensor(heads(st_dec[:, :]), heads(state[:, (c - 1) % 2, :]),
                                                   per_head(ex[:, 2, c * NH:(c + 1) * NH]), ALU.mult))
                        dve.wait_ge(s_stp, b * (TPB - 1) + c + 1)
                        if c:
                            dve.tensor_tensor(state[:, c % 2, :], st_dec[:, :], ps[:, STP, :],
                                              ALU.add).then_inc(s_state, 1)
                        else:
                            dve.tensor_copy(state[:, c % 2, :], ps[:, STP, :]).then_inc(s_state, 1)
                    dve.wait_ge(s_ssq, n + 1)
                    dve.tensor_scalar(msq[:, n:n + 1], ssq[:, n:n + 1], 1.0 / DI, EPS, ALU.mult,
                                      ALU.add).then_inc(s_msq, 1)
                    dve.wait_ge(s_rr, n + 1)
                    dve.wait_ge(s_o, n + 1)
                    dve.scalar_tensor_tensor(T.x[:, n, :], ps[:, SMALL, DM:2 * DM], rr[:, n:n + 1], T.x[:, n, :],
                                             ALU.mult, ALU.add).then_inc(s_x, 1)
            dve.wait_ge(s_x, NT)


def ffn(nc, T, tag, out=None):
    with ExitStack() as ctx:
        def sb(name, shape, dt=F32):
            return ctx.enter_context(nc.sbuf_tensor(f"{tag}_{name}", shape, dt))

        def sem(name):
            return ctx.enter_context(nc.semaphore(f"{tag}_{name}"))

        ps = T.ps
        lg = sb("lg", [P, NT, NE])
        top = sb("top", [P, NT, NE])
        idx = sb("idx", [P, NT, NE], U32)
        idf = sb("idf", [P, NT, NE])
        neg = sb("neg", [P, NT])
        pr = sb("pr", [P, NT, NE])
        pk = sb("pk", [P, NT, 2])
        psum_ = sb("psum", [P, NT])
        rs = sb("rs", [P, NT])
        w = sb("w", [P, NT, 2])
        wsum = sb("wsum", [P, NT])
        oh = sb("oh", [P, NT, 2, NE])
        ohw = sb("ohw", [P, NT, 2, NE])
        ohd = sb("ohd", [P, NT, 2, NE])
        tm = sb("tm", [P, 2, 2, P])
        tmT = sb("tmT", [P, 2, SEQ])
        aT = sb("aT", [P, 2, FT, SEQ])
        t2 = sb("t2", [P, 2, 3, P])
        t2T = sb("t2T", [P, 2, P])
        xa = sb("xa", [P, 2, 3, DM])
        norm = Norm(nc, ctx, T, tag + "_ln")
        s_rt = sem("rt")
        s_lg = sem("lg")
        s_neg = sem("neg")
        s_pr = sem("pr")
        s_tm = sem("tm")
        s_tmTp = sem("tmTp")
        s_tmT = sem("tmT")
        s_h0 = sem("h0")
        s_g0 = sem("g0")
        s_h1 = sem("h1")
        s_g1 = sem("g1")
        s_dn = sem("dn")
        s_t2 = sem("t2")
        s_xa = sem("xa")
        s_t2p = sem("t2p")
        s_t2T = sem("t2T")
        s_l2 = sem("l2")
        s_x = sem("x")
        s_out = sem("out")
        s_dve = sem("dve")
        block = ctx.enter_context(nc.Block())
        RT, HB, DN, TP, L2 = (2, 3), (6, 7, 2, 3), (0, 1), 4, 5

        def by_rank(ap):
            return ap.rearrange("p (e r) -> p e r", e=NE)

        def per_rank(ap):
            return ap.unsqueeze(2).to_broadcast([P, NE, RK])

        @block.tensor
        def _(pe):
            for b in range(BATCH):
                xT = T.xnT[:, b, :, :]
                if b:
                    pe.wait_ge(s_x, b * TPB)
                norm.tensor(pe, b)
                pe.wait_ge(norm.ready, b + 1)
                for t in range(TPB):
                    g = b * TPB + t
                    if t >= 2:
                        pe.wait_ge(s_tm, g - 1)
                    for k in range(KD):
                        last = pe.matmul(ps[:, RT[g % 2], 0:NE + P], xT[:, k, t * P:(t + 1) * P], T.w_ra[:, k, :],
                                         start=(k == 0), stop=(k == KD - 1))
                    last.then_inc(s_rt, 1)
                for t in range(TPB):
                    g = b * TPB + t
                    pe.wait_ge(s_tm, g + 1)
                    for s in range(2):
                        last = pe.transpose(ps[:, TP + s, t * P:(t + 1) * P], tm[:, g % 2, s, :], T.ident[:, :])
                    last.then_inc(s_tmTp, 1)
                pe.wait_ge(s_tmT, b + 1)

                def second(f):
                    i = b * FT + f
                    pe.wait_ge(s_g0, i + 1)
                    pe.matmul(ps[:, HB[f % 4], :], T.b1l[:, f * P:(f + 1) * P], tmT[:, 1, :], start=False, stop=True,
                              skip_group_check=True).then_inc(s_h1, 1)

                for f in range(FT):
                    i = b * FT + f
                    if f >= 4:
                        pe.wait_ge(s_g1, i - 3)
                    o = ps[:, HB[f % 4], :]
                    for k in range(KD):
                        pe.matmul(o, T.w1[:, k, f * P:(f + 1) * P], xT[:, k, :], start=(k == 0), stop=False,
                                  skip_group_check=True)
                    pe.matmul(o, T.b1l[:, f * P:(f + 1) * P], tmT[:, 0, :], start=False, stop=True,
                              skip_group_check=True).then_inc(s_h0, 1)
                    if f:
                        second(f - 1)
                second(FT - 1)
                pe.wait_ge(s_g1, (b + 1) * FT)
                for t in range(TPB):
                    g = b * TPB + t
                    if t:
                        pe.wait_ge(s_xa, g)
                    for s in range(2):
                        for f in range(FT):
                            last = pe.matmul(ps[:, DN[s], 0:DM + P], aT[:, s, f, t * P:(t + 1) * P], T.w2a[:, f, :],
                                             start=(f == 0), stop=(f == FT - 1))
                    last.then_inc(s_dn, 1)
                    pe.wait_ge(s_t2, g + 1)
                    pe.transpose(ps[:, TP, 0:P], t2[:, g % 2, 2, :], T.ident[:, :]).then_inc(s_t2p, 1)
                    pe.wait_ge(s_t2T, g + 1)
                    if t:
                        pe.wait_ge(s_x, g)
                    pe.matmul(ps[:, L2, 0:DM], t2T[:, g % 2, :], T.b2l[:, :], start=True, stop=True).then_inc(s_l2, 1)

        @block.scalar
        def _(act):
            for b in range(BATCH):
                norm.scalar(act, b)
                for g in range(b * TPB, (b + 1) * TPB):
                    act.wait_ge(s_neg, g + 1)
                    act.activation(pr[:, g, :], lg[:, g, :], ACT.Exp, bias=neg[:, g:g + 1],
                                   accum_out=psum_[:, g:g + 1]).then_inc(s_pr, 1)
                    act.activation(pk[:, g, :], top[:, g, 0:2], ACT.Exp, bias=neg[:, g:g + 1]).then_inc(s_pr, 1)
                act.wait_ge(s_tmTp, (b + 1) * TPB)
                act.activation(tmT[:, :, :], ps[:, TP:TP + 2, :], ACT.Copy).then_inc(s_tmT, 1)
                if b:
                    act.wait_ge(s_dn, b * TPB)

                def gelu(f, s, ready, done):
                    i = b * FT + f
                    act.wait_ge(ready, i + 1)
                    act.activation(aT[:, s, f, :], ps[:, HB[f % 4], :], ACT.Gelu_apprx_tanh,
                                   bias=T.cols[:, C_B1 + f:C_B1 + f + 1]).then_inc(done, 1)

                for f in range(FT):
                    gelu(f, 0, s_h0, s_g0)
                    if f:
                        gelu(f - 1, 1, s_h1, s_g1)
                gelu(FT - 1, 1, s_h1, s_g1)
                for t in range(TPB):
                    g = b * TPB + t
                    act.wait_ge(s_t2p, g + 1)
                    act.activation(t2T[:, g % 2, :], ps[:, TP, 0:P], ACT.Copy).then_inc(s_t2T, 1)

        @block.gpsimd
        def _(pool):
            for b in range(BATCH):
                norm.gpsimd(pool, b)

        @block.vector
        def _(dve):
            done = [0]

            def link(ins):
                done[0] += 1
                ins.then_inc(s_dve, 1)
                dve.wait_ge(s_dve, done[0])

            for b in range(BATCH):
                norm.vector(dve, b)
                for t in range(TPB):
                    g = b * TPB + t
                    dve.wait_ge(s_rt, g + 1)
                    link(dve.tensor_tensor(lg[:, g, :], ps[:, RT[g % 2], 0:NE], T.rows[:, R_BR:R_BR + NE], ALU.add))
                    link(dve.max(top[:, g, :], lg[:, g, :]))
                    dve.tensor_scalar(neg[:, g:g + 1], top[:, g, 0:1], -1.0, None, ALU.mult).then_inc(s_neg, 1)
                    link(dve.max_index(idx[:, g, :], top[:, g, :], lg[:, g, :]))
                    link(dve.tensor_copy(idf[:, g, :], idx[:, g, :]))
                    for s in range(2):
                        ins = dve.tensor_scalar(oh[:, g, s, :], T.iota8, idf[:, g, s:s + 1], None, ALU.is_equal)
                    link(ins)
                    dve.tensor_scalar(ohd[:, g, 0, :], oh[:, g, 0, :], LORA, None, ALU.mult)
                    link(dve.tensor_tensor(ohd[:, g, 1, :], oh[:, g, 1, :], oh[:, g, 0, :], ALU.subtract))
                    link(dve.tensor_scalar(ohd[:, g, 1, :], ohd[:, g, 1, :], LORA, None, ALU.mult))
                    if g >= 2:
                        dve.wait_ge(s_tmTp, g - 1)
                    for s in range(2):
                        ins = dve.tensor_tensor(by_rank(tm[:, g % 2, s, :]), by_rank(ps[:, RT[g % 2], NE:NE + P]),
                                                per_rank(ohd[:, g, s, :]), ALU.mult)
                    ins.then_inc(s_tm, 1)
                for t in range(TPB):
                    g = b * TPB + t
                    dve.wait_ge(s_pr, 2 * g + 2)
                    link(dve.reciprocal(rs[:, g:g + 1], psum_[:, g:g + 1]))
                    link(dve.tensor_scalar(w[:, g, :], pk[:, g, :], rs[:, g:g + 1], None, ALU.mult))
                    link(dve.tensor_tensor(wsum[:, g:g + 1], w[:, g, 0:1], w[:, g, 1:2], ALU.add))
                    for s in range(2):
                        ins = dve.tensor_scalar(ohw[:, g, s, :], oh[:, g, s, :], w[:, g, s:s + 1], LORA, ALU.mult,
                                                ALU.mult)
                    link(ins)
                for t in range(TPB):
                    g, q = b * TPB + t, (b * TPB + t) % 2
                    dve.wait_ge(s_dn, g + 1)
                    for s in range(2):
                        ins = dve.tensor_tensor(by_rank(t2[:, q, s, :]), by_rank(ps[:, DN[s], DM:DM + P]),
                                                per_rank(ohw[:, g, s, :]), ALU.mult)
                    link(ins)
                    dve.tensor_tensor(t2[:, q, 2, :], t2[:, q, 0, :], t2[:, q, 1, :], ALU.add).then_inc(s_t2, 1)
                    link(dve.scalar_tensor_tensor(xa[:, q, 0, :], ps[:, DN[0], 0:DM], w[:, g, 0:1], T.x[:, g, :],
                                                  ALU.mult, ALU.add))
                    dve.scalar_tensor_tensor(xa[:, q, 1, :], ps[:, DN[1], 0:DM], w[:, g, 1:2], xa[:, q, 0, :],
                                             ALU.mult, ALU.add).then_inc(s_xa, 1)
                    dve.wait_ge(s_xa, g + 1)
                    link(dve.scalar_tensor_tensor(xa[:, q, 2, :], T.rows[:, R_B2:R_B2 + DM], wsum[:, g:g + 1],
                                                  xa[:, q, 1, :], ALU.mult, ALU.add))
                    dve.wait_ge(s_l2, g + 1)
                    dve.tensor_tensor(T.x[:, g, :], ps[:, L2, 0:DM], xa[:, q, 2, :], ALU.add).then_inc(s_x, 1)
            dve.wait_ge(s_x, NT)

        @block.sync
        def _(sp):
            if out is not None:
                for g in range(NT):
                    b, t = divmod(g, TPB)
                    sp.wait_ge(s_x, g + 1)
                    sp.dma_start(out[b, t * P:(t + 1) * P, :], T.x[:, g, :]).then_inc(s_out, 16)
                sp.wait_ge(s_out, 16 * NT)


def attention(nc, T):
    with ExitStack() as ctx:
        def sb(name, shape, dt=F32):
            return ctx.enter_context(nc.sbuf_tensor("a_" + name, shape, dt))

        def sem(name):
            return ctx.enter_context(nc.semaphore("a_" + name))

        ps = T.ps
        WMAX = SEQ + PRE
        ROUNDS = TOPK // 8
        VW = AD + 1
        qT = sb("qT", [P, QT, SEQ])
        kT = sb("kT", [P, QT, WMAX])
        v = sb("v", [P, TPB, AH, VW])
        pre_v = sb("pre_v", [PRE, AH, VW])
        bqs = sb("bqs", [P, QT])
        k_tok = sb("k_tok", [P, TPB, AH * SLOT])
        q_tok = sb("q_tok", [P, 2, AH * SLOT])
        gram = sb("gram", [P, QT, P])
        k_sum = sb("k_sum", [P, QT, HPT])
        prod = sb("prod", [P, AH * SLOT])
        mom1 = sb("mom1", [P, TPB, AH])
        mom2 = sb("mom2", [P, TPB, AH])
        sd = sb("sd", [P, TPB, AH])
        tmp = sb("tmp", [P, TPB, AH])
        shift = sb("shift", [P, TPB, AH])
        thr0 = sb("thr0", [P, TPB, AH])
        gain = sb("gain", [P, TPB, AH])
        half_p = sb("half_p", [P, AH * TPB])
        y = sb("y", [P, YR, GH, WMAX])
        E = sb("E", [P, ER, GH, WMAX])
        ymax = sb("ymax", [P, YR, GH])
        nmax = sb("nmax", [P, NR, GH])
        junk = sb("junk", [P, 3, GH, WMAX], BF16)
        c0 = sb("c0", [P, 2, GH])
        c1 = sb("c1", [P, 2, GH])
        c2 = sb("c2", [P, 2, GH])
        w = sb("w", [P, 16, GH])
        off0 = sb("off0", [P, 2, GH])
        move = sb("move", [P, 2, GH])
        thr1 = sb("thr1", [P, 2, GH])
        thr2 = sb("thr2", [P, 2, GH])
        hi = sb("hi", [P, 2, GH])
        below = sb("below", [P, GH, WMAX])
        m16 = sb("m16", [P, 2, GH, DEPTH])
        pick = sb("pick", [P, GH, DEPTH - 1])
        part = sb("part", [P, 2, GH, DEPTH])
        gap = sb("gap", [P, GH, DEPTH - 1])
        thr = sb("thr", [P, 2, GH])
        bad = sb("bad", [P, GH])
        any_bad = sb("any_bad", [P, GH])
        tot_bad = sb("tot_bad", [P, GH // 2])
        flags = sb("flags", [P, 2, 1 + GH], I32)
        left = sb("left", [P, WMAX])
        m8 = sb("m8", [P, ROUNDS, 8])
        prT = sb("prT", [P, 2, SEQ])
        preT = sb("preT", [PRE, 2, P])
        rinv = sb("rinv", [P, 2, AH])
        o = sb("o", [P, 2, DM])
        oT = sb("oT", [P, 2, KD, P])
        xa = sb("xa", [P, DM])
        norm = Norm(nc, ctx, T, "a_ln")
        s_bqs = sem("bqs")
        s_qk = sem("qk")
        s_qkT = sem("qkT")
        s_v = sem("v")
        s_vs = sem("vs")
        s_one = sem("one")
        s_pk = sem("pk")
        s_kt = sem("kt")
        s_ktok = sem("ktok")
        s_gram = sem("gram")
        s_gm = sem("gm")
        s_qt = sem("qt")
        s_qtok = sem("qtok")
        s_qg = sem("qg")
        s_mom = sem("mom")
        s_thr0 = sem("thr0")
        s_sc = sem("sc")
        s_y = sem("y")
        s_nmax = sem("nmax")
        s_c0 = sem("c0")
        s_c1 = sem("c1")
        s_c2 = sem("c2")
        s_thr1 = sem("thr1")
        s_thr2 = sem("thr2")
        s_m16 = sem("m16")
        s_flag = sem("flag")
        s_E = sem("E")
        s_sel = sem("sel")
        s_tp = sem("tp")
        s_pT = sem("pT")
        s_pv = sem("pv")
        s_on = sem("on")
        s_oTp = sem("oTp")
        s_oT = sem("oT")
        s_f = sem("f")
        s_x = sem("x")
        s_dve = sem("dve")
        s_pool = sem("pool")
        s_gen = sem("gen")
        s_low = sem("low")
        block = ctx.enter_context(nc.Block())
        QB, VB = (2, 3, 4, 5), (6, 7)
        KTB, GB, QTB, QGB = (2, 3), (4, 5), (2, 3), (6, 7)
        SC, TB, XT, OB, FB = (2, 4), 6, 7, 0, 1
        GPT = AH // GH
        GPB = TPB * GPT
        NG = BATCH * GPB
        LAG = 4

        def place_of(g):
            return g // GPB, g % GPB // GPT, g % GPT * GH

        def width(g):
            return (g % GPB // GPT + 1) * P + PRE

        def wide(i):
            return ps[:, SC[i % 2]:SC[i % 2] + 2, :].rearrange("p a c -> p (a c)")

        def steps(b):
            return range(b * GPB - 1, (b + 1) * GPB + LAG)

        def mine(b, g):
            return b * GPB <= g < (b + 1) * GPB

        @block.tensor
        def _(pe):
            def project(b):
                xT = T.xnT[:, b, :, :]
                norm.tensor(pe, b)
                pe.wait_ge(norm.ready, b + 1)
                for i in range(2 * QT):
                    wt, m = (T.wk, T.wq)[i // QT], i % QT
                    if i >= 4:
                        pe.wait_ge(s_qkT, b * 2 * QT + i - 3)
                    for k in range(KD):
                        last = pe.matmul(ps[:, QB[i % 4], :], wt[:, k, m * P:(m + 1) * P], xT[:, k, :], start=(k == 0),
                                         stop=(k == KD - 1))
                    last.then_inc(s_qk, 1)
                for t in range(TPB):
                    if t >= 2:
                        pe.wait_ge(s_vs, b * TPB + t - 1)
                    for k in range(KD):
                        last = pe.matmul(ps[:, VB[t % 2], 0:DM], xT[:, k, t * P:(t + 1) * P], T.wv[:, k, :],
                                         start=(k == 0), stop=(k == KD - 1))
                    last.then_inc(s_v, 1)
                pe.wait_ge(s_qkT, (b + 1) * 2 * QT)

            def moments(b):
                for j in range(TPB):
                    n = b * TPB + j
                    if j >= 2:
                        pe.wait_ge(s_ktok, n - 1)
                    for m in range(QT):
                        last = pe.transpose(ps[:, KTB[j % 2], m * P:(m + 1) * P], kT[:, m, j * P:(j + 1) * P],
                                            T.ident[:, :])
                    last.then_inc(s_kt, 1)
                pe.wait_ge(s_ktok, (b + 1) * TPB)
                for m in range(QT):
                    for j in range(TPB):
                        kt = k_tok[:, j, m * P:(m + 1) * P]
                        pe.matmul(ps[:, GB[0], m * P:(m + 1) * P], kt, kt, start=(j == 0), stop=(j == TPB - 1))
                    for j in range(TPB):
                        last = pe.matmul(ps[:, GB[1], m:m + 1], k_tok[:, j, m * P:(m + 1) * P], T.ones[:, 0:1],
                                         start=(j == 0), stop=(j == TPB - 1))
                last.then_inc(s_gram, 1)
                pe.wait_ge(s_vs, (b + 1) * TPB)
                for t in range(TPB):
                    n = b * TPB + t
                    if t >= 2:
                        pe.wait_ge(s_qtok, n - 1)
                    for m in range(QT):
                        last = pe.transpose(ps[:, QTB[t % 2], m * P:(m + 1) * P], qT[:, m, t * P:(t + 1) * P],
                                            T.ident[:, :])
                    last.then_inc(s_qt, 1)
                    pe.wait_ge(s_gm, b + 1)
                    if t:
                        pe.wait_ge(s_mom, n)
                    for m in range(QT):
                        q = qT[:, m, t * P:(t + 1) * P]
                        pe.matmul(ps[:, QGB[0], m * P:(m + 1) * P], q, gram[:, m, :], start=True, stop=True)
                        last = pe.matmul(ps[:, QGB[1], m * HPT:(m + 1) * HPT], q, k_sum[:, m, :], start=True, stop=True)
                    last.then_inc(s_qg, 1)
                pe.wait_ge(s_mom, (b + 1) * TPB)
                pe.wait_ge(s_pk, 2)

            def scores(g, u):
                b, t, h0 = place_of(g)
                i, h = g * GH + u, h0 + u
                if i >= 2:
                    pe.wait_ge(s_y, i - 1)
                m, r = h // HPT, SLOT * (h % HPT)
                q = qT[r:r + AD, m, t * P:(t + 1) * P]
                out = wide(i)
                lo, top = t * P, min(width(g), SEQ)
                pe.matmul(out[:, 0:top], q, kT[r:r + AD, m, 0:top], start=True, stop=False, skip_group_check=True)
                last = pe.matmul(out[:, lo:top], T.ident_b[:, :], T.mask_b[:, 0:top - lo], start=False, stop=True,
                                 skip_group_check=True)
                if width(g) > SEQ:
                    pe.matmul(out[:, SEQ:WMAX], q, kT[r:r + AD, m, SEQ:WMAX], start=True, stop=False,
                              skip_group_check=True)
                    last = pe.matmul(out[:, SEQ:WMAX], T.ident_b[:, :], T.mask_b[:, P:DIAG], start=False, stop=True,
                                     skip_group_check=True)
                last.then_inc(s_sc, 1)

            def turn(g, u):
                b, t, h0 = place_of(g)
                i = g * GH + u
                pe.wait_ge(s_sel, i + 1)
                if i:
                    pe.wait_ge(s_pT, i)
                pr = E[:, g % ER, u, :]
                for j in range(t + 1):
                    pe.transpose(ps[:, TB, j * P:(j + 1) * P], pr[:, j * P:(j + 1) * P], T.ident[:, :])
                pe.transpose(ps[0:PRE, XT, 0:P], pr[:, (t + 1) * P:(t + 1) * P + PRE],
                             T.ident[:, :]).then_inc(s_tp, 1)

            def values(g, u):
                b, t, h0 = place_of(g)
                i, h = g * GH + u, h0 + u
                pe.wait_ge(s_pT, i + 1)
                if h == 0 and i:
                    pe.wait_ge(s_on, i // AH)
                out = ps[:, OB, h * VW:(h + 1) * VW]
                for j in range(t + 1):
                    pe.matmul(out, prT[:, i % 2, j * P:(j + 1) * P], v[:, j, h, :], start=(j == 0), stop=False)
                tail = v[0:PRE, t + 1, h, :] if t + 1 < TPB else pre_v[:, h, :]
                pe.matmul(out, preT[:, i % 2, :], tail, start=False, stop=True).then_inc(s_pv, 1)

            def finish(n):
                pe.wait_ge(s_on, n + 1)
                if n:
                    pe.wait_ge(s_x, n)
                for k in range(KD):
                    last = pe.transpose(ps[:, FB, k * P:(k + 1) * P], o[:, n % 2, k * P:(k + 1) * P], T.ident[:, :])
                last.then_inc(s_oTp, 1)
                pe.wait_ge(s_oT, n + 1)
                for k in range(KD):
                    last = pe.matmul(ps[:, FB, DM:2 * DM], oT[:, n % 2, k, :], T.wo[:, k, :], start=(k == 0),
                                     stop=(k == KD - 1))
                last.then_inc(s_f, 1)

            for b in range(BATCH):
                project(b)
                moments(b)
                for k in steps(b):
                    if mine(b, k + 1):
                        scores(k + 1, 0)
                        scores(k + 1, 1)
                    if mine(b, k - LAG):
                        for u in range(GH):
                            turn(k - LAG, u)
                            values(k - LAG, u)
                    if mine(b, k + 1):
                        for u in range(2, GH):
                            scores(k + 1, u)
                    if mine(b, k - LAG - 1) and (k - LAG) % GPT == 0:
                        finish((k - LAG) // GPT - 1)
                finish((b + 1) * TPB - 1)
                pe.wait_ge(s_x, (b + 1) * TPB)

        @block.scalar
        def _(act):
            act.activation(bqs[:, :], T.cols[:, C_BQ:C_BQ + QT], ACT.Copy, scale=AD ** -0.5).then_inc(s_bqs, 1)
            act.wait_ge(s_bqs, 1)

            def project(b):
                norm.scalar(act, b)
                for i in range(2 * QT):
                    m = i % QT
                    act.wait_ge(s_qk, b * 2 * QT + i + 1)
                    if i >= QT:
                        ins = act.activation(qT[:, m, :], ps[:, QB[i % 4], :], ACT.Identity, bias=bqs[:, m:m + 1],
                                             scale=AD ** -0.5)
                    else:
                        ins = act.activation(kT[:, m, 0:SEQ], ps[:, QB[i % 4], :], ACT.Identity,
                                             bias=T.cols[:, C_BK + m:C_BK + m + 1])
                    ins.then_inc(s_qkT, 1)

            def moments(b):
                for j in range(TPB):
                    act.wait_ge(s_kt, b * TPB + j + 1)
                    act.activation(k_tok[:, j, :], ps[:, KTB[j % 2], :], ACT.Copy).then_inc(s_ktok, 1)
                for t in range(TPB):
                    act.wait_ge(s_qt, b * TPB + t + 1)
                    if t >= 2:
                        act.wait_ge(s_mom, b * TPB + t - 1)
                    act.activation(q_tok[:, t % 2, :], ps[:, QTB[t % 2], :], ACT.Copy).then_inc(s_qtok, 1)

            def count(g, n, bias, out, done, used):
                if g >= 2:
                    act.wait_ge(used, g - 1)
                if g:
                    act.wait_ge(done, g * GH)
                for u in range(GH):
                    if done is s_c0:
                        act.wait_ge(s_y, g * GH + u + 1)
                    act.activation(junk[:, n, u, 0:width(g)], y[:, g % YR, u, 0:width(g)], ACT.Sign, bias=bias[:, u:u + 1],
                                   accum_out=out[:, g % 2, u:u + 1]).then_inc(done, 1)

            def exponents(g):
                act.wait_ge(s_nmax, g + 1)
                if g >= ER:
                    act.wait_ge(s_tp, (g - ER + 1) * GH)
                for u in range(GH):
                    act.activation(E[:, g % ER, u, 0:width(g)], y[:, g % YR, u, 0:width(g)], ACT.Exp,
                                   bias=nmax[:, g % NR, u:u + 1]).then_inc(s_E, 1)

            def turn(g):
                t = place_of(g)[1]
                for u in range(GH):
                    i = g * GH + u
                    act.wait_ge(s_tp, i + 1)
                    if i >= 2:
                        act.wait_ge(s_pv, i - 1)
                    act.activation(prT[:, i % 2, 0:(t + 1) * P], ps[:, TB, 0:(t + 1) * P], ACT.Copy)
                    act.activation(preT[:, i % 2, :], ps[0:PRE, XT, 0:P], ACT.Copy).then_inc(s_pT, 1)

            def turn_out(n):
                act.wait_ge(s_oTp, n + 1)
                act.activation(oT[:, n % 2, :, :], ps[:, FB, 0:DM].rearrange("p (k t) -> p k t", k=KD),
                               ACT.Copy).then_inc(s_oT, 1)

            for b in range(BATCH):
                project(b)
                moments(b)
                act.wait_ge(s_thr0, b + 1)
                for k in steps(b):
                    if mine(b, k):
                        _, t, h0 = place_of(k)
                        count(k, 0, thr0[:, t, h0:h0 + GH], c0, s_c0, s_thr1)
                    if mine(b, k - 1):
                        act.wait_ge(s_thr1, k)
                        count(k - 1, 1, thr1[:, (k - 1) % 2, :], c1, s_c1, s_thr2)
                    if mine(b, k - 2):
                        exponents(k - 2)
                    if mine(b, k - LAG):
                        turn(k - LAG)
                    if mine(b, k - 2):
                        act.wait_ge(s_thr2, k - 1)
                        count(k - 2, 2, thr2[:, k % 2, :], c2, s_c2, s_flag)
                    if mine(b, k - LAG - 1) and (k - LAG) % GPT == 0:
                        turn_out((k - LAG) // GPT - 1)
                turn_out((b + 1) * TPB - 1)

        @block.gpsimd
        def _(pool):
            done = [0]

            def link(ins):
                done[0] += 1
                ins.then_inc(s_pool, 1)
                pool.wait_ge(s_pool, done[0])

            def heads_of(ap):
                return ap.rearrange("p t h -> p (t h)")

            pool.memset(half_p[:, :], 0.5).then_inc(s_pk, 1)
            pool.tensor_copy(kT[:, :, SEQ:WMAX], T.pre_k[:, :, :]).then_inc(s_pk, 1)
            pool.memset(part[:, :, :, :], 0.0).then_inc(s_one, 1)
            pool.memset(v[:, :, :, AD:VW], 1.0).then_inc(s_one, 1)
            pool.memset(pre_v[:, :, AD:VW], 1.0).then_inc(s_one, 1)
            pool.tensor_copy(pre_v[:, :, 0:AD], T.pre_v[:, :].rearrange("p (h d) -> p h d", h=AH)).then_inc(s_one, 1)
            pool.wait_ge(s_pk, 2)
            pool.wait_ge(s_one, 4)

            def first_thresholds(b):
                pool.wait_ge(s_mom, (b + 1) * TPB)
                if b:
                    pool.wait_ge(s_y, b * GPB * GH)
                    pool.wait_ge(s_c0, b * GPB * GH)
                link(pool.tensor_tensor(tmp[:, :, :], mom1[:, :, :], mom1[:, :, :], ALU.mult))
                link(pool.tensor_tensor(sd[:, :, :], mom2[:, :, :], tmp[:, :, :], ALU.subtract))
                link(pool.tensor_scalar(sd[:, :, :], sd[:, :, :], 1e-20, None, ALU.max))
                link(pool.tensor_tensor(heads_of(tmp[:, :, :]), heads_of(sd[:, :, :]), half_p[:, :], ALU.pow))
                for t in range(TPB):
                    pool.tensor_scalar(thr0[:, t, :], tmp[:, t, :], T.tab[:, t, 0:1], None, ALU.mult)
                    pool.tensor_scalar(gain[:, t, :], tmp[:, t, :], T.tab[:, t, 1:2], None, ALU.mult)
                link(pool.tensor_scalar(sd[:, :, :], tmp[:, :, :], SHIFT, None, ALU.mult))
                pool.tensor_tensor(shift[:, :, :], sd[:, :, :], mom1[:, :, :], ALU.subtract).then_inc(s_thr0, 1)

            def newton(g):
                _, t, h0 = place_of(g)
                q = g % 2
                t0 = thr0[:, t, h0:h0 + GH]
                if g >= 2:
                    pool.wait_ge(s_c1, (g - 1) * GH)
                link(pool.tensor_scalar(off0[:, q, :], c0[:, q, :], float(width(g) - 2 * AIM), None, ALU.add))
                link(pool.tensor_tensor(w[:, 1, :], off0[:, q, :], off0[:, q, :], ALU.mult))
                link(pool.tensor_scalar(w[:, 2, :], w[:, 1, :], FAR, None, ALU.is_gt))
                link(pool.tensor_tensor(w[:, 3, :], w[:, 2, :], off0[:, q, :], ALU.mult))
                link(pool.tensor_tensor(move[:, q, :], w[:, 3, :], gain[:, t, h0:h0 + GH], ALU.mult))
                pool.tensor_tensor(thr1[:, q, :], t0, move[:, q, :], ALU.add).then_inc(s_thr1, 1)

            def secant(g):
                q = g % 2
                link(pool.tensor_scalar(w[:, 5, :], c1[:, q, :], float(width(g) - 2 * AIM), None, ALU.add))
                link(pool.tensor_tensor(w[:, 6, :], off0[:, q, :], w[:, 5, :], ALU.subtract))
                link(pool.tensor_tensor(w[:, 7, :], w[:, 6, :], w[:, 6, :], ALU.mult))
                link(pool.tensor_scalar(w[:, 8, :], w[:, 7, :], 1.0, None, ALU.max))
                link(pool.tensor_tensor(w[:, 9, :], w[:, 8, :], T.minus1[:, 0:GH], ALU.pow))
                link(pool.tensor_tensor(w[:, 10, :], move[:, q, :], move[:, q, :], ALU.mult))
                link(pool.tensor_tensor(w[:, 11, :], w[:, 10, :], w[:, 9, :], ALU.mult))
                link(pool.tensor_tensor(w[:, 12, :], w[:, 11, :], half_p[:, 0:GH], ALU.pow))
                link(pool.tensor_tensor(w[:, 13, :], w[:, 5, :], w[:, 5, :], ALU.mult))
                link(pool.tensor_scalar(w[:, 14, :], w[:, 13, :], FAR, None, ALU.is_gt))
                link(pool.tensor_tensor(w[:, 13, :], w[:, 14, :], w[:, 5, :], ALU.mult))
                link(pool.tensor_tensor(w[:, 15, :], w[:, 13, :], w[:, 12, :], ALU.mult))
                link(pool.tensor_tensor(thr2[:, q, :], thr1[:, q, :], w[:, 15, :], ALU.subtract))
                pool.tensor_scalar(hi[:, q, :], thr2[:, q, :], -1.0, None, ALU.mult).then_inc(s_thr2, 1)

            def pick_threshold(g):
                t, q = place_of(g)[1], g % 2
                pool.wait_ge(s_c2, (g + 1) * GH)
                link(pool.tensor_scalar(w[:, 0, :], c2[:, q, :], -0.5, TOPK - 1 - 0.5 * width(g), ALU.mult, ALU.add))
                shape = [P, GH, DEPTH - 1]
                link(pool.tensor_tensor(gap[:, :, :], T.iota16[:, 0:DEPTH - 1].unsqueeze(1).to_broadcast(shape),
                                        w[:, 0, :].unsqueeze(2).to_broadcast(shape), ALU.subtract))
                link(pool.tensor_scalar(pick[:, :, :], gap[:, :, :], 0.0, None, ALU.is_equal))
                pool.wait_ge(s_m16, (g + 1) * GH)
                pool.tensor_tensor(part[:, 0, :, 0:DEPTH - 1], pick[:, :, :], m16[:, q, :, 0:DEPTH - 1], ALU.mult)
                link(pool.tensor_tensor(part[:, 1, :, 0:DEPTH - 1], pick[:, :, :], m16[:, q, :, 1:DEPTH], ALU.mult))
                half = DEPTH // 2
                while half:
                    link(pool.tensor_tensor(part[:, :, :, 0:half], part[:, :, :, 0:half], part[:, :, :, half:2 * half],
                                            ALU.add))
                    half //= 2
                link(pool.tensor_scalar(w[:, 3, :], part[:, 1, :, 0], 0.0, None, ALU.max))
                link(pool.tensor_tensor(w[:, 4, :], part[:, 0, :, 0], w[:, 3, :], ALU.subtract))
                link(pool.tensor_scalar(w[:, 5, :], w[:, 4, :], 0.0, None, ALU.is_le))
                if g >= 2:
                    pool.wait_ge(s_sel, (g - 1) * GH)
                pool.tensor_scalar(thr[:, q, :], part[:, 0, :, 0], T.tab[:, t, 2:3], T.tab[:, t, 3:4], ALU.mult, ALU.add)
                link(pool.tensor_scalar(bad[:, :], w[:, 5, :], T.tab[:, t, 2:3], None, ALU.mult))
                link(pool.partition_all_reduce(any_bad[:, :], bad[:, :], P, RADD))
                link(pool.tensor_tensor(tot_bad[:, :], any_bad[:, 0:GH // 2], any_bad[:, GH // 2:GH], ALU.add))
                link(pool.tensor_tensor(tot_bad[:, 0:1], tot_bad[:, 0:1], tot_bad[:, 1:2], ALU.add))
                link(pool.tensor_copy(flags[:, q, 0:1], tot_bad[:, 0:1]))
                pool.tensor_copy(flags[:, q, 1:1 + GH], any_bad[:, :]).then_inc(s_flag, 1)

            for b in range(BATCH):
                norm.gpsimd(pool, b)
                first_thresholds(b)
                for k in steps(b):
                    if mine(b, k):
                        pool.wait_ge(s_y, (k + 1) * GH)
                        if k >= NR:
                            pool.wait_ge(s_E, (k - NR + 1) * GH)
                        pool.tensor_scalar(nmax[:, k % NR, :], ymax[:, k % YR, :], -1.0, None,
                                           ALU.mult).then_inc(s_nmax, 1)
                        pool.wait_ge(s_c0, (k + 1) * GH)
                        newton(k)
                    if mine(b, k - 1):
                        pool.wait_ge(s_c1, k * GH)
                        secant(k - 1)
                    if mine(b, k - 2):
                        pick_threshold(k - 2)

        @block.vector
        def _(dve):
            done = [0]

            def link(ins):
                done[0] += 1
                ins.then_inc(s_dve, 1)
                dve.wait_ge(s_dve, done[0])

            def moments(b):
                dve.wait_ge(s_gram, b + 1)
                dve.tensor_tensor(gram[:, :, :], ps[:, GB[0], :].rearrange("p (m c) -> p m c", m=QT),
                                  T.blocks[:, :].unsqueeze(1).to_broadcast([P, QT, P]), ALU.mult)
                dve.tensor_tensor(k_sum[:, :, :], ps[:, GB[1], 0:QT].unsqueeze(2).to_broadcast([P, QT, HPT]),
                                  T.blocks[:, 0:P:SLOT].unsqueeze(1).to_broadcast([P, QT, HPT]),
                                  ALU.mult).then_inc(s_gm, 1)
                if b:
                    dve.wait_ge(s_thr0, b)
                for t in range(TPB):
                    n = b * TPB + t
                    dve.wait_ge(s_qg, n + 1)
                    dve.wait_ge(s_qtok, n + 1)
                    dve.tensor_scalar(mom1[:, t, :], ps[:, QGB[1], 0:AH], 1.0 / SEQ, None, ALU.mult)
                    link(dve.scalar_tensor_tensor(prod[:, :], ps[:, QGB[0], :], 1.0 / SEQ, q_tok[:, t % 2, :],
                                                  ALU.mult, ALU.mult))
                    dve.tensor_reduce(mom2[:, t, :], prod[:, :].rearrange("p (h c) -> p h c", h=AH), AX_X,
                                      ALU.add).then_inc(s_mom, 1)

            def take_scores(g):
                b, t, h0 = place_of(g)
                dve.wait_ge(s_thr0, b + 1)
                if g >= YR:
                    dve.wait_ge(s_E, (g - YR + 1) * GH)
                    dve.wait_ge(s_c2, (g - YR + 1) * GH)
                    dve.wait_ge(s_nmax, g - YR + 1)
                    dve.wait_ge(s_sel, (g - YR + 1) * GH)
                for u in range(GH):
                    i = g * GH + u
                    dve.wait_ge(s_sc, i + 1)
                    dve.tensor_scalar(y[:, g % YR, u, 0:width(g)], wide(i)[:, 0:width(g)],
                                      shift[:, t, h0 + u:h0 + u + 1], None, ALU.add, ALU.max,
                                      accum_out=ymax[:, g % YR, u:u + 1]).then_inc(s_y, 1)

            def largest_below(g):
                q = g % 2
                dve.wait_ge(s_thr2, g + 1)
                if g >= 2:
                    dve.wait_ge(s_flag, g - 1)
                if g:
                    dve.wait_ge(s_m16, g * GH)
                for stage in range(4):
                    for u in range(GH):
                        yu, z = y[:, g % YR, u, 0:width(g)], below[:, u, 0:width(g)]
                        if stage:
                            dve.wait_ge(s_low, (g * 3 + stage - 1) * GH + u + 1)
                        if stage == 0:
                            dve.scalar_tensor_tensor(z, yu, hi[:, q, u:u + 1], yu, ALU.is_lt,
                                                     ALU.mult).then_inc(s_low, 1)
                        elif stage == 1:
                            dve.max(m16[:, q, u, 0:8], z).then_inc(s_low, 1)
                        elif stage == 2:
                            dve.match_replace(z, m16[:, q, u, 0:8], z, SENT).then_inc(s_low, 1)
                        else:
                            dve.max(m16[:, q, u, 8:16], z).then_inc(s_m16, 1)

            def general(g, u):
                wd = width(g)
                yu = y[:, g % YR, u, 0:wd]
                dve.max(m8[:, 0, :], yu).then_inc(s_gen, 1)
                n = 1
                for r in range(ROUNDS):
                    dve.wait_ge(s_gen, n)
                    dve.match_replace(left[:, 0:wd], m8[:, r, :], yu if r == 0 else left[:, 0:wd],
                                      SENT).then_inc(s_gen, 1)
                    n += 1
                    dve.wait_ge(s_gen, n)
                    if r + 1 < ROUNDS:
                        dve.max(m8[:, r + 1, :], left[:, 0:wd]).then_inc(s_gen, 1)
                        n += 1
                dve.scalar_tensor_tensor(E[:, g % ER, u, 0:wd], left[:, 0:wd], SENT, E[:, g % ER, u, 0:wd],
                                         ALU.is_equal, ALU.mult).then_inc(s_gen, 1)
                dve.wait_ge(s_gen, n + 1)
                dve.sem_clear(s_gen)

            def probabilities(g):
                q, wd = g % 2, width(g)
                dve.wait_ge(s_flag, g + 1)
                dve.wait_ge(s_E, (g + 1) * GH)
                any_head = dve.value_load(flags[0:1, q, 0:1])
                with dve.If(any_head > 0):
                    for u in range(GH):
                        bad_head = dve.value_load(flags[0:1, q, 1 + u:2 + u])
                        with dve.If(bad_head > 0):
                            general(g, u)
                            dve.memset(thr[:, q, u:u + 1], SENT)
                            dve.drain()
                for u in range(GH):
                    dve.scalar_tensor_tensor(E[:, g % ER, u, 0:wd], y[:, g % YR, u, 0:wd], thr[:, q, u:u + 1],
                                             E[:, g % ER, u, 0:wd], ALU.is_ge, ALU.mult).then_inc(s_sel, 1)

            def normalise(n):
                dve.wait_ge(s_pv, (n + 1) * AH)
                ov = ps[:, OB, 0:AH * VW].rearrange("p (h d) -> p h d", h=AH)
                link(dve.reciprocal(rinv[:, n % 2, :], ov[:, :, AD]))
                dve.tensor_tensor(o[:, n % 2, :].rearrange("p (h d) -> p h d", h=AH), ov[:, :, 0:AD],
                                  rinv[:, n % 2, :].unsqueeze(2).to_broadcast([P, AH, AD]), ALU.mult).then_inc(s_on, 1)

            def residual(n):
                link(dve.tensor_tensor(xa[:, :], T.x[:, n, :], T.rows[:, R_BO:R_BO + DM], ALU.add))
                dve.wait_ge(s_f, n + 1)
                dve.tensor_tensor(T.x[:, n, :], ps[:, FB, DM:2 * DM], xa[:, :], ALU.add).then_inc(s_x, 1)

            for b in range(BATCH):
                norm.vector(dve, b)
                dve.wait_ge(s_one, 4)
                for t in range(TPB):
                    dve.wait_ge(s_v, b * TPB + t + 1)
                    dve.tensor_tensor(v[:, t, :, 0:AD], ps[:, VB[t % 2], 0:DM].rearrange("p (h d) -> p h d", h=AH),
                                      T.rows[:, R_BV:R_BV + DM].rearrange("p (h d) -> p h d", h=AH),
                                      ALU.add).then_inc(s_vs, 1)
                moments(b)
                for k in steps(b):
                    n = (k - LAG) // GPT - 1
                    if mine(b, k - LAG - 1) and (k - LAG) % GPT == 0:
                        normalise(n)
                    if mine(b, k - 2):
                        largest_below(k - 2)
                    if mine(b, k - 3):
                        probabilities(k - 3)
                    if mine(b, k + 1):
                        take_scores(k + 1)
                    if mine(b, k - LAG - 1 - GPT) and (k - LAG) % GPT == 1:
                        residual(n)
                normalise((b + 1) * TPB - 1)
                residual((b + 1) * TPB - 1)
            dve.wait_ge(s_x, NT)


def hybrid_layer(nc, d, out):
    with ExitStack() as ctx:
        T = place(nc, ctx)
        with nc.sbuf_tensor("w_in", [P, KD, IN_PROJ], F32) as w_in, nc.sbuf_tensor("w_out", [P, ET, DM], F32) as w_out:
            T.w_in, T.w_out = w_in, w_out
            start_up(nc, T, d)
            mamba(nc, T)
        ffn(nc, T, "f1")
        attention(nc, T)
        ffn(nc, T, "f2", out)


def threshold_table():
    import numpy as np

    def quantile(share):
        lo, hi = -8.0, 8.0
        for _ in range(60):
            mid = 0.5 * (lo + hi)
            if 0.5 * (1.0 + math.erf(mid / math.sqrt(2.0))) < share:
                lo = mid
            else:
                hi = mid
        return lo

    tab = np.zeros((P, TPB, 4), np.float32)
    for t in range(TPB):
        for p in range(P):
            n = t * P + p + 1 + PRE
            share = min(max(1.0 - AIM / n, 0.02), 0.98)
            z = quantile(share)
            density = math.exp(-0.5 * z * z) / math.sqrt(2.0 * math.pi)
            tab[p, t] = (-(z + SHIFT), -0.5 / (n * density), float(n > TOPK), 0.1 * NEG * (n <= TOPK))
    return tab


def kernel(**inputs):
    import numpy as np
    import concourse.bacc as bacc
    from concourse.bass_utils import run_bass_kernel_spmd

    a = {k[3:]: np.asarray(v) for k, v in inputs.items()}

    def columns(v):
        return v.reshape(-1, P).T

    def slots(w):
        p = np.zeros((w.shape[0], AH, SLOT), w.dtype)
        p[:, :, :AD] = w.reshape(w.shape[0], AH, AD)
        return p.reshape(w.shape[0], AH * SLOT)

    cw = a["attn_a_conv_w"].reshape(CT, P, DCONV).transpose(1, 0, 2).reshape(P, CT * DCONV)
    bq, bk = (columns(slots(a[f"attn_b_{n}"][None])[0]) for n in ("bq", "bk"))
    host = {
        "x": a["attn_a_u"],
        "cols": np.concatenate([cw, columns(a["attn_a_conv_b"]), columns(a["attn_a_norm_w"]), columns(a["ffn_b1"]),
                                bq, bk], axis=1),
        "rows": np.concatenate([a["attn_a_dt_bias"], a["attn_a_A_log"], a["attn_a_D"], a["ffn_br"], a["ffn_b2"],
                                a["attn_b_bv"], a["attn_b_bo"]]),
        "w_in": a["attn_a_W_in"].T,
        "w_out": a["attn_a_W_out"].T,
        "w_ra": np.concatenate([a["ffn_Wr"], a["ffn_A1"].reshape(NE * RK, DM).T], axis=1),
        "w1": a["ffn_W1"],
        "b1l": a["ffn_B1"].transpose(0, 2, 1).reshape(NE * RK, FF),
        "w2a": np.concatenate([a["ffn_W2"], a["ffn_A2"].reshape(NE * RK, FF).T], axis=1),
        "b2l": a["ffn_B2"].transpose(0, 2, 1).reshape(NE * RK, DM),
        "wq": slots(a["attn_b_Wq"]),
        "wk": slots(a["attn_b_Wk"]),
        "wv": a["attn_b_Wv"],
        "wo": a["attn_b_Wo"],
        "pre_k": slots(a["attn_b_pk"][0]).T.reshape(QT, P, PRE).transpose(1, 0, 2),
        "pre_v": a["attn_b_pv"][0],
    }
    host["tab"] = threshold_table()
    nc = bacc.Bacc("TRN2", target_bir_lowering=False, num_devices=1)
    arrays, d = {}, {}
    for name, v in host.items():
        v = np.ascontiguousarray(v)
        arrays[f"in_{name}"] = v
        d[name] = nc.dram_tensor(f"in_{name}", v.shape, mybir.dt.from_np(v.dtype), kind="ExternalInput").ap()
    out = nc.dram_tensor("out", (BATCH, SEQ, DM), F32, kind="ExternalOutput").ap()
    hybrid_layer(nc, d, out)
    r = run_bass_kernel_spmd(nc, [arrays], core_ids=[0])
    return r.results[0]["out"]
```

```python
import math
from contextlib import ExitStack

import concourse.bass as bass
from concourse import mybir

P = 128
BATCH, SEQ, DM = 2, 512, 256
TPB = SEQ // P
NT = BATCH * TPB
KD = DM // P
EPS = 1e-5

DI, DS, NH, HD, DCONV = 512, 128, 8, 64, 4
CD = DI + 2 * DS
CT = CD // P
IN_PROJ = DI + CD + NH
ET = DI // P

AH, AD, PRE, TOPK = 16, 16, 4, 64
SLOT = 32
QT = AH * SLOT // P
KT = AH * AD // P
HPT = P // SLOT
SENT = -3.0e38
NEG = -1.0e30
GH = 4
YR, ER, NR = 5, 3, 4
DEPTH = 16
AIM = TOPK - DEPTH // 2
FAR = (DEPTH - 1.5) ** 2
SHIFT = 2.0
DIAG = P + PRE

NE, RK, FF = 8, 16, 1024
FT = FF // P
LORA = 2.0

F32 = mybir.dt.float32
BF16 = mybir.dt.bfloat16
I32 = mybir.dt.int32
U32 = mybir.dt.uint32
ALU = mybir.AluOpType
ACT = mybir.ActivationFunctionType
AX_X = mybir.AxisListType.X
RADD = bass.bass_isa.ReduceOp.add

LATER = 11

C_CW, C_CB, C_NW, C_B1, C_BQ, C_BK = 0, 24, 30, 34, 42, 46
NCOL = 48
R_DTB, R_AL, R_D, R_BR, R_B2, R_BV, R_BO = 0, 8, 16, 24, 32, 288, 544
NROW = 800


class Tiles:
    pass


def place(nc, ctx):
    def sb(name, shape, dt=F32):
        return ctx.enter_context(nc.sbuf_tensor(name, shape, dt))

    T = Tiles()
    T.x = sb("x", [P, NT, DM])
    T.xn = sb("xn", [P, NT, DM])
    T.xnT = sb("xnT", [P, BATCH, KD, SEQ])
    T.ln_st = sb("ln_st", [P, NT, 6])
    T.ln_mv = sb("ln_mv", [P, NT, 2])
    T.ln_ve = sb("ln_ve", [P, NT])
    T.ln_r = sb("ln_r", [P, NT])
    T.cols = sb("cols", [P, NCOL])
    T.rows = sb("rows", [P, NROW])
    T.wq = sb("wq", [P, KD, AH * SLOT])
    T.wk = sb("wk", [P, KD, DM])
    T.wv = sb("wv", [P, KD, DM])
    T.wo = sb("wo", [P, KD, DM])
    T.pre_k = sb("pre_k", [P, KT, PRE])
    T.w_ra = sb("w_ra", [P, KD, NE + P])
    T.w1 = sb("w1", [P, KD, FF])
    T.b1l = sb("b1l", [P, FF])
    T.w2a = sb("w2a", [P, FT, DM + P])
    T.b2l = sb("b2l", [P, DM])
    T.ident = sb("ident", [P, P])
    T.ones = sb("ones", [P, P])
    T.upto = sb("upto", [P, P])
    T.after = sb("after", [P, P])
    T.half = sb("half", [P, NT])
    T.iota16 = sb("iota16", [P, DEPTH])
    T.iota8 = T.iota16[:, 0:NE]
    T.minus1 = sb("minus1", [P, GH])
    T.blocks = sb("blocks", [P, P])
    T.tab = sb("tab", [P, TPB, 4])
    T.ident_b = sb("ident_b", [P, P], BF16)
    T.mask_b = sb("mask_b", [P, DIAG], BF16)
    T.ps = ctx.enter_context(nc.psum_tensor("ps", [P, 8, 512], F32))
    return T


def start_up(nc, T, d):
    with ExitStack() as ctx:
        s_load = ctx.enter_context(nc.semaphore("s_load"))
        s_zero = ctx.enter_context(nc.semaphore("s_zero"))
        s_const = ctx.enter_context(nc.semaphore("s_const"))
        s_nw = ctx.enter_context(nc.semaphore("s_nw"))
        loads = [
            (T.x[:, :, :], d["x"].rearrange("b (t p) m -> p (b t) m", p=P)),
            (T.cols[:, :], d["cols"]),
            (T.rows[:, :], d["rows"].partition_broadcast(P)),
            (T.w_in[:, :, :], d["w_in"].rearrange("(k p) e -> p k e", p=P)),
            (T.w_out[:, :, :], d["w_out"].rearrange("(k p) e -> p k e", p=P)),
        ]
        later_loads = [
            (T.w_ra[:, :, :], d["w_ra"].rearrange("(k p) e -> p k e", p=P)),
            (T.w1[:, :, :], d["w1"].rearrange("(k p) e -> p k e", p=P)),
            (T.b1l[:, :], d["b1l"]),
            (T.w2a[:, :, :], d["w2a"].rearrange("(k p) e -> p k e", p=P)),
            (T.b2l[:, :], d["b2l"]),
            (T.wq[:, :, :], d["wq"].rearrange("(k p) e -> p k e", p=P)),
            (T.wk[:, :, :], d["wk"].rearrange("(k p) e -> p k e", p=P)),
            (T.wv[:, :, :], d["wv"].rearrange("(k p) e -> p k e", p=P)),
            (T.wo[:, :, :], d["wo"].rearrange("(k p) e -> p k e", p=P)),
            (T.pre_k[:, :, :], d["pre_k"]),
            (T.tab[:, :, :], d["tab"]),
        ]

        with nc.Block() as block:
            @block.sync
            def _(sp):
                for dst, src in loads:
                    sp.dma_start(dst, src).then_inc(s_load, 16)
                for dst, src in later_loads:
                    sp.dma_start(dst, src).then_inc(T.s_later, 16)
                sp.wait_ge(s_load, 16 * len(loads))

            @block.gpsimd
            def _(pool):
                pool.memset(T.ident[:, :], 0.0).then_inc(s_zero, 1)
                pool.memset(T.ones[:, :], 1.0).then_inc(s_zero, 1)
                pool.memset(T.mask_b[:, :], 0.0).then_inc(s_zero, 1)
                pool.memset(T.ident_b[:, :], 0.0).then_inc(s_zero, 1)
                pool.memset(T.half[:, :], -0.5).then_inc(s_zero, 1)
                pool.memset(T.minus1[:, :], -1.0).then_inc(s_zero, 1)
                for e in range(DEPTH):
                    pool.memset(T.iota16[:, e:e + 1], float(e)).then_inc(s_zero, 1)
                pool.wait_ge(s_zero, 6 + DEPTH)
                pool.affine_select(out=T.ident[:, :], in_=T.ident[:, :], compare_op=ALU.not_equal, fill=1.0, base=0,
                                   pattern=[[-1, P]], channel_multiplier=1).then_inc(s_const, 1)
                pool.affine_select(out=T.ident_b[:, :], in_=T.ident_b[:, :], compare_op=ALU.not_equal, fill=1.0, base=0,
                                   pattern=[[-1, P]], channel_multiplier=1).then_inc(s_const, 1)
                pool.affine_select(out=T.upto[:, :], in_=T.ones[:, :], compare_op=ALU.is_ge, fill=0.0, base=0,
                                   pattern=[[1, P]], channel_multiplier=-1).then_inc(s_const, 1)
                pool.affine_select(out=T.after[:, :], in_=T.ones[:, :], compare_op=ALU.is_gt, fill=0.0, base=0,
                                   pattern=[[-1, P]], channel_multiplier=1).then_inc(s_const, 1)
                pool.affine_select(out=T.mask_b[:, :], in_=T.mask_b[:, :], compare_op=ALU.is_ge, fill=NEG, base=PRE,
                                   pattern=[[-1, DIAG]], channel_multiplier=1).then_inc(s_const, 1)
                blocks = T.blocks[:, :].rearrange("p (a c) -> p a c", a=HPT)
                pool.affine_select(out=blocks, in_=T.ones[:, :].rearrange("p (a c) -> p a c", a=HPT),
                                   compare_op=ALU.is_ge, fill=0.0, base=0, pattern=[[-SLOT, HPT], [0, SLOT]],
                                   channel_multiplier=1).then_inc(s_const, 1)
                pool.wait_ge(s_const, 6)
                pool.affine_select(out=blocks, in_=blocks, compare_op=ALU.is_ge, fill=0.0, base=SLOT - 1,
                                   pattern=[[SLOT, HPT], [0, SLOT]], channel_multiplier=-1).then_inc(s_const, 1)
                pool.wait_ge(s_const, 7)

            @block.vector
            def _(dve):
                dve.wait_ge(s_load, 16 * len(loads))
                for e in range(ET):
                    dve.tensor_scalar(T.w_out[:, e, :], T.w_out[:, e, :], T.cols[:, C_NW + e:C_NW + e + 1], None,
                                      ALU.mult).then_inc(s_nw, 1)
                dve.wait_ge(s_nw, ET)

        with nc.Block() as block:
            @block.gpsimd
            def _(pool):
                for sem in (s_load, s_zero, s_const, s_nw):
                    pool.sem_clear(sem)


class Norm:

    def __init__(self, nc, ctx, T, tag):
        def sem(name):
            return ctx.enter_context(nc.semaphore(f"{tag}_{name}"))
        self.T = T
        self.stat = sem("stat")
        self.mean = sem("mean")
        self.var_eps = sem("var_eps")
        self.rstd = sem("rstd")
        self.normed = sem("normed")
        self.turned = sem("turned")
        self.ready = sem("ready")

    def vector(self, dve, b):
        T, lo, hi = self.T, b * TPB, (b + 1) * TPB
        for g in range(lo, hi):
            dve.bn_stats(T.ln_st[:, g, :], T.x[:, g, :]).then_inc(self.stat, 1)
        dve.wait_ge(self.stat, hi)
        for g in range(lo, hi):
            dve.bn_aggr(T.ln_mv[:, g, :], T.ln_st[:, g, :]).then_inc(self.mean, 1)
        dve.wait_ge(self.mean, hi)
        dve.tensor_scalar(T.ln_ve[:, lo:hi], T.ln_mv[:, lo:hi, 1], EPS, None, ALU.add).then_inc(self.var_eps, 1)
        dve.wait_ge(self.rstd, b + 1)
        for g in range(lo, hi):
            dve.tensor_scalar(T.xn[:, g, :], T.x[:, g, :], T.ln_mv[:, g, 0:1], T.ln_r[:, g:g + 1], ALU.subtract,
                              ALU.mult).then_inc(self.normed, 1)

    def gpsimd(self, pool, b):
        T, lo, hi = self.T, b * TPB, (b + 1) * TPB
        pool.wait_ge(self.var_eps, b + 1)
        pool.tensor_tensor(T.ln_r[:, lo:hi], T.ln_ve[:, lo:hi], T.half[:, lo:hi], ALU.pow).then_inc(self.rstd, 1)

    def tensor(self, pe, b):
        T = self.T
        for t in range(TPB):
            pe.wait_ge(self.normed, b * TPB + t + 1)
            for k in range(KD):
                last = pe.transpose(T.ps[:, k, t * P:(t + 1) * P], T.xn[:, b * TPB + t, k * P:(k + 1) * P],
                                    T.ident[:, :])
        last.then_inc(self.turned, 1)

    def scalar(self, act, b):
        T = self.T
        act.wait_ge(self.turned, b + 1)
        act.activation(T.xnT[:, b, :, :], T.ps[:, 0:KD, :], ACT.Copy).then_inc(self.ready, 1)


def mamba(nc, T):
    with ExitStack() as ctx:
        def sb(name, shape, dt=F32):
            return ctx.enter_context(nc.sbuf_tensor("m_" + name, shape, dt))

        def sem(name):
            return ctx.enter_context(nc.semaphore("m_" + name))

        ps = T.ps
        acc = sb("acc", [P, 2, SEQ])
        xcT = sb("xcT", [P, CT, SEQ])
        zs = sb("zs", [P, TPB, DI])
        NS = TPB * NH
        sm = sb("sm", [P, 12, NS])
        v, rl, na, u, s1, s2, s3, s4, dts, a, dw, _ = [sm[:, i, :] for i in range(12)]
        neg_a = sb("neg_a", [P, NH])
        ex = sb("ex", [P, 3, NS])
        rhs_a = sb("rhs_a", [P, 2, NH, P])
        decay = sb("decay", [P, 2, NH, P])
        gm = sb("gm", [P, 2, P])
        mix = sb("mix", [P, 2, NH, P])
        b_tok = sb("b_tok", [P, 2, P])
        xh = sb("xh", [P, 2, DI])
        xw = sb("xw", [P, 2, DI])
        xd = sb("xd", [P, 2, DI])
        state = sb("state", [P, 2, DI])
        st_dec = sb("st_dec", [P, DI])
        y = sb("y", [P, 3, DI])
        yg = sb("yg", [P, 2, DI])
        sq = sb("sq", [P, DI])
        ygT = sb("ygT", [P, 2, ET, P])
        ssq = sb("ssq", [P, NT])
        msq = sb("msq", [P, NT])
        rr = sb("rr", [P, NT])

        norm = Norm(nc, ctx, T, "m_ln")
        s_xbc = sem("xbc")
        s_pre = sem("pre")
        s_conv = sem("conv")
        s_silu = sem("silu")
        s_z = sem("z")
        s_zs = sem("zs")
        s_dt = sem("dt")
        s_na = sem("na")
        s_u = sem("u")
        s_nega = sem("nega")
        s_a = sem("a")
        s_cum = sem("cum")
        s_ex = sem("ex")
        s_dw = sem("dw")
        s_ra = sem("ra")
        s_g = sem("g")
        s_gm = sem("gm")
        s_seg = sem("seg")
        s_decay = sem("decay")
        s_mix = sem("mix")
        s_xhp = sem("xhp")
        s_xh = sem("xh")
        s_xw = sem("xw")
        s_xd = sem("xd")
        s_y = sem("y")
        s_stp = sem("stp")
        s_state = sem("state")
        s_yg = sem("yg")
        s_ssq = sem("ssq")
        s_msq = sem("msq")
        s_rr = sem("rr")
        s_ygTp = sem("ygTp")
        s_ygT = sem("ygT")
        s_o = sem("o")
        s_x = sem("x")
        s_dve = sem("dve")
        block = ctx.enter_context(nc.Block())
        XB, ZB, SEG, Y1, Y2, SMALL, STP = (4, 5), (7, 2), 2, 4, 5, 6, 7

        def heads(ap):
            return ap.rearrange("p (h q) -> p h q", h=NH)

        def per_head(ap, n=HD):
            return ap.unsqueeze(2).to_broadcast([P, NH, n])

        @block.sync
        def _(sp):
            sp.wait_ge(T.s_later, 16 * LATER)

        @block.tensor
        def _(pe):
            def prepare(b, c):
                n, q = b * TPB + c, (b * TPB + c) % 2
                cols = slice(c * P, (c + 1) * P)
                if n:
                    pe.wait_ge(s_xh, n)
                for e in range(ET):
                    last = pe.transpose(ps[:, 0, e * P:(e + 1) * P], xcT[:, e, cols], T.ident[:, :])
                last.then_inc(s_xhp, 1)
                if n:
                    pe.wait_ge(s_gm, 2 * n)
                pe.transpose(ps[:, 1, P:2 * P], xcT[:, ET, cols], T.ident[:, :])
                pe.matmul(ps[:, 1, 0:P], xcT[:, ET, cols], xcT[:, ET + 1, cols], start=True,
                          stop=True).then_inc(s_g, 1)
                pe.wait_ge(s_ra, n + 1)
                if n:
                    pe.wait_ge(s_decay, n)
                for i in range(2):
                    last = pe.matmul(ps[:, SEG + i, :], T.after[:, :], rhs_a[:, q, 4 * i:4 * i + 4, :], start=True,
                                     stop=True)
                last.then_inc(s_seg, 1)

            def outputs(b, c):
                n, q = b * TPB + c, (b * TPB + c) % 2
                pe.wait_ge(s_mix, n + 1)
                pe.wait_ge(s_xh, n + 1)
                if c:
                    pe.wait_ge(s_state, b * (TPB - 1) + c)
                    pe.matmul(ps[:, Y2, :], xcT[:, ET + 1, c * P:(c + 1) * P], state[:, (c - 1) % 2, :], start=True,
                              stop=True)
                for h in range(NH):
                    last = pe.matmul(ps[:, Y1, h * HD:(h + 1) * HD], mix[:, q, h, :], xh[:, q, h * HD:(h + 1) * HD],
                                     start=True, stop=True)
                last.then_inc(s_y, 1)
                if c < TPB - 1:
                    pe.wait_ge(s_xw, n + 1)
                    pe.matmul(ps[:, STP, :], b_tok[:, q, :], xw[:, q, :], start=True, stop=True).then_inc(s_stp, 1)

            def project_out(b, c):
                n, q = b * TPB + c, (b * TPB + c) % 2
                pe.wait_ge(s_yg, n + 1)
                for e in range(ET):
                    last = pe.transpose(ps[:, Y1, e * P:(e + 1) * P], yg[:, q, e * P:(e + 1) * P], T.ident[:, :])
                last.then_inc(s_ygTp, 1)
                pe.wait_ge(s_ygT, n + 1)
                for e in range(ET):
                    last = pe.matmul(ps[:, SMALL, DM:2 * DM], ygT[:, q, e, :], T.w_out[:, e, :], start=(e == 0),
                                     stop=(e == ET - 1))
                last.then_inc(s_o, 1)

            for b in range(BATCH):
                xT = T.xnT[:, b, :, :]
                if b:
                    pe.wait_ge(s_x, b * TPB)
                norm.tensor(pe, b)
                pe.wait_ge(norm.ready, b + 1)
                for t in range(TPB):
                    for k in range(KD):
                        last = pe.matmul(ps[:, SMALL, t * NH:(t + 1) * NH], xT[:, k, t * P:(t + 1) * P],
                                         T.w_in[:, k, DI + CD:IN_PROJ], start=(k == 0), stop=(k == KD - 1))
                last.then_inc(s_dt, 1)
                for ct in range(CT):
                    i = b * CT + ct
                    if i >= 2:
                        pe.wait_ge(s_conv, i - 1)
                    for k in range(KD):
                        last = pe.matmul(ps[:, XB[i % 2], :], T.w_in[:, k, DI + ct * P:DI + (ct + 1) * P], xT[:, k, :],
                                         start=(k == 0), stop=(k == KD - 1))
                    last.then_inc(s_xbc, 1)
                for t in range(TPB):
                    j = b * TPB + t
                    if j >= 2:
                        pe.wait_ge(s_zs, j - 1)
                    for k in range(KD):
                        last = pe.matmul(ps[:, ZB[j % 2], :], xT[:, k, t * P:(t + 1) * P], T.w_in[:, k, 0:DI],
                                         start=(k == 0), stop=(k == KD - 1))
                    last.then_inc(s_z, 1)
                pe.wait_ge(s_a, b + 1)
                for n, w in enumerate((T.upto, T.after, T.ones)):
                    last = pe.matmul(ps[:, SMALL, (n + 1) * NS:(n + 2) * NS], w[:, :], a, start=True, stop=True)
                last.then_inc(s_cum, 1)
                pe.wait_ge(s_zs, (b + 1) * TPB)
                pe.wait_ge(s_silu, (b + 1) * CT)
                prepare(b, 0)
                for c in range(TPB):
                    outputs(b, c)
                    if c + 1 < TPB:
                        prepare(b, c + 1)
                    project_out(b, c)

        @block.scalar
        def _(act):
            def prepare(b, c):
                n, q = b * TPB + c, (b * TPB + c) % 2
                act.wait_ge(s_xhp, n + 1)
                act.activation(xh[:, q, :], ps[:, 0, :], ACT.Copy).then_inc(s_xh, 1)
                act.wait_ge(s_seg, n + 1)
                act.activation(decay[:, q, :, :].rearrange("p h t -> p (h t)"),
                               ps[:, SEG:SEG + 2, :].rearrange("p i t -> p (i t)"), ACT.Exp).then_inc(s_decay, 1)

            for b in range(BATCH):
                norm.scalar(act, b)

                def silu(i):
                    act.wait_ge(s_conv, i + 1)
                    act.activation(xcT[:, i % CT, :], acc[:, i % 2, :], ACT.Silu).then_inc(s_silu, 1)

                act.wait_ge(s_na, b + 1)
                act.activation(u, na, ACT.Exp).then_inc(s_u, 1)
                if b == 0:
                    act.activation(neg_a[:, :], T.rows[:, R_AL:R_AL + NH], ACT.Exp).then_inc(s_nega, 1)
                for ct in range(CT):
                    i = b * CT + ct
                    act.wait_ge(s_xbc, i + 1)
                    if i >= 2:
                        act.wait_ge(s_silu, i - 1)
                    act.activation(acc[:, i % 2, :], ps[:, XB[i % 2], :], ACT.Identity,
                                   bias=T.cols[:, C_CB + ct:C_CB + ct + 1],
                                   scale=T.cols[:, C_CW + 4 * ct + 3:C_CW + 4 * ct + 4]).then_inc(s_pre, 1)
                    if ct:
                        silu(i - 1)
                silu(b * CT + CT - 1)
                for t in range(TPB):
                    j = b * TPB + t
                    act.wait_ge(s_z, j + 1)
                    act.activation(zs[:, t, :], ps[:, ZB[j % 2], :], ACT.Silu).then_inc(s_zs, 1)
                act.wait_ge(s_cum, b + 1)
                act.activation(ex[:, :, :], ps[:, SMALL, NS:4 * NS].rearrange("p (n s) -> p n s", n=3),
                               ACT.Exp).then_inc(s_ex, 1)
                prepare(b, 0)
                for c in range(TPB):
                    n, q = b * TPB + c, (b * TPB + c) % 2
                    if c + 1 < TPB:
                        prepare(b, c + 1)
                    act.wait_ge(s_yg, n + 1)
                    act.activation(sq[:, :], yg[:, q, :], ACT.Square, accum_out=ssq[:, n:n + 1]).then_inc(s_ssq, 1)
                    act.wait_ge(s_ygTp, n + 1)
                    act.activation(ygT[:, q, :, :].rearrange("p e t -> p (e t)"), ps[:, Y1, :],
                                   ACT.Copy).then_inc(s_ygT, 1)
                    act.wait_ge(s_ssq, n + 1)

        @block.gpsimd
        def _(pool):
            def spread(b, c):
                n, q = b * TPB + c, (b * TPB + c) % 2
                if n >= 2:
                    pool.wait_ge(s_seg, n - 1)
                pool.tensor_tensor(rhs_a[:, q, :, :], T.upto[:, :].unsqueeze(1).to_broadcast([P, NH, P]),
                                   per_head(a[:, c * NH:(c + 1) * NH], P), ALU.mult).then_inc(s_ra, 1)

            for b in range(BATCH):
                norm.gpsimd(pool, b)
            for b in range(BATCH):
                pool.wait_ge(s_ex, b + 1)
                pool.wait_ge(s_a, b + 1)
                pool.tensor_tensor(dw, ex[:, 1, :], dts, ALU.mult).then_inc(s_dw, 1)
                spread(b, 0)
                for c in range(TPB):
                    n, q = b * TPB + c, (b * TPB + c) % 2
                    pool.wait_ge(s_xh, n + 1)
                    if n >= 2:
                        pool.wait_ge(s_yg, n - 1)
                    pool.tensor_tensor(heads(xd[:, q, :]), heads(xh[:, q, :]), per_head(T.rows[:, R_D:R_D + NH]),
                                       ALU.mult).then_inc(s_xd, 1)
                    pool.wait_ge(s_dw, b + 1)
                    if c >= 2:
                        pool.wait_ge(s_stp, b * (TPB - 1) + c - 1)
                    elif b:
                        pool.wait_ge(s_stp, b * (TPB - 1))
                    pool.tensor_tensor(heads(xw[:, q, :]), heads(xh[:, q, :]), per_head(dw[:, c * NH:(c + 1) * NH]),
                                       ALU.mult).then_inc(s_xw, 1)
                    if c + 1 < TPB:
                        spread(b, c + 1)
                    pool.wait_ge(s_msq, n + 1)
                    pool.tensor_tensor(rr[:, n:n + 1], msq[:, n:n + 1], T.half[:, 0:1], ALU.pow).then_inc(s_rr, 1)

        @block.vector
        def _(dve):
            done = [0]

            def link(ins):
                done[0] += 1
                ins.then_inc(s_dve, 1)
                dve.wait_ge(s_dve, done[0])

            def take_products(b, c):
                n, q = b * TPB + c, (b * TPB + c) % 2
                dve.wait_ge(s_g, n + 1)
                dve.tensor_tensor(gm[:, q, :], ps[:, 1, 0:P], T.upto[:, :], ALU.mult).then_inc(s_gm, 1)
                dve.tensor_copy(b_tok[:, q, :], ps[:, 1, P:2 * P]).then_inc(s_gm, 1)

            def decay_products(b, c):
                n, q = b * TPB + c, (b * TPB + c) % 2
                dve.wait_ge(s_gm, 2 * n + 2)
                dve.wait_ge(s_decay, n + 1)
                if n >= 2:
                    dve.wait_ge(s_y, n - 1)
                for h in range(NH):
                    ins = dve.scalar_tensor_tensor(mix[:, q, h, :], decay[:, q, h, :],
                                                   dts[:, c * NH + h:c * NH + h + 1], gm[:, q, :], ALU.mult,
                                                   ALU.mult)
                ins.then_inc(s_mix, 1)

            for b in range(BATCH):
                if b == 0:
                    norm.vector(dve, 0)
                dve.wait_ge(s_dt, b + 1)
                if b:
                    dve.wait_ge(s_ra, b * TPB)
                    dve.wait_ge(s_dw, b)
                    dve.wait_ge(s_cum, b)
                for c in range(TPB):
                    ins = dve.tensor_tensor(v[:, c * NH:(c + 1) * NH], ps[:, SMALL, c * NH:(c + 1) * NH],
                                            T.rows[:, R_DTB:R_DTB + NH], ALU.add)
                link(ins)
                dve.scalar_tensor_tensor(na, v, -1.0, v, ALU.mult, ALU.min).then_inc(s_na, 1)
                link(dve.tensor_scalar(rl, v, 0.0, None, ALU.max))
                for ct in range(CT):
                    i = b * CT + ct
                    dve.wait_ge(s_pre, i + 1)
                    for lag in range(1, DCONV):
                        w = T.cols[:, C_CW + 4 * ct + 3 - lag:C_CW + 4 * ct + 4 - lag]
                        ins = dve.scalar_tensor_tensor(acc[:, i % 2, lag:SEQ], ps[:, XB[i % 2], 0:SEQ - lag], w,
                                                       acc[:, i % 2, lag:SEQ], ALU.mult, ALU.add)
                        if lag < DCONV - 1:
                            link(ins)
                        else:
                            ins.then_inc(s_conv, 1)
                if b + 1 < BATCH:
                    norm.vector(dve, b + 1)
                dve.wait_ge(s_u, b + 1)
                link(dve.tensor_scalar(s1, u, 2.0, None, ALU.add))
                link(dve.reciprocal(s2, s1))
                link(dve.tensor_tensor(s1, u, s2, ALU.mult))
                link(dve.tensor_tensor(s2, s1, s1, ALU.mult))
                link(dve.tensor_scalar(s3, s2, 2.0 / 17, 2.0 / 15, ALU.mult, ALU.add))
                for k in range(13, -1, -2):
                    link(dve.tensor_tensor(s4, s3, s2, ALU.mult))
                    if k > 0:
                        link(dve.tensor_scalar(s3, s4, 2.0 / k, None, ALU.add))
                link_last = dve.tensor_tensor(s4, s3, s1, ALU.mult)
                link(link_last)
                link(dve.tensor_tensor(dts, s4, rl, ALU.add))
                if b == 0:
                    dve.wait_ge(s_nega, 1)
                    link(dve.tensor_scalar(neg_a[:, :], neg_a[:, :], -1.0, None, ALU.mult))
                dve.tensor_tensor(a.rearrange("p (c h) -> p c h", h=NH), dts.rearrange("p (c h) -> p c h", h=NH),
                                  neg_a[:, :].unsqueeze(1).to_broadcast([P, TPB, NH]), ALU.mult).then_inc(s_a, 1)
                take_products(b, 0)
                decay_products(b, 0)
                for c in range(TPB):
                    n, q = b * TPB + c, (b * TPB + c) % 2
                    dve.wait_ge(s_y, n + 1)
                    dve.wait_ge(s_ex, b + 1)
                    dve.wait_ge(s_xd, n + 1)
                    link(dve.tensor_tensor(y[:, 0, :], ps[:, Y1, :], xd[:, q, :], ALU.add))
                    if c:
                        link(dve.tensor_tensor(heads(y[:, 1, :]), heads(ps[:, Y2, :]),
                                               per_head(ex[:, 0, c * NH:(c + 1) * NH]), ALU.mult))
                        link(dve.tensor_tensor(y[:, 2, :], y[:, 0, :], y[:, 1, :], ALU.add))
                    dve.wait_ge(s_zs, (b + 1) * TPB)
                    if n >= 2:
                        dve.wait_ge(s_ygTp, n - 1)
                    dve.tensor_tensor(yg[:, q, :], y[:, 2 if c else 0, :], zs[:, c, :], ALU.mult).then_inc(s_yg, 1)
                    if c < TPB - 1:
                        take_products(b, c + 1)
                        if c:
                            link(dve.tensor_tensor(heads(st_dec[:, :]), heads(state[:, (c - 1) % 2, :]),
                                                   per_head(ex[:, 2, c * NH:(c + 1) * NH]), ALU.mult))
                        dve.wait_ge(s_stp, b * (TPB - 1) + c + 1)
                        if c:
                            dve.tensor_tensor(state[:, c % 2, :], st_dec[:, :], ps[:, STP, :],
                                              ALU.add).then_inc(s_state, 1)
                        else:
                            dve.tensor_copy(state[:, c % 2, :], ps[:, STP, :]).then_inc(s_state, 1)
                        decay_products(b, c + 1)
                    dve.wait_ge(s_ssq, n + 1)
                    dve.tensor_scalar(msq[:, n:n + 1], ssq[:, n:n + 1], 1.0 / DI, EPS, ALU.mult,
                                      ALU.add).then_inc(s_msq, 1)
                    dve.wait_ge(s_rr, n + 1)
                    dve.wait_ge(s_o, n + 1)
                    dve.scalar_tensor_tensor(T.x[:, n, :], ps[:, SMALL, DM:2 * DM], rr[:, n:n + 1], T.x[:, n, :],
                                             ALU.mult, ALU.add).then_inc(s_x, 1)
            dve.wait_ge(s_x, NT)


def ffn(nc, T, tag, out=None):
    with ExitStack() as ctx:
        def sb(name, shape, dt=F32):
            return ctx.enter_context(nc.sbuf_tensor(f"{tag}_{name}", shape, dt))

        def sem(name):
            return ctx.enter_context(nc.semaphore(f"{tag}_{name}"))

        ps = T.ps
        lg = sb("lg", [P, NT, NE])
        top = sb("top", [P, NT, NE])
        idx = sb("idx", [P, NT, NE], U32)
        idf = sb("idf", [P, NT, NE])
        neg = sb("neg", [P, NT])
        pr = sb("pr", [P, NT, NE])
        pk = sb("pk", [P, NT, 2])
        psum_ = sb("psum", [P, NT])
        rs = sb("rs", [P, NT])
        w = sb("w", [P, NT, 2])
        wsum = sb("wsum", [P, NT])
        oh = sb("oh", [P, NT, 2, NE])
        ohw = sb("ohw", [P, NT, 2, NE])
        ohd = sb("ohd", [P, NT, 2, NE])
        tm = sb("tm", [P, TPB, 2, P])
        tmT = sb("tmT", [P, 2, SEQ])
        aT = sb("aT", [P, 2, FT, SEQ])
        mixT = sb("mixT", [P, FT, SEQ])
        part = sb("part", [P, 2, 2, SEQ])
        wide_w = sb("wide_w", [P, TPB, 2, P])
        wide_e = sb("wide_e", [P, TPB, 2, P])
        wT = sb("wT", [P, 2, SEQ])
        eT = sb("eT", [P, 2, SEQ])
        t2T = sb("t2T", [P, SEQ])
        xa = sb("xa", [P, TPB, DM])
        norm = Norm(nc, ctx, T, tag + "_ln")
        s_rt = sem("rt")
        s_neg = sem("neg")
        s_pr = sem("pr")
        s_tm = sem("tm")
        s_tmTp = sem("tmTp")
        s_tmT = sem("tmT")
        s_h0 = sem("h0")
        s_g0 = sem("g0")
        s_h1 = sem("h1")
        s_g1 = sem("g1")
        s_dn = sem("dn")
        s_wide = sem("wide")
        s_wTp = sem("wTp")
        s_wT = sem("wT")
        s_rank = sem("rank")
        s_mix = sem("mix")
        s_t2T = sem("t2T")
        s_x = sem("x")
        s_out = sem("out")
        s_dve = sem("dve")
        block = ctx.enter_context(nc.Block())
        RT, HB, DN, TP, RK_ACC = (0, 1, 2, 3), (6, 7, 2, 3), (6, 7), 4, (0, 1)

        def by_rank(ap):
            return ap.rearrange("p (e r) -> p e r", e=NE)

        def per_rank(ap):
            return ap.unsqueeze(2).to_broadcast([P, NE, RK])

        @block.tensor
        def _(pe):
            def route(b):
                xT = T.xnT[:, b, :, :]
                pe.wait_ge(norm.ready, b + 1)
                for t in range(TPB):
                    for k in range(KD):
                        last = pe.matmul(ps[:, RT[t], 0:NE + P], xT[:, k, t * P:(t + 1) * P], T.w_ra[:, k, :],
                                         start=(k == 0), stop=(k == KD - 1))
                    last.then_inc(s_rt, 1)

            def turn_ranks(b):
                for t in range(TPB):
                    g = b * TPB + t
                    pe.wait_ge(s_tm, g + 1)
                    for s in range(2):
                        last = pe.transpose(ps[:, TP + s, t * P:(t + 1) * P], tm[:, t, s, :], T.ident[:, :])
                    last.then_inc(s_tmTp, 1)
                pe.wait_ge(s_tmT, b + 1)


            def hidden(b):
                xT = T.xnT[:, b, :, :]

                def second(f):
                    i = b * FT + f
                    pe.wait_ge(s_g0, i + 1)
                    pe.matmul(ps[:, HB[f % 4], :], T.b1l[:, f * P:(f + 1) * P], tmT[:, 1, :], start=False, stop=True,
                              skip_group_check=True).then_inc(s_h1, 1)

                def ranks(f, s):
                    pe.wait_ge((s_g0, s_g1)[s], b * FT + f + 1)
                    last = pe.matmul(ps[:, RK_ACC[s], :], T.w2a[:, f, DM:DM + P], aT[:, s, f, :], start=(f == 0),
                                     stop=(f == FT - 1), skip_group_check=True)
                    if f == FT - 1:
                        last.then_inc(s_rank, 1)

                for f in range(FT):
                    i = b * FT + f
                    if f >= 4:
                        pe.wait_ge(s_g1, i - 3)
                    o = ps[:, HB[f % 4], :]
                    for k in range(KD):
                        pe.matmul(o, T.w1[:, k, f * P:(f + 1) * P], xT[:, k, :], start=(k == 0), stop=False,
                                  skip_group_check=True)
                    pe.matmul(o, T.b1l[:, f * P:(f + 1) * P], tmT[:, 0, :], start=False, stop=True,
                              skip_group_check=True).then_inc(s_h0, 1)
                    if f:
                        second(f - 1)
                        ranks(f - 1, 0)
                    if f >= 2:
                        ranks(f - 2, 1)
                    if f in (2, 4):
                        n, wide = 2 * b + (f == 4), (wide_w, wide_e)[f == 4]
                        pe.wait_ge(s_wide, n + 1)
                        if n:
                            pe.wait_ge(s_wT, n)
                        for t in range(TPB):
                            for s in range(2):
                                last = pe.transpose(ps[:, TP + s, t * P:(t + 1) * P], wide[:, t, s, :], T.ident[:, :])
                        last.then_inc(s_wTp, 1)
                second(FT - 1)
                ranks(FT - 1, 0)
                ranks(FT - 2, 1)
                ranks(FT - 1, 1)

            def down(b, t):
                g = b * TPB + t
                if t >= 2:
                    pe.wait_ge(s_x, g - 1)
                out, cols = ps[:, DN[t % 2], 0:DM], slice(t * P, (t + 1) * P)
                for f in range(FT):
                    pe.matmul(out, mixT[:, f, cols], T.w2a[:, f, 0:DM], start=(f == 0), stop=False)
                pe.matmul(out, t2T[:, cols], T.b2l[:, :], start=False, stop=True).then_inc(s_dn, 1)

            norm.tensor(pe, 0)
            route(0)
            turn_ranks(0)
            for b in range(BATCH):
                hidden(b)
                pe.wait_ge(s_g1, (b + 1) * FT)
                pe.wait_ge(s_t2T, b + 1)
                if b + 1 < BATCH:
                    norm.tensor(pe, b + 1)
                pe.wait_ge(s_mix, (b + 1) * FT)
                for t in range(TPB):
                    down(b, t)
                    if t == 0 and b + 1 < BATCH:
                        route(b + 1)
                if b + 1 < BATCH:
                    pe.wait_ge(s_x, (b + 1) * TPB)
                    pe.wait_ge(s_wT, 2 * (b + 1))
                    turn_ranks(b + 1)

        @block.scalar
        def _(act):
            def route(b):
                for g in range(b * TPB, (b + 1) * TPB):
                    act.wait_ge(s_neg, b + 1)
                    act.activation(pr[:, g, :], lg[:, g, :], ACT.Exp, bias=neg[:, g:g + 1],
                                   accum_out=psum_[:, g:g + 1]).then_inc(s_pr, 1)
                    act.activation(pk[:, g, :], top[:, g, 0:2], ACT.Exp, bias=neg[:, g:g + 1]).then_inc(s_pr, 1)

            norm.scalar(act, 0)
            route(0)
            for b in range(BATCH):
                act.wait_ge(s_tmTp, (b + 1) * TPB)
                act.activation(tmT[:, :, :], ps[:, TP:TP + 2, :], ACT.Copy).then_inc(s_tmT, 1)
                if b:
                    act.wait_ge(s_dn, b * TPB)

                def gelu(f, s, ready, done):
                    i = b * FT + f
                    act.wait_ge(ready, i + 1)
                    act.activation(aT[:, s, f, :], ps[:, HB[f % 4], :], ACT.Gelu_apprx_tanh,
                                   bias=T.cols[:, C_B1 + f:C_B1 + f + 1]).then_inc(done, 1)

                for f in range(FT):
                    gelu(f, 0, s_h0, s_g0)
                    if f:
                        gelu(f - 1, 1, s_h1, s_g1)
                    if f in (3, 5):
                        n, turned = 2 * b + (f == 5), (wT, eT)[f == 5]
                        act.wait_ge(s_wTp, n + 1)
                        act.activation(turned[:, :, :], ps[:, TP:TP + 2, :], ACT.Copy).then_inc(s_wT, 1)
                gelu(FT - 1, 1, s_h1, s_g1)
                if b + 1 < BATCH:
                    norm.scalar(act, b + 1)
                if b + 1 < BATCH:
                    route(b + 1)

        @block.gpsimd
        def _(pool):
            for b in range(BATCH):
                norm.gpsimd(pool, b)

        @block.vector
        def _(dve):
            done = [0]

            def link(ins):
                done[0] += 1
                ins.then_inc(s_dve, 1)
                dve.wait_ge(s_dve, done[0])

            def route(b):
                own = slice(b * TPB, (b + 1) * TPB)
                dve.wait_ge(s_rt, (b + 1) * TPB)
                link(dve.tensor_tensor(lg[:, own, :], ps[:, RT[0]:RT[0] + TPB, 0:NE],
                                       T.rows[:, R_BR:R_BR + NE].unsqueeze(1).to_broadcast([P, TPB, NE]), ALU.add))
                for g in range(b * TPB, (b + 1) * TPB):
                    ins = dve.max(top[:, g, :], lg[:, g, :])
                link(ins)
                dve.tensor_scalar(neg[:, own], top[:, own, 0], -1.0, None, ALU.mult).then_inc(s_neg, 1)
                for g in range(b * TPB, (b + 1) * TPB):
                    ins = dve.max_index(idx[:, g, :], top[:, g, :], lg[:, g, :])
                link(ins)
                link(dve.tensor_copy(idf[:, own, :], idx[:, own, :]))
                for s in range(2):
                    ins = dve.tensor_tensor(oh[:, own, s, :], T.iota8.unsqueeze(1).to_broadcast([P, TPB, NE]),
                                            idf[:, own, s:s + 1].to_broadcast([P, TPB, NE]), ALU.is_equal)
                link(ins)
                dve.tensor_scalar(ohd[:, own, 0, :], oh[:, own, 0, :], LORA, None, ALU.mult)
                link(dve.tensor_tensor(ohd[:, own, 1, :], oh[:, own, 1, :], oh[:, own, 0, :], ALU.subtract))
                link(dve.tensor_scalar(ohd[:, own, 1, :], ohd[:, own, 1, :], LORA, None, ALU.mult))
                if b:
                    dve.wait_ge(s_tmTp, b * TPB)
                for t in range(TPB):
                    for s in range(2):
                        ins = dve.tensor_tensor(by_rank(tm[:, t, s, :]), by_rank(ps[:, RT[t], NE:NE + P]),
                                                per_rank(ohd[:, b * TPB + t, s, :]), ALU.mult)
                    ins.then_inc(s_tm, 1)

            norm.vector(dve, 0)
            route(0)
            for b in range(BATCH):
                for t in range(TPB):
                    g = b * TPB + t
                    dve.wait_ge(s_pr, 2 * g + 2)
                    link(dve.reciprocal(rs[:, g:g + 1], psum_[:, g:g + 1]))
                    link(dve.tensor_scalar(w[:, g, :], pk[:, g, :], rs[:, g:g + 1], None, ALU.mult))
                    link(dve.tensor_tensor(wsum[:, g:g + 1], w[:, g, 0:1], w[:, g, 1:2], ALU.add))
                    for s in range(2):
                        ins = dve.tensor_scalar(ohw[:, g, s, :], oh[:, g, s, :], w[:, g, s:s + 1], LORA, ALU.mult,
                                                ALU.mult)
                    link(ins)
                for n, (wide, narrow) in enumerate(((wide_w, w), (wide_e, ohw))):
                    for t in range(TPB):
                        for s in range(2):
                            g = b * TPB + t
                            if n == 0:
                                ins = dve.tensor_copy(wide[:, t, s, :], narrow[:, g, s:s + 1].to_broadcast([P, P]))
                            else:
                                ins = dve.tensor_copy(by_rank(wide[:, t, s, :]), per_rank(narrow[:, g, s, :]))
                    ins.then_inc(s_wide, 1)
                if b + 1 < BATCH:
                    norm.vector(dve, b + 1)
                for t in range(TPB):
                    g = b * TPB + t
                    dve.scalar_tensor_tensor(xa[:, t, :], T.rows[:, R_B2:R_B2 + DM], wsum[:, g:g + 1], T.x[:, g, :],
                                             ALU.mult, ALU.add)
                dve.wait_ge(s_wT, 2 * b + 1)
                for f in range(FT):
                    i = b * FT + f
                    dve.wait_ge(s_g0, i + 1)
                    dve.wait_ge(s_g1, i + 1)
                    if i >= 2:
                        dve.wait_ge(s_mix, i - 1)
                    for s in range(2):
                        ins = dve.tensor_tensor(part[:, i % 2, s, :], aT[:, s, f, :], wT[:, s, :], ALU.mult)
                    link(ins)
                    dve.tensor_tensor(mixT[:, f, :], part[:, i % 2, 0, :], part[:, i % 2, 1, :],
                                      ALU.add).then_inc(s_mix, 1)
                dve.wait_ge(s_rank, 2 * (b + 1))
                dve.wait_ge(s_wT, 2 * b + 2)
                dve.wait_ge(s_mix, (b + 1) * FT)
                for s in range(2):
                    ins = dve.tensor_tensor(part[:, 0, s, :], ps[:, RK_ACC[s], :], eT[:, s, :], ALU.mult)
                link(ins)
                dve.tensor_tensor(t2T[:, :], part[:, 0, 0, :], part[:, 0, 1, :], ALU.add).then_inc(s_t2T, 1)
                dve.wait_ge(s_t2T, b + 1)
                for t in range(TPB):
                    if t == 1 and b + 1 < BATCH:
                        route(b + 1)
                    g = b * TPB + t
                    dve.wait_ge(s_dn, g + 1)
                    dve.tensor_tensor(T.x[:, g, :], ps[:, DN[t % 2], 0:DM], xa[:, t, :], ALU.add).then_inc(s_x, 1)
            dve.wait_ge(s_x, NT)

        @block.sync
        def _(sp):
            if out is not None:
                for g in range(NT):
                    b, t = divmod(g, TPB)
                    sp.wait_ge(s_x, g + 1)
                    sp.dma_start(out[b, t * P:(t + 1) * P, :], T.x[:, g, :]).then_inc(s_out, 16)
                sp.wait_ge(s_out, 16 * NT)


def attention(nc, T):
    with ExitStack() as ctx:
        def sb(name, shape, dt=F32):
            return ctx.enter_context(nc.sbuf_tensor("a_" + name, shape, dt))

        def sem(name):
            return ctx.enter_context(nc.semaphore("a_" + name))

        ps = T.ps
        WMAX = SEQ + PRE
        ROUNDS = TOPK // 8
        VW = SLOT
        TAIL = GH * PRE
        qT = sb("qT", [P, QT, SEQ])
        kT = sb("kT", [P, KT, WMAX])
        v = sb("v", [P, TPB, AH, VW])
        v_tail = sb("v_tail", [TAIL, TPB, AH, VW])
        bqs = sb("bqs", [P, QT])
        gram = sb("gram", [P, KT, P])
        k_sum = sb("k_sum", [P, KT, HPT])
        mom1 = sb("mom1", [P, TPB, AH])
        mom2 = sb("mom2", [P, TPB, AH])
        sd = sb("sd", [P, TPB, AH])
        tmp = sb("tmp", [P, TPB, AH])
        shift = sb("shift", [P, TPB, AH])
        thr0 = sb("thr0", [P, TPB, AH])
        gain = sb("gain", [P, TPB, AH])
        y = sb("y", [P, YR, GH, WMAX])
        k_tok = y[:, 0, :, 0:DM]
        q_tok = y[:, 1, 0:2, 0:SEQ]
        prod = y[:, 1, 2, 0:SEQ]
        E = sb("E", [P, ER, GH, WMAX])
        ymax = sb("ymax", [P, YR, GH])
        nmax = sb("nmax", [P, NR, GH])
        junk = sb("junk", [P, 3, GH, WMAX], BF16)
        c0 = sb("c0", [P, 2, GH])
        c1 = sb("c1", [P, 2, GH])
        c2 = sb("c2", [P, 2, GH])
        w = sb("w", [P, 8, GH])
        off0 = sb("off0", [P, 2, GH])
        move = sb("move", [P, 2, GH])
        thr1 = sb("thr1", [P, 2, GH])
        thr2 = sb("thr2", [P, 2, GH])
        below = sb("below", [P, GH, WMAX])
        m16 = sb("m16", [P, 2, GH, DEPTH])
        rank = sb("rank", [P, TPB, DEPTH - 1])
        place = sb("place", [P, GH, DEPTH - 1])
        picked = sb("picked", [P, 2, GH, DEPTH - 1])
        thr = sb("thr", [P, 2, 2, GH])
        bad = sb("bad", [P, 2, GH + 1])
        flags = sb("flags", [P, 2, GH + 1])
        left = sb("left", [P, WMAX])
        m8 = sb("m8", [P, ROUNDS, 8])
        prT = sb("prT", [P, 2, SEQ])
        tail = sb("tail", [P, 2, TAIL])
        tailT = sb("tailT", [TAIL, P])
        ohT = sb("ohT", [P, P])
        rinv = sb("rinv", [P, 2, GH])
        o = sb("o", [P, TPB, DM])
        oT = qT[:, :, 0:DM].rearrange("p t (k c) -> p t k c", k=KD)
        xa = qT[:, :, DM:2 * DM]
        norm = Norm(nc, ctx, T, "a_ln")
        s_bqs = sem("bqs")
        s_qk = sem("qk")
        s_qkT = sem("qkT")
        s_v = sem("v")
        s_vs = sem("vs")
        s_one = sem("one")
        s_kt = sem("kt")
        s_ktok = sem("ktok")
        s_gram = sem("gram")
        s_gm = sem("gm")
        s_qt = sem("qt")
        s_qtok = sem("qtok")
        s_qg = sem("qg")
        s_mom = sem("mom")
        s_var = sem("var")
        s_sd = sem("sd")
        s_thr0 = sem("thr0")
        s_sc = sem("sc")
        s_y = sem("y")
        s_nmax = sem("nmax")
        s_c0 = sem("c0")
        s_c1 = sem("c1")
        s_c2 = sem("c2")
        s_thr1 = sem("thr1")
        s_thr2 = sem("thr2")
        s_m16 = sem("m16")
        s_rank = sem("rank")
        s_flag = sem("flag")
        s_E = sem("E")
        s_sel = sem("sel")
        s_tp = sem("tp")
        s_pT = sem("pT")
        s_tail = sem("tail")
        s_tt = sem("tt")
        s_tailT = sem("tailT")
        s_ohT = sem("ohT")
        s_back = sem("back")
        s_vt = sem("vt")
        s_pv = sem("pv")
        s_on = sem("on")
        s_oTp = sem("oTp")
        s_oT = sem("oT")
        s_f = sem("f")
        s_x = sem("x")
        s_dve = sem("dve")
        s_pool = sem("pool")
        s_gen = sem("gen")
        s_ht = sem("ht")
        s_low = sem("low")
        block = ctx.enter_context(nc.Block())
        QB, VB = (2, 3, 4, 5), (6, 7)
        KTB, GB, QTB, QGB = (2, 3), (4, 5), (2, 3), ((6, 7), (0, 1))
        SC, TB, HT, OB = (2, 4), (6, 7), 1, 0
        FB, FO = (2, 3, 4, 5), (6, 7)
        GPT = AH // GH
        GPB = TPB * GPT
        LAG = 4

        def place_of(g):
            half, j = divmod(g % GPB, GPB // 2)
            return g // GPB, ((1, 2), (3, 0))[half][j % 2], j // 2 * GH

        def tile_of(h):
            odd, half, slot = h % 2, h // 2 // HPT, h // 2 % HPT
            return odd * KT + half, half, SLOT * slot

        def by_head(ap):
            return ap.rearrange("p (half slot odd) -> p odd half slot", half=KT, odd=2)

        def width(g):
            return (place_of(g)[1] + 1) * P + PRE

        def banks(g, u):
            if width(g) <= SEQ:
                return ps[:, SC[0] + u, :]
            return ps[:, SC[u % 2]:SC[u % 2] + 2, :].rearrange("p a c -> p (a c)")

        def steps(b):
            return range(b * GPB - 1, (b + 1) * GPB + LAG)

        def mine(b, g):
            return b * GPB <= g < (b + 1) * GPB

        @block.tensor
        def _(pe):
            def project(b):
                xT = T.xnT[:, b, :, :]
                norm.tensor(pe, b)
                pe.wait_ge(norm.ready, b + 1)
                for i in range(KT + QT):
                    wt, m = (T.wk, i) if i < KT else (T.wq, i - KT)
                    if i >= 4:
                        pe.wait_ge(s_qkT, b * (KT + QT) + i - 3)
                    for k in range(KD):
                        last = pe.matmul(ps[:, QB[i % 4], :], wt[:, k, m * P:(m + 1) * P], xT[:, k, :], start=(k == 0),
                                         stop=(k == KD - 1))
                    last.then_inc(s_qk, 1)
                for t in range(TPB):
                    if t >= 2:
                        pe.wait_ge(s_vs, b * TPB + t - 1)
                    for k in range(KD):
                        last = pe.matmul(ps[:, VB[t % 2], 0:DM], xT[:, k, t * P:(t + 1) * P], T.wv[:, k, :],
                                         start=(k == 0), stop=(k == KD - 1))
                    last.then_inc(s_v, 1)
                pe.wait_ge(s_qkT, (b + 1) * (KT + QT))

            def moments(b):
                for j in range(TPB):
                    n = b * TPB + j
                    if j >= 2:
                        pe.wait_ge(s_ktok, n - 1)
                    for m in range(KT):
                        last = pe.transpose(ps[:, KTB[j % 2], m * P:(m + 1) * P], kT[:, m, j * P:(j + 1) * P],
                                            T.ident[:, :])
                    last.then_inc(s_kt, 1)
                pe.wait_ge(s_ktok, (b + 1) * TPB)
                for m in range(KT):
                    for j in range(TPB):
                        kt = k_tok[:, j, m * P:(m + 1) * P]
                        pe.matmul(ps[:, GB[0], m * P:(m + 1) * P], kt, kt, start=(j == 0), stop=(j == TPB - 1))
                    for j in range(TPB):
                        last = pe.matmul(ps[:, GB[1], m:m + 1], k_tok[:, j, m * P:(m + 1) * P], T.ones[:, 0:1],
                                         start=(j == 0), stop=(j == TPB - 1))
                last.then_inc(s_gram, 1)
                pe.wait_ge(s_vs, (b + 1) * TPB)
                for t in range(TPB):
                    n = b * TPB + t
                    if t >= 2:
                        pe.wait_ge(s_qtok, n - 1)
                    for m in range(QT):
                        last = pe.transpose(ps[:, QTB[t % 2], m * P:(m + 1) * P], qT[:, m, t * P:(t + 1) * P],
                                            T.ident[:, :])
                    last.then_inc(s_qt, 1)
                    pe.wait_ge(s_gm, b + 1)
                    if t >= 2:
                        pe.wait_ge(s_mom, n - 1)
                    for m in range(QT):
                        q = qT[:, m, t * P:(t + 1) * P]
                        pe.matmul(ps[:, QGB[t % 2][0], m * P:(m + 1) * P], q, gram[:, m % KT, :], start=True, stop=True)
                        last = pe.matmul(ps[:, QGB[t % 2][1], m * HPT:(m + 1) * HPT], q, k_sum[:, m % KT, :],
                                         start=True, stop=True)
                    last.then_inc(s_qg, 1)
                pe.wait_ge(s_mom, (b + 1) * TPB)
                pe.wait_ge(s_one, 4)
                pe.wait_ge(s_vt, 16 * (b + 1) * (GH + 1))

            def scores(g, u):
                b, t, h0 = place_of(g)
                h = h0 + u
                if width(g) > SEQ and u >= 2:
                    pe.wait_ge(s_y, g * GH + u - 1)
                elif g:
                    pe.wait_ge(s_y, g * GH)
                mq, m, r = tile_of(h)
                q = qT[r:r + SLOT, mq, t * P:(t + 1) * P]
                out = banks(g, u)
                lo, top = t * P, min(width(g), SEQ)
                pe.matmul(out[:, 0:top], q, kT[r:r + SLOT, m, 0:top], start=True, stop=False, skip_group_check=True)
                last = pe.matmul(out[:, lo:top], T.ident_b[:, :], T.mask_b[:, 0:top - lo], start=False, stop=True,
                                 skip_group_check=True)
                if width(g) > SEQ:
                    pe.matmul(out[:, SEQ:WMAX], q, kT[r:r + SLOT, m, SEQ:WMAX], start=True, stop=False,
                              skip_group_check=True)
                    last = pe.matmul(out[:, SEQ:WMAX], T.ident_b[:, :], T.mask_b[:, P:DIAG], start=False, stop=True,
                                     skip_group_check=True)
                last.then_inc(s_sc, 1)

            def turn_tails(g):
                pe.wait_ge(s_tail, g + 1)
                if g:
                    pe.wait_ge(s_ohT, g)
                pe.transpose(ps[0:TAIL, HT, P:2 * P], tail[:, g % 2, :], T.ident[:, :]).then_inc(s_tt, 1)

            def turn(g, u):
                t, i = place_of(g)[1], g * GH + u
                if i >= 2:
                    pe.wait_ge(s_pT, i - 1)
                for j in range(t + 1):
                    last = pe.transpose(ps[:, TB[i % 2], j * P:(j + 1) * P], E[:, g % ER, u, j * P:(j + 1) * P],
                                        T.ident[:, :])
                last.then_inc(s_tp, 1)

            def values(g, u):
                b, t, h0 = place_of(g)
                i = g * GH + u
                pe.wait_ge(s_pT, i + 1)
                for j in range(t + 1):
                    last = pe.matmul(ps[u * SLOT:(u + 1) * SLOT, HT, 0:P], v[:, j, h0 + u, :],
                                     prT[:, i % 2, j * P:(j + 1) * P], start=(j == 0), stop=False,
                                     skip_group_check=True)
                last.then_inc(s_pv, 1)
                if u == GH - 1:
                    pe.matmul(ps[:, HT, 0:P], v_tail[:, t, h0:h0 + GH, :].rearrange("p h c -> p (h c)"), tailT[:, :],
                              start=False, stop=True, skip_group_check=True).then_inc(s_ht, 1)

            def turn_back(g):
                pe.wait_ge(s_ohT, g + 1)
                if g:
                    pe.wait_ge(s_on, g)
                pe.transpose(ps[:, OB, 0:P], ohT[:, :], T.ident[:, :]).then_inc(s_back, 1)

            def turn_tokens(n):
                t = n % TPB
                pe.wait_ge(s_on, (n // TPB + 1) * GPB)
                for k in range(KD):
                    last = pe.transpose(ps[:, FB[t], k * P:(k + 1) * P], o[:, t, k * P:(k + 1) * P], T.ident[:, :])
                last.then_inc(s_oTp, 1)

            def finish(n):
                t = n % TPB
                pe.wait_ge(s_oT, n + 1)
                if t >= 2:
                    pe.wait_ge(s_x, n - 1)
                for k in range(KD):
                    last = pe.matmul(ps[:, FO[t % 2], 0:DM], oT[:, t, k, :], T.wo[:, k, :], start=(k == 0),
                                     stop=(k == KD - 1))
                last.then_inc(s_f, 1)

            for b in range(BATCH):
                project(b)
                moments(b)
                for k in steps(b):
                    first = (GH if width(k + 1) <= SEQ else 2) if mine(b, k + 1) else 0
                    for u in range(first):
                        scores(k + 1, u)
                    if mine(b, k - LAG):
                        g = k - LAG
                        turn_tails(g)
                        turn(g, 0)
                        for u in range(GH):
                            if u + 1 < GH:
                                turn(g, u + 1)
                            values(g, u)
                    if mine(b, k + 1):
                        for u in range(first, GH):
                            scores(k + 1, u)
                    if mine(b, k - LAG):
                        turn_back(k - LAG)
                for n in range(b * TPB, (b + 1) * TPB):
                    turn_tokens(n)
                for n in range(b * TPB, (b + 1) * TPB):
                    finish(n)
                pe.wait_ge(s_x, (b + 1) * TPB)

        @block.scalar
        def _(act):
            act.activation(bqs[:, :], T.cols[:, C_BQ:C_BQ + QT], ACT.Copy, scale=AD ** -0.5).then_inc(s_bqs, 1)
            act.wait_ge(s_bqs, 1)

            def project(b):
                norm.scalar(act, b)
                for i in range(KT + QT):
                    m = i if i < KT else i - KT
                    act.wait_ge(s_qk, b * (KT + QT) + i + 1)
                    if i >= KT:
                        ins = act.activation(qT[:, m, :], ps[:, QB[i % 4], :], ACT.Identity, bias=bqs[:, m:m + 1],
                                             scale=AD ** -0.5)
                    else:
                        ins = act.activation(kT[:, m, 0:SEQ], ps[:, QB[i % 4], :], ACT.Identity,
                                             bias=T.cols[:, C_BK + m:C_BK + m + 1])
                    ins.then_inc(s_qkT, 1)

            def moments(b):
                if b:
                    act.wait_ge(s_sel, b * GPB * GH)
                for j in range(TPB):
                    act.wait_ge(s_kt, b * TPB + j + 1)
                    act.activation(k_tok[:, j, :], ps[:, KTB[j % 2], 0:DM], ACT.Copy).then_inc(s_ktok, 1)
                for t in range(TPB):
                    act.wait_ge(s_qt, b * TPB + t + 1)
                    if t >= 2:
                        act.wait_ge(s_mom, b * TPB + t - 1)
                    act.activation(q_tok[:, t % 2, :], ps[:, QTB[t % 2], :], ACT.Copy).then_inc(s_qtok, 1)
                act.wait_ge(s_var, b + 1)
                act.activation(tmp[:, :, :], sd[:, :, :], ACT.Sqrt).then_inc(s_sd, 1)

            def count(g, n, bias, out, done, used):
                if g >= 2:
                    act.wait_ge(used, g - 1)
                if g:
                    act.wait_ge(done, g * GH)
                for u in range(GH):
                    if done is s_c0:
                        act.wait_ge(s_y, g * GH + u + 1)
                    act.activation(junk[:, n, u, 0:width(g)], y[:, g % YR, u, 0:width(g)], ACT.Sign,
                                   bias=bias[:, u:u + 1], scale=-1.0,
                                   accum_out=out[:, g % 2, u:u + 1]).then_inc(done, 1)

            def exponents(g):
                act.wait_ge(s_nmax, g + 1)
                if g >= ER:
                    act.wait_ge(s_tp, (g - ER + 1) * GH)
                for u in range(GH):
                    act.activation(E[:, g % ER, u, 0:width(g)], y[:, g % YR, u, 0:width(g)], ACT.Exp,
                                   bias=nmax[:, g % NR, u:u + 1]).then_inc(s_E, 1)

            def turn(g):
                t = place_of(g)[1]
                act.wait_ge(s_tt, g + 1)
                act.activation(tailT[:, :], ps[0:TAIL, HT, P:2 * P], ACT.Copy).then_inc(s_tailT, 1)
                for u in range(GH):
                    i = g * GH + u
                    act.wait_ge(s_tp, i + 1)
                    if i >= 2:
                        act.wait_ge(s_pv, i - 1)
                    act.activation(prT[:, i % 2, 0:(t + 1) * P], ps[:, TB[i % 2], 0:(t + 1) * P],
                                   ACT.Copy).then_inc(s_pT, 1)

            def take_heads(g):
                act.wait_ge(s_ht, g + 1)
                if g:
                    act.wait_ge(s_back, g)
                act.activation(ohT[:, :], ps[:, HT, 0:P], ACT.Copy).then_inc(s_ohT, 1)

            def turn_out(n):
                act.wait_ge(s_oTp, n + 1)
                act.activation(oT[:, n % TPB, :, :], ps[:, FB[n % TPB], 0:DM].rearrange("p (k t) -> p k t", k=KD),
                               ACT.Copy).then_inc(s_oT, 1)

            for b in range(BATCH):
                project(b)
                moments(b)
                act.wait_ge(s_thr0, b + 1)
                for k in steps(b):
                    if mine(b, k - 2):
                        act.wait_ge(s_thr2, k - 1)
                        count(k - 2, 2, thr2[:, k % 2, :], c2, s_c2, s_rank)
                    if mine(b, k):
                        _, t, h0 = place_of(k)
                        count(k, 0, thr0[:, t, h0:h0 + GH], c0, s_c0, s_thr1)
                    if mine(b, k - 1):
                        act.wait_ge(s_thr1, k)
                        count(k - 1, 1, thr1[:, (k - 1) % 2, :], c1, s_c1, s_thr2)
                    if mine(b, k - 2):
                        exponents(k - 2)
                    if mine(b, k - LAG):
                        turn(k - LAG)
                    if mine(b, k - LAG):
                        take_heads(k - LAG)
                for n in range(b * TPB, (b + 1) * TPB):
                    turn_out(n)

        @block.gpsimd
        def _(pool):
            done = [0]

            def link(ins):
                done[0] += 1
                ins.then_inc(s_pool, 1)
                pool.wait_ge(s_pool, done[0])

            pool.tensor_copy(kT[:, :, SEQ:WMAX], T.pre_k[:, :, :]).then_inc(s_one, 1)
            pool.memset(v[:, :, :, AD:AD + 1], 1.0).then_inc(s_one, 1)
            pool.memset(v[:, :, :, AD + 1:VW], 0.0).then_inc(s_one, 1)
            pool.memset(v_tail[:, :, :, :], 0.0).then_inc(s_one, 1)
            pool.wait_ge(s_one, 4)

            def first_thresholds(b):
                pool.wait_ge(s_mom, (b + 1) * TPB)
                if b:
                    pool.wait_ge(s_y, b * GPB * GH)
                    pool.wait_ge(s_c0, b * GPB * GH)
                link(pool.tensor_tensor(tmp[:, :, :], mom1[:, :, :], mom1[:, :, :], ALU.mult))
                link(pool.tensor_tensor(sd[:, :, :], mom2[:, :, :], tmp[:, :, :], ALU.subtract))
                pool.tensor_scalar(sd[:, :, :], sd[:, :, :], 1e-20, None, ALU.max).then_inc(s_var, 1)
                pool.wait_ge(s_sd, b + 1)
                pool.tensor_scalar(thr0[:, :, :], tmp[:, :, :], SHIFT, None, ALU.mult)
                pool.tensor_tensor(gain[:, :, :], tmp[:, :, :], T.tab[:, :, 1:2].to_broadcast([P, TPB, AH]), ALU.mult)
                link(pool.tensor_tensor(sd[:, :, :], tmp[:, :, :], T.tab[:, :, 0:1].to_broadcast([P, TPB, AH]),
                                        ALU.mult))
                pool.tensor_tensor(shift[:, :, :], sd[:, :, :], mom1[:, :, :], ALU.subtract).then_inc(s_thr0, 1)

            def newton(g):
                _, t, h0 = place_of(g)
                q = g % 2
                t0 = thr0[:, t, h0:h0 + GH]
                if g >= 2:
                    pool.wait_ge(s_c1, (g - 1) * GH)
                link(pool.tensor_scalar(off0[:, q, :], c0[:, q, :], float(2 * AIM - width(g)), None, ALU.add))
                link(pool.tensor_tensor(move[:, q, :], off0[:, q, :], gain[:, t, h0:h0 + GH], ALU.mult))
                pool.tensor_tensor(thr1[:, q, :], t0, move[:, q, :], ALU.add).then_inc(s_thr1, 1)

            def secant(g):
                q = g % 2
                off1, diff, square, far, rise, least, over, step = (w[:, i, :] for i in range(8))
                link(pool.tensor_scalar(off1, c1[:, q, :], float(2 * AIM - width(g)), None, ALU.add))
                pool.tensor_tensor(diff, off1, off0[:, q, :], ALU.subtract)
                link(pool.tensor_tensor(square, off1, off1, ALU.mult))
                pool.tensor_tensor(least, diff, diff, ALU.mult)
                pool.tensor_scalar(far, square, FAR, None, ALU.is_gt)
                link(pool.tensor_tensor(rise, diff, move[:, q, :], ALU.mult))
                pool.tensor_scalar(least, least, 1.0, None, ALU.max)
                link(pool.tensor_tensor(far, far, off1, ALU.mult))
                pool.tensor_tensor(over, least, T.minus1[:, 0:GH], ALU.pow)
                link(pool.tensor_tensor(step, far, rise, ALU.mult))
                link(pool.tensor_tensor(step, step, over, ALU.mult))
                if g >= 2:
                    pool.wait_ge(s_c2, (g - 1) * GH)
                    pool.wait_ge(s_m16, (g - 1) * GH)
                pool.tensor_tensor(thr2[:, q, :], thr1[:, q, :], step, ALU.subtract).then_inc(s_thr2, 1)

            def spread_flags(g):
                t, q = place_of(g)[1], g % 2
                pool.wait_ge(s_rank, g + 1)
                if t * P + 1 + PRE <= TOPK:
                    pool.tensor_scalar(thr[:, q, 0, :], thr[:, q, 0, :], T.tab[:, t, 2:3], T.tab[:, t, 3:4], ALU.mult,
                                       ALU.add)
                    link(pool.tensor_scalar(bad[:, q, :], bad[:, q, :], T.tab[:, t, 2:3], None, ALU.mult))
                if g >= 2:
                    pool.wait_ge(s_sel, (g - 1) * GH)
                pool.partition_all_reduce(flags[:, q, :], bad[:, q, :], P, RADD).then_inc(s_flag, 1)

            for b in range(BATCH):
                norm.gpsimd(pool, b)
            for b in range(BATCH):
                first_thresholds(b)
                for k in steps(b):
                    if mine(b, k):
                        pool.wait_ge(s_y, (k + 1) * GH)
                        if k >= NR:
                            pool.wait_ge(s_E, (k - NR + 1) * GH)
                        pool.tensor_scalar(nmax[:, k % NR, :], ymax[:, k % YR, :], -1.0, None,
                                           ALU.mult).then_inc(s_nmax, 1)
                        pool.wait_ge(s_c0, (k + 1) * GH)
                        newton(k)
                    if mine(b, k - 1):
                        pool.wait_ge(s_c1, k * GH)
                        secant(k - 1)
                    if mine(b, k - 2):
                        spread_flags(k - 2)

        @block.vector
        def _(dve):
            done = [0]

            def signal(ins):
                done[0] += 1
                ins.then_inc(s_dve, 1)

            def link(ins):
                signal(ins)
                dve.wait_ge(s_dve, done[0])

            def moments(b):
                dve.wait_ge(s_gram, b + 1)
                dve.tensor_tensor(gram[:, :, :], ps[:, GB[0], 0:DM].rearrange("p (m c) -> p m c", m=KT),
                                  T.blocks[:, :].unsqueeze(1).to_broadcast([P, KT, P]), ALU.mult)
                dve.tensor_tensor(k_sum[:, :, :], ps[:, GB[1], 0:KT].unsqueeze(2).to_broadcast([P, KT, HPT]),
                                  T.blocks[:, 0:P:SLOT].unsqueeze(1).to_broadcast([P, KT, HPT]),
                                  ALU.mult).then_inc(s_gm, 1)
                if b:
                    dve.wait_ge(s_thr0, b)
                for t in range(TPB):
                    n = b * TPB + t
                    dve.wait_ge(s_qg, n + 1)
                    dve.wait_ge(s_qtok, n + 1)
                    dve.tensor_scalar(by_head(mom1[:, t, :]), ps[:, QGB[t % 2][1], 0:AH].rearrange(
                        "p (odd half slot) -> p odd half slot", odd=2, half=KT), 1.0 / SEQ, None, ALU.mult)
                    if t:
                        dve.wait_ge(s_mom, n)
                    link(dve.scalar_tensor_tensor(prod[:, :], ps[:, QGB[t % 2][0], :], 1.0 / SEQ, q_tok[:, t % 2, :],
                                                  ALU.mult, ALU.mult))
                    squares = prod[:, :].rearrange("p (odd half slot c) -> p odd half slot c", odd=2, half=KT, slot=HPT)
                    dve.tensor_reduce(by_head(mom2[:, t, :]), squares, AX_X, ALU.add).then_inc(s_mom, 1)

            def take_scores(g, u):
                b, t, h0 = place_of(g)
                dve.wait_ge(s_thr0, b + 1)
                if g >= YR and u == 0:
                    dve.wait_ge(s_E, (g - YR + 1) * GH)
                    dve.wait_ge(s_c2, (g - YR + 1) * GH)
                    dve.wait_ge(s_nmax, g - YR + 1)
                    dve.wait_ge(s_sel, (g - YR + 1) * GH)
                i = g * GH + u
                dve.wait_ge(s_sc, i + 1)
                dve.tensor_scalar(y[:, g % YR, u, 0:width(g)], banks(g, u)[:, 0:width(g)],
                                  shift[:, t, h0 + u:h0 + u + 1], None, ALU.add, ALU.max,
                                  accum_out=ymax[:, g % YR, u:u + 1]).then_inc(s_y, 1)

            def largest_below(g):
                q = g % 2
                dve.wait_ge(s_thr2, g + 1)
                if g >= 2:
                    dve.wait_ge(s_rank, g - 1)
                if g:
                    dve.wait_ge(s_m16, g * GH)
                for stage in range(4):
                    for u in range(GH):
                        yu, z = y[:, g % YR, u, 0:width(g)], below[:, u, 0:width(g)]
                        if stage:
                            dve.wait_ge(s_low, (g * 3 + stage - 1) * GH + u + 1)
                        if stage == 0:
                            dve.scalar_tensor_tensor(z, yu, thr2[:, q, u:u + 1], yu, ALU.is_lt,
                                                     ALU.mult).then_inc(s_low, 1)
                        elif stage == 1:
                            dve.max(m16[:, q, u, 0:8], z).then_inc(s_low, 1)
                        elif stage == 2:
                            dve.match_replace(z, m16[:, q, u, 0:8], z, SENT).then_inc(s_low, 1)
                        else:
                            dve.max(m16[:, q, u, 8:16], z).then_inc(s_m16, 1)

            def find_rank(g, stage):
                t, q = place_of(g)[1], g % 2
                shape = [P, GH, DEPTH - 1]
                if stage == 0:
                    dve.wait_ge(s_m16, (g + 1) * GH)
                    dve.wait_ge(s_c2, (g + 1) * GH)
                    ins = dve.tensor_tensor(place[:, :, :], rank[:, t, :].unsqueeze(1).to_broadcast(shape),
                                            c2[:, q, :].unsqueeze(2).to_broadcast(shape), ALU.is_equal)
                    signal(ins)
                dve.wait_ge(s_dve, done[0])
                if stage == 1:
                    for n in range(2):
                        ins = dve.tensor_tensor(picked[:, n, :, :], place[:, :, :], m16[:, q, :, n:n + DEPTH - 1],
                                                ALU.mult)
                    signal(ins)
                elif stage == 2:
                    if g >= 2:
                        dve.wait_ge(s_sel, (g - 1) * GH)
                        dve.wait_ge(s_flag, g - 1)
                    signal(dve.tensor_reduce(thr[:, q, :, :], picked[:, :, :, :], AX_X, ALU.add))
                elif stage == 3:
                    dve.scalar_tensor_tensor(bad[:, q, 0:GH], thr[:, q, 1, :], 0.0, thr[:, q, 0, :], ALU.max, ALU.is_ge,
                                             accum_out=bad[:, q, GH:GH + 1]).then_inc(s_rank, 1)

            def general(g, u):
                wd = width(g)
                yu = y[:, g % YR, u, 0:wd]
                dve.max(m8[:, 0, :], yu).then_inc(s_gen, 1)
                n = 1
                for r in range(ROUNDS):
                    dve.wait_ge(s_gen, n)
                    dve.match_replace(left[:, 0:wd], m8[:, r, :], yu if r == 0 else left[:, 0:wd],
                                      SENT).then_inc(s_gen, 1)
                    n += 1
                    dve.wait_ge(s_gen, n)
                    if r + 1 < ROUNDS:
                        dve.max(m8[:, r + 1, :], left[:, 0:wd]).then_inc(s_gen, 1)
                        n += 1
                dve.scalar_tensor_tensor(E[:, g % ER, u, 0:wd], left[:, 0:wd], SENT, E[:, g % ER, u, 0:wd],
                                         ALU.is_equal, ALU.mult).then_inc(s_gen, 1)
                dve.wait_ge(s_gen, n + 1)
                dve.sem_clear(s_gen)

            def probabilities(g):
                q, wd = g % 2, width(g)
                dve.wait_ge(s_flag, g + 1)
                dve.wait_ge(s_E, (g + 1) * GH)
                any_head = dve.value_load(flags[0:1, q, GH:GH + 1].bitcast(I32))
                with dve.If(any_head > 0):
                    for u in range(GH):
                        bad_head = dve.value_load(flags[0:1, q, u:u + 1].bitcast(I32))
                        with dve.If(bad_head > 0):
                            general(g, u)
                            dve.memset(thr[:, q, 0, u:u + 1], SENT)
                            dve.drain()
                for u in range(GH):
                    dve.scalar_tensor_tensor(E[:, g % ER, u, 0:wd], y[:, g % YR, u, 0:wd], thr[:, q, 0, u:u + 1],
                                             E[:, g % ER, u, 0:wd], ALU.is_ge, ALU.mult).then_inc(s_sel, 1)

            def take_tail(g):
                t = place_of(g)[1]
                dve.wait_ge(s_sel, (g + 1) * GH)
                if g >= 2:
                    dve.wait_ge(s_tt, g - 1)
                dve.tensor_copy(tail[:, g % 2, :].rearrange("p (h c) -> p h c", h=GH),
                                E[:, g % ER, :, (t + 1) * P:(t + 1) * P + PRE]).then_inc(s_tail, 1)

            def normalise(g):
                _, t, h0 = place_of(g)
                dve.wait_ge(s_back, g + 1)
                ov = ps[:, OB, 0:P].rearrange("p (h d) -> p h d", h=GH)
                link(dve.reciprocal(rinv[:, g % 2, :], ov[:, :, AD]))
                dve.tensor_tensor(o[:, t, h0 * AD:(h0 + GH) * AD].rearrange("p (h d) -> p h d", h=GH), ov[:, :, 0:AD],
                                  rinv[:, g % 2, :].unsqueeze(2).to_broadcast([P, GH, AD]), ALU.mult).then_inc(s_on, 1)

            def residual(n):
                dve.wait_ge(s_f, n + 1)
                dve.tensor_tensor(T.x[:, n, :], ps[:, FO[n % 2], 0:DM], xa[:, n % TPB, :], ALU.add).then_inc(s_x, 1)

            for b in range(BATCH):
                if b == 0:
                    norm.vector(dve, 0)
                dve.wait_ge(s_one, 4)
                for t in range(TPB if b == 0 else 0):
                    link(dve.tensor_scalar(rank[:, t, :], T.iota16[:, 0:DEPTH - 1], 2.0,
                                           float((t + 1) * P + PRE - 2 * (TOPK - 1)), ALU.mult, ALU.add))
                for t in range(TPB):
                    dve.wait_ge(s_v, b * TPB + t + 1)
                    dve.tensor_tensor(v[:, t, :, 0:AD], ps[:, VB[t % 2], 0:DM].rearrange("p (h d) -> p h d", h=AH),
                                      T.rows[:, R_BV:R_BV + DM].rearrange("p (h d) -> p h d", h=AH),
                                      ALU.add).then_inc(s_vs, 1)
                if b + 1 < BATCH:
                    norm.vector(dve, b + 1)
                moments(b)
                for k in steps(b):
                    if mine(b, k - 2):
                        largest_below(k - 2)
                    if mine(b, k + 1):
                        take_scores(k + 1, 0)
                        take_scores(k + 1, 1)
                    if mine(b, k - LAG - 1):
                        normalise(k - LAG - 1)
                    if mine(b, k - 3):
                        probabilities(k - 3)
                    for stage in range(4):
                        if mine(b, k - 2):
                            find_rank(k - 2, stage)
                        if mine(b, k + 1) and stage in (1, 2):
                            take_scores(k + 1, stage + 1)
                    if mine(b, k - 3):
                        take_tail(k - 3)
                dve.wait_ge(s_sc, (b + 1) * GPB * GH)
                for t in range(TPB):
                    ins = dve.tensor_tensor(xa[:, t, :], T.x[:, b * TPB + t, :], T.rows[:, R_BO:R_BO + DM], ALU.add)
                link(ins)
                normalise((b + 1) * GPB - 1)
                for n in range(b * TPB, (b + 1) * TPB):
                    residual(n)
            dve.wait_ge(s_x, NT)

        @block.sync
        def _(sp):
            sp.wait_ge(s_one, 4)
            for b in range(BATCH):
                if b:
                    sp.wait_ge(s_ht, b * GPB)
                sp.wait_ge(s_vs, (b + 1) * TPB)
                for u in range(GH):
                    rows = slice(u * PRE, (u + 1) * PRE)
                    sp.dma_start(v_tail[rows, 0:TPB - 1, u:AH:GH, :], v[0:PRE, 1:TPB, u:AH:GH, :]).then_inc(s_vt, 16)
                sp.dma_start(v_tail[:, TPB - 1, :, :], T.pre_v).then_inc(s_vt, 16)
            sp.wait_ge(s_vt, 16 * BATCH * (GH + 1))


def hybrid_layer(nc, d, out):
    with ExitStack() as ctx:
        T = place(nc, ctx)
        T.s_later = ctx.enter_context(nc.semaphore("s_later"))
        with nc.sbuf_tensor("w_in", [P, KD, IN_PROJ], F32) as w_in, nc.sbuf_tensor("w_out", [P, ET, DM], F32) as w_out:
            T.w_in, T.w_out = w_in, w_out
            T.pre_v = d["pre_v"]
            start_up(nc, T, d)
            mamba(nc, T)
        ffn(nc, T, "f1")
        attention(nc, T)
        ffn(nc, T, "f2", out)


def prefix_values(pv):
    import numpy as np

    p = np.zeros((GH, PRE, AH // GH, GH, SLOT), pv.dtype)
    for u in range(GH):
        p[u, :, :, u, :AD] = pv.reshape(PRE, AH // GH, GH, AD)[:, :, u]
        p[u, :, :, u, AD] = 1
    return p.reshape(GH * PRE, AH, SLOT)


def threshold_table():
    import numpy as np

    def quantile(share):
        lo, hi = -8.0, 8.0
        for _ in range(60):
            mid = 0.5 * (lo + hi)
            if 0.5 * (1.0 + math.erf(mid / math.sqrt(2.0))) < share:
                lo = mid
            else:
                hi = mid
        return lo

    tab = np.zeros((P, TPB, 4), np.float32)
    for t in range(TPB):
        for p in range(P):
            n = t * P + p + 1 + PRE
            share = min(max(1.0 - AIM / n, 0.02), 0.98)
            z = quantile(share)
            density = math.exp(-0.5 * z * z) / math.sqrt(2.0 * math.pi)
            tab[p, t] = (SHIFT - z, -0.5 / (n * density), float(n > TOPK), 0.1 * NEG * (n <= TOPK))
    return tab


def kernel(**inputs):
    import numpy as np
    import concourse.bacc as bacc
    from concourse.bass_utils import run_bass_kernel_spmd

    a = {k[3:]: np.asarray(v) for k, v in inputs.items()}

    def columns(v):
        return v.reshape(-1, P).T

    def slots(w):
        heads = w.reshape(w.shape[0], AH // 2, 2, AD)
        p = np.zeros((w.shape[0], 2, AH // 2, 2, AD), w.dtype)
        for odd in range(2):
            p[:, odd, :, odd] = heads[:, :, odd]
        return p.reshape(w.shape[0], AH * SLOT)

    cw = a["attn_a_conv_w"].reshape(CT, P, DCONV).transpose(1, 0, 2).reshape(P, CT * DCONV)
    bq, bk = columns(slots(a["attn_b_bq"][None])[0]), columns(a["attn_b_bk"])
    host = {
        "x": a["attn_a_u"],
        "cols": np.concatenate([cw, columns(a["attn_a_conv_b"]), columns(a["attn_a_norm_w"]), columns(a["ffn_b1"]),
                                bq, bk], axis=1),
        "rows": np.concatenate([a["attn_a_dt_bias"], a["attn_a_A_log"], a["attn_a_D"], a["ffn_br"], a["ffn_b2"],
                                a["attn_b_bv"], a["attn_b_bo"]]),
        "w_in": a["attn_a_W_in"].T,
        "w_out": a["attn_a_W_out"].T,
        "w_ra": np.concatenate([a["ffn_Wr"], a["ffn_A1"].reshape(NE * RK, DM).T], axis=1),
        "w1": a["ffn_W1"],
        "b1l": a["ffn_B1"].transpose(0, 2, 1).reshape(NE * RK, FF),
        "w2a": np.concatenate([a["ffn_W2"], a["ffn_A2"].reshape(NE * RK, FF).T], axis=1),
        "b2l": a["ffn_B2"].transpose(0, 2, 1).reshape(NE * RK, DM),
        "wq": slots(a["attn_b_Wq"]),
        "wk": a["attn_b_Wk"],
        "wv": a["attn_b_Wv"],
        "wo": a["attn_b_Wo"],
        "pre_k": a["attn_b_pk"][0].T.reshape(KT, P, PRE).transpose(1, 0, 2),
        "pre_v": prefix_values(a["attn_b_pv"][0]),
    }
    host["tab"] = threshold_table()
    nc = bacc.Bacc("TRN2", target_bir_lowering=False, num_devices=1)
    arrays, d = {}, {}
    for name, v in host.items():
        v = np.ascontiguousarray(v)
        arrays[f"in_{name}"] = v
        d[name] = nc.dram_tensor(f"in_{name}", v.shape, mybir.dt.from_np(v.dtype), kind="ExternalInput").ap()
    out = nc.dram_tensor("out", (BATCH, SEQ, DM), F32, kind="ExternalOutput").ap()
    hybrid_layer(nc, d, out)
    r = run_bass_kernel_spmd(nc, [arrays], core_ids=[0])
    return r.results[0]["out"]
```
